# Optimizing a Trainium2 kernel written in Bass

```python
import numpy as np
import jax
import jax.numpy as jnp

def _softmax(x, axis=-1):
    return jax.nn.softmax(x, axis=axis)

def _gelu(x):
    return jax.nn.gelu(x, approximate=True)

def _silu(x):
    return jax.nn.silu(x)

def _sigmoid(x):
    return jax.nn.sigmoid(x)

def _layernorm(x, axis=-1, eps=1e-05):
    m = jnp.mean(x, axis=axis, keepdims=True)
    v = jnp.var(x, axis=axis, keepdims=True)
    return (x - m) / jnp.sqrt(v + eps)

def _scatter_add(tgt, idx, src, axis=0):
    return tgt.at[idx].add(src)

def _segment_sum(src, seg, n):
    return jax.ops.segment_sum(src, seg, n)
kernel_name = 'mk_seq_postln_d2_jaxref_r4_2c34e3'

def setup_inputs(seed: int=0):
    np.random.seed(seed)
    _w = jnp.asarray

    def _L0_attn_setup():
        import math
        import jax, jax.numpy as jnp
        import numpy as np
        B, L, DIM, HEADS = (4, 512, 256, 8)
        HEAD = DIM // HEADS
        SCALE_BASE = 512.0
        EPS = 1e-05

        def _xpos(x, downscale=False):
            l, dh = (x.shape[-2], x.shape[-1])
            half = dh // 2
            pos = jnp.arange(l, dtype=x.dtype)
            base = (jnp.arange(0, dh, 2, dtype=x.dtype) + 0.4 * dh) / (1.4 * dh)
            scale = base[None, :] ** (pos[:, None] / SCALE_BASE)
            inv_freq = 1.0 / 10000.0 ** (jnp.arange(half, dtype=x.dtype) / half)
            sinusoid = pos[:, None] * inv_freq[None, :]
            sin, cos = (jnp.sin(sinusoid), jnp.cos(sinusoid))
            if downscale:
                scale = 1.0 / scale
            s = jnp.repeat(sin * scale, 2, axis=-1)
            c = jnp.repeat(cos * scale, 2, axis=-1)
            x1, x2 = (x[..., ::2], x[..., 1::2])
            rot = jnp.stack([-x2, x1], axis=-1).reshape(x.shape)
            return x * c + rot * s

        def _decay_mask(l, gammas):
            n = jnp.arange(l)[:, None]
            m = jnp.arange(l)[None, :]
            lg = jnp.log(gammas)
            expo = (n - m).astype(jnp.float32)[None, :, :] * lg[:, None, None]
            return jnp.where((n >= m)[None], jnp.exp(expo), 0.0)
        key = jax.random.key(seed)
        ks = jax.random.split(key, 6)
        d = DIM
        return {'X': jax.random.normal(ks[0], (B, L, DIM), dtype=jnp.float32), 'W_Q': jax.random.normal(ks[1], (HEADS, DIM, HEAD), dtype=jnp.float32) / d, 'W_K': jax.random.normal(ks[2], (HEADS, DIM, HEAD), dtype=jnp.float32) / d, 'W_V': jax.random.normal(ks[3], (HEADS, DIM, HEAD), dtype=jnp.float32) / d, 'W_G': jax.random.normal(ks[4], (DIM, DIM), dtype=jnp.float32) / d, 'W_O': jax.random.normal(ks[5], (DIM, DIM), dtype=jnp.float32) / d, 'gn_weight': jnp.ones((DIM,), dtype=jnp.float32), 'gn_bias': jnp.zeros((DIM,), dtype=jnp.float32)}
    _L0_attn_in = _L0_attn_setup()

    def _L0_ffn_setup():
        import jax, jax.numpy as jnp
        import numpy as np
        D_IN, D_HID = (256, 1024)

        def _ternary(key, shape):
            return jax.random.randint(key, shape, -1, 2).astype(jnp.float32)

        def _tlin(x, w, s):
            return jnp.einsum('bsi,oi->bso', x, w) * s
        key = jax.random.key(seed)
        ks = jax.random.split(key, 12)
        inv = lambda fan: 1.0 / np.sqrt(fan).astype(np.float32)
        return {'x': jax.random.normal(ks[0], (4, 512, D_IN), dtype=jnp.float32), 'w1_w': _ternary(ks[1], (D_HID, D_IN)), 'w1_s': jax.random.uniform(ks[2], (D_HID,), dtype=jnp.float32) * inv(D_IN), 'w2_w': _ternary(ks[3], (D_HID, D_IN)), 'w2_s': jax.random.uniform(ks[4], (D_HID,), dtype=jnp.float32) * inv(D_IN), 'h1_w': _ternary(ks[5], (D_HID, D_HID)), 'h1_s': jax.random.uniform(ks[6], (D_HID,), dtype=jnp.float32) * inv(D_HID), 'h2_w': _ternary(ks[7], (D_HID, D_HID)), 'h2_s': jax.random.uniform(ks[8], (D_HID,), dtype=jnp.float32) * inv(D_HID), 'w3_w': _ternary(ks[9], (D_IN, D_HID)), 'w3_s': jax.random.uniform(ks[10], (D_IN,), dtype=jnp.float32) * inv(D_HID)}
    _L0_ffn_in = _L0_ffn_setup()

    def _L1_attn_setup():
        import jax, jax.numpy as jnp
        import numpy as np
        T, B, D = (256, 32, 256)
        N_STATE, BLOCK = (256, 8)
        NB = N_STATE // BLOCK

        def _xavier(key, shape):
            fan_out, fan_in = shape
            a = (6.0 / (fan_in + fan_out)) ** 0.5
            return jax.random.uniform(key, shape, jnp.float32, -a, a)
        key = jax.random.key(seed)
        kx, kk, kv, kq = jax.random.split(key, 4)
        return {'x': jax.random.normal(kx, (T, B, D), jnp.float32), 'W_k': _xavier(kk, (N_STATE, D)), 'W_v': _xavier(kv, (N_STATE, D)), 'W_q': _xavier(kq, (N_STATE, D))}
    _L1_attn_in = _L1_attn_setup()

    def _L1_ffn_setup():
        import jax, jax.numpy as jnp
        import numpy as np
        DIM = 256

        def _reference_tuple_inner(x, W_r, W_k, W_v, mu_r, mu_k):
            B, T, C = x.shape
            x_prev = jnp.concatenate([jnp.zeros((B, 1, C), x.dtype), x[:, :-1, :]], axis=1)
            xr = mu_r * x + (1.0 - mu_r) * x_prev
            xk = mu_k * x + (1.0 - mu_k) * x_prev
            r = jax.nn.sigmoid(jnp.einsum('btc,dc->btd', xr, W_r))
            k = jnp.einsum('btc,dc->btd', xk, W_k)
            k_act = jnp.square(jax.nn.relu(k))
            out = r * jnp.einsum('btc,dc->btd', k_act, W_v)
            new_state = x[:, -1, :]
            return (out, new_state)
        key = jax.random.key(seed)
        ks = jax.random.split(key, 6)
        B, T, C = (8, 512, DIM)
        x = jax.random.normal(ks[0], (B, T, C), dtype=jnp.float32)
        s = 1.0 / np.sqrt(C)
        W_r = jax.random.uniform(ks[1], (C, C), jnp.float32, -s, s)
        W_k = jax.random.uniform(ks[2], (C, C), jnp.float32, -s, s)
        W_v = jax.random.uniform(ks[3], (C, C), jnp.float32, -s, s)
        mu_r = jax.random.uniform(ks[4], (C,), jnp.float32)
        mu_k = jax.random.uniform(ks[5], (C,), jnp.float32)
        return {'x': x, 'W_r': W_r, 'W_k': W_k, 'W_v': W_v, 'mu_r': mu_r, 'mu_k': mu_k}
    _L1_ffn_in = _L1_ffn_setup()
    _d = {'L0_attn_X': _L0_attn_in['X'], 'L0_attn_W_Q': _L0_attn_in['W_Q'], 'L0_attn_W_K': _L0_attn_in['W_K'], 'L0_attn_W_V': _L0_attn_in['W_V'], 'L0_attn_W_G': _L0_attn_in['W_G'], 'L0_attn_W_O': _L0_attn_in['W_O'], 'L0_attn_gn_weight': _L0_attn_in['gn_weight'], 'L0_attn_gn_bias': _L0_attn_in['gn_bias'], 'L0_ffn_w1_w': _L0_ffn_in['w1_w'], 'L0_ffn_w1_s': _L0_ffn_in['w1_s'], 'L0_ffn_w2_w': _L0_ffn_in['w2_w'], 'L0_ffn_w2_s': _L0_ffn_in['w2_s'], 'L0_ffn_h1_w': _L0_ffn_in['h1_w'], 'L0_ffn_h1_s': _L0_ffn_in['h1_s'], 'L0_ffn_h2_w': _L0_ffn_in['h2_w'], 'L0_ffn_h2_s': _L0_ffn_in['h2_s'], 'L0_ffn_w3_w': _L0_ffn_in['w3_w'], 'L0_ffn_w3_s': _L0_ffn_in['w3_s'], 'L1_attn_W_k': _L1_attn_in['W_k'], 'L1_attn_W_v': _L1_attn_in['W_v'], 'L1_attn_W_q': _L1_attn_in['W_q'], 'L1_ffn_W_r': _L1_ffn_in['W_r'], 'L1_ffn_W_k': _L1_ffn_in['W_k'], 'L1_ffn_W_v': _L1_ffn_in['W_v'], 'L1_ffn_mu_r': _L1_ffn_in['mu_r'], 'L1_ffn_mu_k': _L1_ffn_in['mu_k']}
    _x0 = _d['L0_attn_X']
    _d['L0_attn_X'] = jax.random.normal(jax.random.fold_in(jax.random.key(seed), 1), (4, 1024, 256), dtype=_x0.dtype)
    del _x0
    return _d

def reference(L0_attn_X, L0_attn_W_Q, L0_attn_W_K, L0_attn_W_V, L0_attn_W_G, L0_attn_W_O, L0_attn_gn_weight, L0_attn_gn_bias, L0_ffn_w1_w, L0_ffn_w1_s, L0_ffn_w2_w, L0_ffn_w2_s, L0_ffn_h1_w, L0_ffn_h1_s, L0_ffn_h2_w, L0_ffn_h2_s, L0_ffn_w3_w, L0_ffn_w3_s, L1_attn_W_k, L1_attn_W_v, L1_attn_W_q, L1_ffn_W_r, L1_ffn_W_k, L1_ffn_W_v, L1_ffn_mu_r, L1_ffn_mu_k):

    def _L0_attn_ref(X, W_Q, W_K, W_V, W_G, W_O, gn_weight, gn_bias):
        import math
        import jax, jax.numpy as jnp
        import numpy as np
        B, L, DIM, HEADS = (4, 512, 256, 8)
        HEAD = DIM // HEADS
        SCALE_BASE = 512.0
        EPS = 1e-05

        def _xpos(x, downscale=False):
            l, dh = (x.shape[-2], x.shape[-1])
            half = dh // 2
            pos = jnp.arange(l, dtype=x.dtype)
            base = (jnp.arange(0, dh, 2, dtype=x.dtype) + 0.4 * dh) / (1.4 * dh)
            scale = base[None, :] ** (pos[:, None] / SCALE_BASE)
            inv_freq = 1.0 / 10000.0 ** (jnp.arange(half, dtype=x.dtype) / half)
            sinusoid = pos[:, None] * inv_freq[None, :]
            sin, cos = (jnp.sin(sinusoid), jnp.cos(sinusoid))
            if downscale:
                scale = 1.0 / scale
            s = jnp.repeat(sin * scale, 2, axis=-1)
            c = jnp.repeat(cos * scale, 2, axis=-1)
            x1, x2 = (x[..., ::2], x[..., 1::2])
            rot = jnp.stack([-x2, x1], axis=-1).reshape(x.shape)
            return x * c + rot * s

        def _decay_mask(l, gammas):
            n = jnp.arange(l)[:, None]
            m = jnp.arange(l)[None, :]
            lg = jnp.log(gammas)
            expo = (n - m).astype(jnp.float32)[None, :, :] * lg[:, None, None]
            return jnp.where((n >= m)[None], jnp.exp(expo), 0.0)
        b, l, d = X.shape
        h = W_Q.shape[0]
        gammas = 1.0 - jnp.exp(jnp.linspace(math.log(1.0 / 32.0), math.log(1.0 / 512.0), h)).astype(jnp.float32)
        Q = jnp.einsum('bld,hde->bhle', X, W_Q)
        K = jnp.einsum('bld,hde->bhle', X, W_K)
        V = jnp.einsum('bld,hdv->bhlv', X, W_V)
        Q = _xpos(Q)
        K = _xpos(K, downscale=True)
        D = _decay_mask(l, gammas).astype(X.dtype)
        scores = jnp.einsum('bhle,bhme->bhlm', Q, K) * D[None]
        Y = jnp.einsum('bhlm,bhmv->bhlv', scores, V)
        mean = Y.mean(axis=-1, keepdims=True)
        var = Y.var(axis=-1, keepdims=True)
        Yn = (Y - mean) * jax.lax.rsqrt(var + EPS)
        Yn = jnp.transpose(Yn, (0, 2, 1, 3)).reshape(b, l, -1)
        Yn = Yn * gn_weight + gn_bias
        G = X @ W_G
        out = G * jax.nn.sigmoid(G) * Yn @ W_O
        return out

    def _L0_ffn_ref(x, w1_w, w1_s, w2_w, w2_s, h1_w, h1_s, h2_w, h2_s, w3_w, w3_s):
        import jax, jax.numpy as jnp
        import numpy as np
        D_IN, D_HID = (256, 1024)

        def _ternary(key, shape):
            return jax.random.randint(key, shape, -1, 2).astype(jnp.float32)

        def _tlin(x, w, s):
            return jnp.einsum('bsi,oi->bso', x, w) * s
        h = jax.nn.silu(_tlin(x, w1_w, w1_s)) * _tlin(x, w2_w, w2_s)
        h = jax.nn.gelu(_tlin(h, h1_w, h1_s), approximate=False)
        h = jax.nn.gelu(_tlin(h, h2_w, h2_s), approximate=False)
        return _tlin(h, w3_w, w3_s)

    def _L1_attn_ref(x, W_k, W_v, W_q):
        import jax, jax.numpy as jnp
        import numpy as np
        T, B, D = (256, 32, 256)
        N_STATE, BLOCK = (256, 8)
        NB = N_STATE // BLOCK

        def _xavier(key, shape):
            fan_out, fan_in = shape
            a = (6.0 / (fan_in + fan_out)) ** 0.5
            return jax.random.uniform(key, shape, jnp.float32, -a, a)
        T_, B_, D_ = x.shape
        n = W_k.shape[0]
        b = BLOCK
        nb = n // b
        k = jnp.einsum('tbd,nd->tbn', x, W_k).reshape(T_, B_, nb, b)
        v = jnp.einsum('tbd,nd->tbn', x, W_v).reshape(T_, B_, nb, b)
        q = jnp.einsum('tbd,nd->tbn', x, W_q).reshape(T_, B_, nb, b)

        def step(S, kvq):
            k_t, v_t, q_t = kvq
            k_norm = k_t / (jnp.linalg.norm(k_t, axis=-1, keepdims=True) + 1e-06)
            retrieved = jnp.einsum('bnij,bnj->bni', S, k_norm)
            delta = v_t - retrieved
            S_new = jnp.tanh(S + jnp.einsum('bni,bnj->bnij', delta, k_norm))
            Sq = jnp.einsum('bnij,bnj->bni', S_new, q_t).reshape(B_, n)
            out = Sq * jax.nn.silu(Sq)
            return (S_new, out)
        S0 = jnp.zeros((B_, nb, b, b), x.dtype)
        _, outputs = jax.lax.scan(step, S0, (k, v, q))
        return outputs

    def _L1_ffn_ref(x, W_r, W_k, W_v, mu_r, mu_k):
        import jax, jax.numpy as jnp
        import numpy as np
        DIM = 256

        def _reference_tuple_inner(x, W_r, W_k, W_v, mu_r, mu_k):
            B, T, C = x.shape
            x_prev = jnp.concatenate([jnp.zeros((B, 1, C), x.dtype), x[:, :-1, :]], axis=1)
            xr = mu_r * x + (1.0 - mu_r) * x_prev
            xk = mu_k * x + (1.0 - mu_k) * x_prev
            r = jax.nn.sigmoid(jnp.einsum('btc,dc->btd', xr, W_r))
            k = jnp.einsum('btc,dc->btd', xk, W_k)
            k_act = jnp.square(jax.nn.relu(k))
            out = r * jnp.einsum('btc,dc->btd', k_act, W_v)
            new_state = x[:, -1, :]
            return (out, new_state)
        return _reference_tuple_inner(x, W_r, W_k, W_v, mu_r, mu_k)[0]
    x = L0_attn_X
    x = _layernorm(x + _L0_attn_ref(x, L0_attn_W_Q, L0_attn_W_K, L0_attn_W_V, L0_attn_W_G, L0_attn_W_O, L0_attn_gn_weight, L0_attn_gn_bias), axis=-1)
    x = _layernorm(x + _L0_ffn_ref(x, L0_ffn_w1_w, L0_ffn_w1_s, L0_ffn_w2_w, L0_ffn_w2_s, L0_ffn_h1_w, L0_ffn_h1_s, L0_ffn_h2_w, L0_ffn_h2_s, L0_ffn_w3_w, L0_ffn_w3_s), axis=-1)
    x = _layernorm(x + _L1_attn_ref(x, L1_attn_W_k, L1_attn_W_v, L1_attn_W_q), axis=-1)
    x = _layernorm(x + _L1_ffn_ref(x, L1_ffn_W_r, L1_ffn_W_k, L1_ffn_W_v, L1_ffn_mu_r, L1_ffn_mu_k), axis=-1)
    return x

_drawn_inputs = setup_inputs


def setup_inputs(seed=0):
    import zlib

    import numpy as np

    out = dict(_drawn_inputs(seed))
    spreads = {'L0_attn_gn_weight': (1.0, 0.6), 'L0_attn_gn_bias': (0.0, 0.8)}
    factors = {'L0_attn_W_Q': 8.0,
     'L0_attn_W_K': 8.0,
     'L0_attn_W_V': 8.0,
     'L0_attn_W_G': 8.0,
     'L0_attn_W_O': 8.0,
     'L0_ffn_w1_w': 8.0,
     'L0_ffn_w1_s': 8.0,
     'L0_ffn_w2_w': 8.0,
     'L0_ffn_w2_s': 8.0,
     'L0_ffn_h1_w': 8.0,
     'L0_ffn_h1_s': 8.0,
     'L0_ffn_h2_w': 8.0,
     'L0_ffn_h2_s': 8.0,
     'L0_ffn_w3_w': 8.0,
     'L0_ffn_w3_s': 8.0,
     'L1_ffn_W_r': 3.179,
     'L1_ffn_mu_r': 6.383}
    for name, (base, spread) in spreads.items():
        noise = np.random.default_rng([zlib.crc32(name.encode()), seed]).standard_normal(out[name].shape)
        drawn = base * np.exp(spread * noise) if base else spread * noise
        out[name] = jnp.asarray(drawn.astype(out[name].dtype))
    for name, factor in factors.items():
        out[name] = (out[name] * factor).astype(out[name].dtype)
    return out
```

```python
from contextlib import ExitStack

import concourse.bass as bass
from concourse import mybir

F32 = mybir.dt.float32
ALU = mybir.AluOpType
ACT = mybir.ActivationFunctionType
AX_X = mybir.AxisListType.X

P = 128
BATCH, LENGTH, DIM = 4, 1024, 256
HEADS, HEAD = 8, 32
GROUPS, PER_GROUP = 2, 4
CHUNKS = LENGTH // P
KD = DIM // P
HID = 1024
KH = HID // P
NB, BS = 32, 8
HALF = NB // 2
TOK = BATCH * P
EPS = 1e-5


class Steps:

    def __init__(self, eng, sem, per_chunk):
        self.eng, self.sem, self.per_chunk = eng, sem, per_chunk

    def begin(self, c):
        self.c, self.k = c, 0

    def done(self, ins):
        ins.then_inc(self.sem, 1)
        self.k += 1

    def wait(self):
        self.eng.wait_ge(self.sem, self.c * self.per_chunk + self.k)

    def end(self):
        assert self.k == self.per_chunk, (self.k, self.per_chunk)


def build(nc, xT_d, x_d, rope_d, causal_d, ident_d, decay_d, wa_d, wo_d, gnw_d, gnb_d,
          w1_d, w2_d, h1_d, h2_d, w3_d, s1_d, s2_d, hs1_d, hs2_d, s3_d, wkvq_d,
          wr_d, wk_d, wv_d, mur_d, muk_d, out_d, x1_d):
    top = ExitStack()

    def sb(ctx, name, shape):
        return ctx.enter_context(nc.sbuf_tensor(name, shape, F32))

    def sem(ctx, name):
        return ctx.enter_context(nc.semaphore(name))

    with top:
        bank = [top.enter_context(nc.psum_tensor(f"bank{n}", [P, 512], F32)) for n in range(8)]

        ident = sb(top, "ident", [P, P])
        half_pow = sb(top, "half_pow", [P, P])
        inv_pow = sb(top, "inv_pow", [P, P])
        w1 = sb(top, "w1", [P, KD, HID])
        w2 = sb(top, "w2", [P, KD, HID])
        h1 = sb(top, "h1", [P, KH, HID])
        h2 = sb(top, "h2", [P, KH, HID])
        w3 = sb(top, "w3", [P, KH, DIM])
        wkvq = sb(top, "wkvq", [P, KD, 3 * DIM])
        wr = sb(top, "wr", [P, KD, DIM])
        wk = sb(top, "wk", [P, KD, DIM])
        wv = sb(top, "wv", [P, KD, DIM])
        s1 = sb(top, "s1", [P, KH])
        s2 = sb(top, "s2", [P, KH])
        hs1 = sb(top, "hs1", [P, KH])
        hs2 = sb(top, "hs2", [P, KH])
        s1half = sb(top, "s1half", [P, KH])
        s12half = sb(top, "s12half", [P, KH])
        s3 = sb(top, "s3", [P, DIM])
        mu_r = sb(top, "mu_r", [P, KD])
        mu_k = sb(top, "mu_k", [P, KD])
        nu_r = sb(top, "nu_r", [P, KD])
        nu_k = sb(top, "nu_k", [P, KD])
        stats = sb(top, "stats", [P, BATCH, 6])
        spread = sb(top, "spread", [P, BATCH])
        ffn_in = sem(top, "ffn_in")
        misc_in = sem(top, "misc_in")
        pow_ready = sem(top, "pow_ready")

        def layernorm(dve, steps, r, mv, rstd, ve_ready, rstd_ready, c, done_sem):
            steps.wait()
            for b in range(BATCH):
                ins = nc.vector.bn_stats(out=stats[:, b, :], in_=r[:, b, :])
            steps.done(ins)
            steps.wait()
            nc.vector.tensor_tensor(mv[:, :, 0], stats[:, :, 1], stats[:, :, 4], ALU.add)
            nc.vector.tensor_tensor(spread[:], stats[:, :, 1], stats[:, :, 4], ALU.subtract)
            steps.done(nc.vector.tensor_tensor(mv[:, :, 1], stats[:, :, 2], stats[:, :, 5], ALU.add))
            steps.wait()
            nc.vector.tensor_scalar(mv[:, :, 0], mv[:, :, 0], 0.5, None, ALU.mult)
            nc.vector.tensor_tensor(spread[:], spread[:], spread[:], ALU.mult)
            steps.done(nc.vector.tensor_scalar(mv[:, :, 1], mv[:, :, 1], 1.0 / DIM, EPS, ALU.mult, ALU.add))
            steps.wait()
            nc.vector.scalar_tensor_tensor(out=mv[:, :, 1], in0=spread[:], scalar=0.25, in1=mv[:, :, 1],
                                           op0=ALU.mult, op1=ALU.add).then_inc(ve_ready, 1)
            dve.wait_ge(rstd_ready, c + 1)
            for b in range(BATCH):
                ins = nc.vector.tensor_scalar(r[:, b, :], r[:, b, :], mv[:, b, 0:1], rstd[:, b:b + 1],
                                              ALU.subtract, ALU.mult)
            ins.then_inc(done_sem, 1)

        with ExitStack() as ctx:
            xT = sb(ctx, "xT", [P, KD, BATCH, P])
            xtok = sb(ctx, "xtok", [P, BATCH, DIM])
            rope = sb(ctx, "rope", [P, 2, 2 * DIM])
            causal = sb(ctx, "causal", [P, P])
            decay = sb(ctx, "decay", [P, GROUPS, P])
            wa = sb(ctx, "wa", [P, KD, 4 * DIM])
            wo = sb(ctx, "wo", [P, KD, DIM])
            gnw = sb(ctx, "gnw", [P, DIM])
            gnb = sb(ctx, "gnb", [P, DIM])
            qk = sb(ctx, "qk", [P, BATCH, 2 * DIM])
            turned = sb(ctx, "turned", [P, 2 * DIM])
            qkT = sb(ctx, "qkT", [P, BATCH, 4, P])
            v = sb(ctx, "v", [P, BATCH, DIM])
            gate = sb(ctx, "gate", [P, 2, BATCH, DIM])
            probs = sb(ctx, "probs", [P, PER_GROUP, 2, GROUPS, P])
            state = sb(ctx, "state", [P, BATCH, GROUPS, P])
            mean = sb(ctx, "mean", [P, BATCH, HEADS])
            var = sb(ctx, "var", [P, BATCH, HEADS])
            rgn = sb(ctx, "rgn", [P, BATCH, HEADS])
            y = sb(ctx, "y", [P, BATCH, DIM])
            ysq = sb(ctx, "ysq", [P, BATCH, DIM])
            zT = sb(ctx, "zT", [P, KD, TOK])
            r1 = sb(ctx, "r1", [P, BATCH, DIM])
            mv1 = sb(ctx, "mv1", [P, BATCH, 2])
            rstd1 = sb(ctx, "rstd1", [P, BATCH])

            const_in = sem(ctx, "const_in")
            xT_in = sem(ctx, "xT_in")
            xtok_in = sem(ctx, "xtok_in")
            rope_in = sem(ctx, "rope_in")
            x1_out = sem(ctx, "x1_out")
            proj_done = sem(ctx, "proj_done")
            v_done = sem(ctx, "v_done")
            tanh_done = sem(ctx, "tanh_done")
            gate_done = sem(ctx, "gate_done")
            rope_done = sem(ctx, "rope_done")
            turn_done = sem(ctx, "turn_done")
            t_done = sem(ctx, "t_done")
            qkT_done = sem(ctx, "qkT_done")
            scores_done = sem(ctx, "scores_done")
            probs_done = sem(ctx, "probs_done")
            y_done = sem(ctx, "y_done")
            mean_done = sem(ctx, "mean_done")
            centre_done = sem(ctx, "centre_done")
            sum_done = sem(ctx, "sum_done")
            state_done = sem(ctx, "state_done")
            ysq_done = sem(ctx, "ysq_done")
            gn_ve = sem(ctx, "gn_ve")
            gn_rstd = sem(ctx, "gn_rstd")
            z_done = sem(ctx, "z_done")
            zt_ps = sem(ctx, "zt_ps")
            zT_done = sem(ctx, "zT_done")
            wo_ps = sem(ctx, "wo_ps")
            r1_done = sem(ctx, "r1_done")
            ve1 = sem(ctx, "ve1")
            rs1 = sem(ctx, "rs1")
            ln1_done = sem(ctx, "ln1_done")
            gn_steps = sem(ctx, "gn_steps")
            N_GN = 7
            N_CONST = 7

            block = ctx.enter_context(nc.Block())

            @block.sync
            def _(sp):
                x_view = x_d.rearrange("b c p d -> p c b d")
                sp.dma_start(xT[:], xT_d[:, :, :, 0:P]).then_inc(xT_in, 16)
                sp.dma_start(wa[:], wa_d).then_inc(const_in, 16)
                sp.dma_start(rope[:], rope_d[0]).then_inc(rope_in, 16)
                sp.dma_start(ident[:], ident_d).then_inc(const_in, 16)
                sp.dma_start(causal[:], causal_d).then_inc(const_in, 16)
                sp.dma_start(xtok[:], x_view[:, 0]).then_inc(xtok_in, 16)
                sp.dma_start(decay[:], decay_d).then_inc(const_in, 16)
                sp.dma_start(gnw[:], gnw_d.broadcast_to([P, DIM])).then_inc(const_in, 16)
                sp.dma_start(gnb[:], gnb_d.broadcast_to([P, DIM])).then_inc(const_in, 16)
                sp.dma_start(wo[:], wo_d).then_inc(const_in, 16)

                def loads(c):
                    sp.wait_ge(proj_done, c * BATCH)
                    sp.dma_start(xT[:], xT_d[:, :, :, bass.ts(c, P)]).then_inc(xT_in, 16)
                    sp.wait_ge(rope_done, c * BATCH)
                    sp.dma_start(rope[:], rope_d[bass.ds(c, 1)].rearrange("o p a d -> (o p) a d")).then_inc(rope_in, 16)

                def loads_late(c):
                    sp.wait_ge(r1_done, c * 2)
                    sp.dma_start(xtok[:], x_rows(c)).then_inc(xtok_in, 16)
                    sp.wait_ge(ln1_done, c)
                    sp.dma_start(x1_rows(c - 1), r1[:]).then_inc(x1_out, 16)

                def x_rows(c):
                    return x_view[:, bass.ds(c, 1)].rearrange("p o b d -> p (o b) d")

                def x1_rows(c):
                    return x1_d[bass.ds(c, 1)].rearrange("o p b d -> (o p) b d")

                loads(1)
                for dst, src in ((w1, w1_d), (w2, w2_d), (h1, h1_d), (h2, h2_d), (w3, w3_d),
                                 (wkvq, wkvq_d), (wr, wr_d), (wk, wk_d), (wv, wv_d), (s1, s1_d),
                                 (s2, s2_d), (hs1, hs1_d), (hs2, hs2_d), (mu_r, mur_d), (mu_k, muk_d)):
                    sp.dma_start(dst[:], src).then_inc(ffn_in, 16)
                sp.dma_start(s3[:], s3_d.broadcast_to([P, DIM])).then_inc(ffn_in, 16)
                loads_late(1)
                with sp.Fori(2, CHUNKS) as c:
                    loads(c)
                    loads_late(c)
                sp.wait_ge(ln1_done, CHUNKS)
                sp.dma_start(x1_rows(CHUNKS - 1), r1[:]).then_inc(x1_out, 16)
                sp.wait_ge(x1_out, 16 * CHUNKS)

            @block.tensor
            def _(pe):
                pe.wait_ge(const_in, 16 * N_CONST)

                def project(c, b):
                    if b == 0:
                        pe.wait_ge(xT_in, (c + 1) * 16)
                    if not (isinstance(c, int) and c == 0 and b == 0):
                        pe.wait_ge(rope_done, c * BATCH + b)
                        pe.wait_ge(v_done, c * BATCH + b)
                        pe.wait_ge(gate_done, c * BATCH + b)
                    for half in range(2):
                        for k in range(KD):
                            ins = nc.tensor.matmul(bank[half][:], xT[:, k, b, :],
                                                   wa[:, k, half * 512:half * 512 + 512],
                                                   start=(k == 0), stop=(k == KD - 1))
                    ins.then_inc(proj_done, 1)

                def turn(c, b, first):
                    pe.wait_ge(rope_done, c * BATCH + b + 1)
                    if not first and b >= 2:
                        pe.wait_ge(r1_done, c * 2 + b - 3)
                    for t in range(4):
                        ins = nc.tensor.transpose(bank[4 + b][:, t * P:t * P + P],
                                                  qk[:, b, t * P:t * P + P], ident[:])
                    ins.then_inc(t_done, 1)

                def scores(c, r):
                    pe.wait_ge(qkT_done, c * BATCH + BATCH)
                    if r == 1:
                        pe.wait_ge(probs_done, c * 8 + 4)
                    for b2 in range(2):
                        for g in range(GROUPS):
                            for j in range(PER_GROUP):
                                rows = slice(HEAD * j, HEAD * j + HEAD)
                                col = (b2 * GROUPS + g) * P
                                ins = nc.tensor.matmul(bank[4 + j][:, col:col + P],
                                                       qkT[rows, 2 * r + b2, 2 + g, :],
                                                       qkT[rows, 2 * r + b2, g, :], start=True, stop=True)
                    ins.then_inc(scores_done, 1)

                def outputs(c, b):
                    if b % 2 == 0:
                        pe.wait_ge(probs_done, c * 8 + 4 * (b // 2) + 4)
                        pe.wait_ge(v_done, c * BATCH + BATCH)
                    pe.wait_ge(state_done, c * BATCH + b + 3)
                    pb = bank[2 + b % 2]
                    for g in range(GROUPS):
                        nc.tensor.matmul(pb[:, g * P:g * P + P], qkT[:, b, g, :], state[:, b, g, :],
                                         start=True, stop=False, skip_group_check=True)
                        for j in range(PER_GROUP):
                            h = g * PER_GROUP + j
                            nc.tensor.matmul(pb[:, h * HEAD:h * HEAD + HEAD], probs[:, j, b % 2, g, :],
                                             v[:, b, h * HEAD:h * HEAD + HEAD], start=False,
                                             stop=(j == PER_GROUP - 1), skip_group_check=True)
                    for g in range(GROUPS):
                        ins = nc.tensor.matmul(pb[:, DIM + g * P:DIM + g * P + P],
                                               qk[:, b, DIM + g * P:DIM + g * P + P],
                                               v[:, b, g * P:g * P + P], start=True, stop=True)
                    ins.then_inc(y_done, 1)

                def out_product(c):
                    pe.wait_ge(z_done, c + 1)
                    for k in range(KD):
                        for b in range(BATCH):
                            ins = nc.tensor.transpose(bank[4 + k][:, b * P:b * P + P],
                                                      y[:, b, k * P:k * P + P], ident[:])
                        ins.then_inc(zt_ps, 1)
                    pe.wait_ge(zT_done, c * 2 + 2)
                    for b in range(BATCH):
                        for k in range(KD):
                            ins = nc.tensor.matmul(bank[6 + b // 2][:, (b % 2) * DIM:(b % 2) * DIM + DIM],
                                                   zT[:, k, b * P:b * P + P], wo[:, k, :],
                                                   start=(k == 0), stop=(k == KD - 1))
                        if b % 2:
                            ins.then_inc(wo_ps, 1)

                def body(c, last=False):
                    scores(c, 0)
                    if not last:
                        project(c + 1, 0)
                    outputs(c, 0)
                    outputs(c, 1)
                    scores(c, 1)
                    if not last:
                        project(c + 1, 1)
                    outputs(c, 2)
                    outputs(c, 3)
                    if not last:
                        project(c + 1, 2)
                        project(c + 1, 3)
                    out_product(c)
                    if not last:
                        for b in range(BATCH):
                            turn(c + 1, b, False)

                for b in range(BATCH):
                    project(0, b)
                for b in range(BATCH):
                    turn(0, b, True)
                body(0)
                with pe.Fori(1, CHUNKS - 1, 2) as c:
                    body(c)
                    body(c + 1)
                body(CHUNKS - 1, last=True)

            @block.scalar
            def _(act):
                def value_gate(c, b, parity, first):
                    act.wait_ge(proj_done, c * BATCH + b + 1)
                    if not first:
                        act.wait_ge(y_done, (c - 1) * BATCH + b + 1)
                    nc.scalar.copy(v[:, b, :], bank[1][:, 0:DIM]).then_inc(v_done, 1)
                    nc.scalar.activation(gate[:, parity, b, :], bank[1][:, DIM:2 * DIM], ACT.Tanh,
                                         scale=0.5).then_inc(tanh_done, 1)

                def square(c, b):
                    act.wait_ge(centre_done, c * BATCH + b + 1)
                    nc.scalar.activation(ysq[:, b, :], y[:, b, :], ACT.Square).then_inc(ysq_done, 1)

                def z_transposed(c):
                    for k in range(KD):
                        act.wait_ge(zt_ps, c * 2 + k + 1)
                        nc.scalar.copy(zT[:, k, :], bank[4 + k][:]).then_inc(zT_done, 1)

                def turned_out(c):
                    for b in range(BATCH):
                        act.wait_ge(t_done, c * BATCH + b + 1)
                        nc.scalar.copy(qkT[:, b, :, :], bank[4 + b][:].rearrange("p (t n) -> p t n", t=4)
                                       ).then_inc(qkT_done, 1)

                def body(c, parity, last=False):
                    nxt = 1 - parity
                    if not last:
                        value_gate(c + 1, 0, nxt, False)
                    square(c, 0)
                    square(c, 1)
                    if not last:
                        value_gate(c + 1, 1, nxt, False)
                    square(c, 2)
                    square(c, 3)
                    if not last:
                        value_gate(c + 1, 2, nxt, False)
                        value_gate(c + 1, 3, nxt, False)
                    z_transposed(c)
                    if not last:
                        turned_out(c + 1)

                for b in range(BATCH):
                    value_gate(0, b, 0, True)
                turned_out(0)
                body(0, 0)
                with act.Fori(1, CHUNKS - 1, 2) as c:
                    body(c, 1)
                    body(c + 1, 0)
                body(CHUNKS - 1, 1, last=True)

            @block.gpsimd
            def _(pool):
                nc.gpsimd.memset(half_pow[:], 0.5).then_inc(pow_ready, 1)
                nc.gpsimd.memset(inv_pow[:], -0.5).then_inc(pow_ready, 1)
                pool.wait_ge(pow_ready, 2)

                def body(c):
                    pool.wait_ge(gn_ve, c + 1)
                    nc.gpsimd.tensor_tensor(rgn[:].rearrange("p b h -> p (b h)"), var[:].rearrange("p b h -> p (b h)"),
                                            inv_pow[:, 0:BATCH * HEADS], ALU.pow).then_inc(gn_rstd, 1)
                    pool.wait_ge(ve1, c + 1)
                    nc.gpsimd.tensor_tensor(rstd1[:], mv1[:, :, 1], inv_pow[:, 0:BATCH], ALU.pow).then_inc(rs1, 1)

                with pool.Fori(0, CHUNKS) as c:
                    body(c)

            @block.vector
            def _(dve):
                for b in range(BATCH):
                    nc.vector.memset(state[:, b, :, :], 0.0).then_inc(state_done, 1)
                dve.wait_ge(const_in, 16 * N_CONST)
                steps = Steps(dve, gn_steps, N_GN)

                def rotate(c, b, parity, first):
                    if b == 0:
                        dve.wait_ge(rope_in, (c + 1) * 16)
                    dve.wait_ge(proj_done, c * BATCH + b + 1)
                    if not first:
                        dve.wait_ge(y_done, (c - 1) * BATCH + b + 1)
                    raw = bank[0][:].rearrange("p (e two) -> p e two", two=2)
                    sin = rope[:, 1, :].rearrange("p (e two) -> p e two", two=2)
                    tur = turned[:].rearrange("p (e two) -> p e two", two=2)
                    nc.vector.tensor_tensor(qk[:, b, :], bank[0][:], rope[:, 0, :], ALU.mult)
                    nc.vector.tensor_tensor(tur[:, :, 0], raw[:, :, 1], sin[:, :, 0], ALU.mult)
                    nc.vector.tensor_tensor(tur[:, :, 1], raw[:, :, 0], sin[:, :, 1], ALU.mult).then_inc(turn_done, 1)
                    dve.wait_ge(turn_done, c * BATCH + b + 1)
                    nc.vector.tensor_tensor(qk[:, b, :], qk[:, b, :], turned[:], ALU.add).then_inc(rope_done, 1)
                    dve.wait_ge(tanh_done, c * BATCH + b + 1)
                    nc.vector.scalar_tensor_tensor(out=gate[:, parity, b, :], in0=gate[:, parity, b, :], scalar=1.0,
                                                   in1=bank[1][:, DIM:2 * DIM], op0=ALU.add,
                                                   op1=ALU.mult).then_inc(gate_done, 1)

                def masked(c, r):
                    dve.wait_ge(scores_done, c * 2 + r + 1)
                    for j in range(PER_GROUP):
                        nc.vector.tensor_tensor(
                            probs[:, j, :, :, :].rearrange("p b g n -> p (b g) n"),
                            bank[4 + j][:].rearrange("p (x n) -> p x n", n=P),
                            causal[:].unsqueeze(1).broadcast_to([P, 4, P]), ALU.mult).then_inc(probs_done, 1)

                def collect(c, b):
                    dve.wait_ge(y_done, c * BATCH + b + 1)
                    pb = bank[2 + b % 2]
                    y3 = pb[:, 0:DIM].rearrange("p (h e) -> p h e", e=HEAD)
                    nc.vector.tensor_reduce(mean[:, b, :], y3, AX_X, ALU.add).then_inc(mean_done, 1)
                    st = state[:, b, :, :].rearrange("p g e -> p (g e)")
                    nc.vector.tensor_tensor(st, st, pb[:, DIM:2 * DIM], ALU.add).then_inc(sum_done, 1)
                    dve.wait_ge(mean_done, c * 2 * BATCH + 2 * b + 1)
                    nc.vector.tensor_scalar(mean[:, b, :], mean[:, b, :], 1.0 / HEAD, None, ALU.mult).then_inc(mean_done, 1)
                    dve.wait_ge(sum_done, c * BATCH + b + 1)
                    dve.wait_ge(mean_done, c * 2 * BATCH + 2 * b + 2)
                    nc.vector.tensor_tensor(y[:, b, :].rearrange("p (h e) -> p h e", e=HEAD), y3,
                                            mean[:, b, :].unsqueeze(2).broadcast_to([P, HEADS, HEAD]),
                                            ALU.subtract).then_inc(centre_done, 1)
                    nc.vector.tensor_tensor(st, st, decay[:].rearrange("p g e -> p (g e)"),
                                            ALU.mult).then_inc(state_done, 1)

                def variance(c):
                    dve.wait_ge(ysq_done, c * BATCH + BATCH)
                    vflat = var[:].rearrange("p b h -> p (b h)")
                    steps.done(nc.vector.tensor_reduce(vflat, ysq[:].rearrange("p b (h e) -> p (b h) e", e=HEAD),
                                                       AX_X, ALU.add))
                    steps.wait()
                    nc.vector.tensor_scalar(vflat, vflat, 1.0 / HEAD, EPS, ALU.mult, ALU.add).then_inc(gn_ve, 1)

                def gated(c, parity):
                    dve.wait_ge(gn_rstd, c + 1)
                    yh = y[:].rearrange("p b (h e) -> p (b h) e", e=HEAD)
                    dve.wait_ge(centre_done, c * BATCH + BATCH)
                    steps.done(nc.vector.tensor_tensor(
                        yh, yh, rgn[:].rearrange("p b h -> p (b h)").unsqueeze(2).broadcast_to([P, BATCH * HEADS, HEAD]),
                        ALU.mult))
                    steps.wait()
                    steps.done(nc.vector.tensor_tensor(y[:], y[:], gnw[:].unsqueeze(1).broadcast_to([P, BATCH, DIM]), ALU.mult))
                    steps.wait()
                    steps.done(nc.vector.tensor_tensor(y[:], y[:], gnb[:].unsqueeze(1).broadcast_to([P, BATCH, DIM]), ALU.add))
                    steps.wait()
                    dve.wait_ge(gate_done, c * BATCH + BATCH)
                    nc.vector.scalar_tensor_tensor(out=y[:].rearrange("p b d -> p (b d)"),
                                                   in0=gate[:, parity, :, :].rearrange("p b d -> p (b d)"), scalar=0.5,
                                                   in1=y[:].rearrange("p b d -> p (b d)"), op0=ALU.mult,
                                                   op1=ALU.mult).then_inc(z_done, 1)

                def residual(c, first):
                    dve.wait_ge(xtok_in, (c + 1) * 16)
                    if not first:
                        dve.wait_ge(x1_out, c * 16)
                    for n in range(2):
                        dve.wait_ge(wo_ps, c * 2 + n + 1)
                        nc.vector.tensor_tensor(r1[:, 2 * n:2 * n + 2, :],
                                                bank[6 + n][:].rearrange("p (b d) -> p b d", b=2),
                                                xtok[:, 2 * n:2 * n + 2, :], ALU.add).then_inc(r1_done, 1)
                    dve.wait_ge(r1_done, c * 2 + 2)
                    layernorm(dve, steps, r1, mv1, rstd1, ve1, rs1, c, ln1_done)
                    steps.end()

                def body(c, parity, first=False, last=False):
                    steps.begin(c)
                    masked(c, 0)
                    if not last:
                        rotate(c + 1, 0, 1 - parity, False)
                    collect(c, 0)
                    collect(c, 1)
                    masked(c, 1)
                    if not last:
                        rotate(c + 1, 1, 1 - parity, False)
                    collect(c, 2)
                    collect(c, 3)
                    variance(c)
                    if not last:
                        rotate(c + 1, 2, 1 - parity, False)
                    gated(c, parity)
                    if not last:
                        rotate(c + 1, 3, 1 - parity, False)
                    residual(c, first)

                for b in range(BATCH):
                    rotate(0, b, 0, True)
                body(0, 0, first=True)
                with dve.Fori(1, CHUNKS - 1, 2) as c:
                    body(c, 1)
                    body(c + 1, 0)
                body(CHUNKS - 1, 1, last=True)

        with ExitStack() as ctx:
            x1in = sb(ctx, "x1in", [P, BATCH, DIM])
            x1res = sb(ctx, "x1res", [P, BATCH, DIM])
            wide_a = sb(ctx, "wide_a", [P, KD, TOK])
            wide_b = sb(ctx, "wide_b", [P, KD, TOK])
            th = sb(ctx, "th", [P, 2, TOK])
            hid_a = sb(ctx, "hid_a", [P, KH, TOK])
            hid_b = sb(ctx, "hid_b", [P, KH, TOK])
            x2 = sb(ctx, "x2", [P, BATCH, DIM])
            kvq = sb(ctx, "kvq", [P, BATCH, 3 * DIM])
            S = sb(ctx, "S", [P, NB, BS, BS])
            tmp = sb(ctx, "tmp", [P, NB, BS, BS])
            norm = sb(ctx, "norm", [P, BATCH, NB])
            delta = sb(ctx, "delta", [P, NB, BS])
            Sq = sb(ctx, "Sq", [P, BATCH, DIM])
            x3 = sb(ctx, "x3", [P, BATCH, DIM])
            x3T = sb(ctx, "x3T", [P, KD, BATCH, P + 1])
            y4 = sb(ctx, "y4", [P, BATCH, DIM])
            mv2 = sb(ctx, "mv2", [P, BATCH, 2])
            rstd2 = sb(ctx, "rstd2", [P, BATCH])
            mv3 = sb(ctx, "mv3", [P, BATCH, 2])
            rstd3 = sb(ctx, "rstd3", [P, BATCH])
            mv4 = sb(ctx, "mv4", [P, BATCH, 2])
            rstd4 = sb(ctx, "rstd4", [P, BATCH])
            sem2 = lambda name: sem(ctx, name)
            x1in_in, x1res_in, out_done = sem2("x1in_in"), sem2("x1res_in"), sem2("out_done")
            prep = sem2("prep")
            x1T_ps, x1T_done = sem2("x1T_ps"), sem2("x1T_done")
            w12_ps, th_done, prod_mid, h0_done = sem2("w12_ps"), sem2("th_done"), sem2("prod_mid"), sem2("h0_done")
            h1_ps, g1_done, h2_ps, g2_done = sem2("h1_ps"), sem2("g1_done"), sem2("h2_ps"), sem2("g2_done")
            w3_ps, scaled_done, r2_done = sem2("w3_ps"), sem2("scaled_done"), sem2("r2_done")
            ve2, rs2, ln2_steps, ln2_done = sem2("ve2"), sem2("rs2"), sem2("ln2_steps"), sem2("ln2_done")
            x2T_ps, x2T_done, kvq_ps, kvq_done = sem2("x2T_ps"), sem2("x2T_done"), sem2("kvq_ps"), sem2("kvq_done")
            ksq_done, nsum, nroot = sem2("ksq_done"), sem2("nsum"), sem2("nroot")
            scan_steps = sem2("scan_steps")
            pre_tanh, post_tanh = sem2("pre_tanh"), sem2("post_tanh")
            sq_done, sq_tanh = sem2("sq_done"), sem2("sq_tanh")
            ve3, rs3, ln3_steps, ln3_done = sem2("ve3"), sem2("rs3"), sem2("ln3_steps"), sem2("ln3_done")
            x3T_ps, x3T_col, x3T_done = sem2("x3T_ps"), sem2("x3T_col"), sem2("x3T_done")
            part_done, mixk_done, mixr_done = sem2("part_done"), sem2("mixk_done"), sem2("mixr_done")
            dk_ps, relu_done, kact_done = sem2("dk_ps"), sem2("relu_done"), sem2("kact_done")
            dr_ps, sig_done, dv_ps, gated4 = sem2("dr_ps"), sem2("sig_done"), sem2("dv_ps"), sem2("gated4")
            ve4, rs4, ln4_steps, ln4_done = sem2("ve4"), sem2("rs4"), sem2("ln4_steps"), sem2("ln4_done")
            N_FFN_IN = 16
            N_LN2, N_LN3, N_LN4 = 3, 6, 4
            N_SCAN = 4 + 2 * BATCH + 2 * 4 * (BATCH - 1)

            block = ctx.enter_context(nc.Block())

            def schedule(eng, body, per_pass=None):
                for i in range(3):
                    body(i, True, i >= 1, i >= 2, i + 1 < CHUNKS)
                with eng.Fori(3, CHUNKS - 1) as i:
                    body(i, True, True, True, True)
                body(CHUNKS - 1, True, True, True, False)
                body(CHUNKS, False, True, True, False)
                body(CHUNKS + 1, False, False, True, False)

            @block.sync
            def _(sp):
                def x1_rows(c):
                    return x1_d[bass.ds(c, 1)].rearrange("o p b d -> (o p) b d")

                out_view = out_d.rearrange("b (c p) d -> p c b d", p=P)
                sp.dma_start(x1in[:], x1_rows(0)).then_inc(x1in_in, 16)
                sp.dma_start(x1res[:], x1_rows(0)).then_inc(x1res_in, 16)

                def body(i, ffn, scan, mix, more):
                    if more:
                        sp.wait_ge(x1T_ps, i * 2 + 2)
                        sp.dma_start(x1in[:], x1_rows(i + 1)).then_inc(x1in_in, 16)
                    if mix:
                        sp.wait_ge(ln4_done, i - 1)
                        sp.dma_start(out_view[:, bass.ds(i - 2, 1)].rearrange("p o b d -> p (o b) d"),
                                     y4[:]).then_inc(out_done, 16)
                    if more:
                        sp.wait_ge(r2_done, i * 2 + 2)
                        sp.dma_start(x1res[:], x1_rows(i + 1)).then_inc(x1res_in, 16)

                schedule(sp, body)
                sp.wait_ge(out_done, 16 * CHUNKS)

            @block.tensor
            def _(pe):
                pe.wait_ge(ffn_in, 16 * N_FFN_IN)

                def transposes(src, ps):
                    for k in range(KD):
                        for b in range(BATCH):
                            ins = nc.tensor.transpose(bank[4 + k][:, b * P:b * P + P], src[:, b, k * P:k * P + P],
                                                      ident[:])
                        ins.then_inc(ps, 1)

                def x1_transposed(c):
                    pe.wait_ge(x1in_in, (c + 1) * 16)
                    transposes(x1in, x1T_ps)

                def up(c, after):
                    pe.wait_ge(x1T_done, c * 2 + 2)
                    for m in range(KH):
                        if m >= 2:
                            pe.wait_ge(h0_done, c * KH + m - 1)
                        elif m == 0 and after:
                            pe.wait_ge(r2_done, c * 2)
                        for n, w in ((0, w1), (1, w2)):
                            for k in range(KD):
                                ins = nc.tensor.matmul(bank[2 * (m % 2) + n][:], w[:, k, m * P:m * P + P],
                                                       wide_a[:, k, :], start=(k == 0), stop=(k == KD - 1))
                        ins.then_inc(w12_ps, 1)

                def hidden(c, m, w, src, ready, ps):
                    if m == 0:
                        pe.wait_ge(ready[0], c * KH + KH)
                    if m >= 4:
                        pe.wait_ge(ready[1], c * KH + m - 3)
                    for k in range(KH):
                        ins = nc.tensor.matmul(bank[m % 4][:], w[:, k, m * P:m * P + P], src[:, k, :],
                                               start=(k == 0), stop=(k == KH - 1))
                    ins.then_inc(ps, 1)

                def down(c):
                    pe.wait_ge(g2_done, c * KH + KH)
                    for b in range(BATCH):
                        for k in range(KH):
                            ins = nc.tensor.matmul(bank[b // 2][:, (b % 2) * DIM:(b % 2) * DIM + DIM],
                                                   hid_a[:, k, b * P:b * P + P], w3[:, k, :],
                                                   start=(k == 0), stop=(k == KH - 1))
                        if b % 2:
                            ins.then_inc(w3_ps, 1)

                def scan_inputs(c):
                    pe.wait_ge(ln2_done, c + 1)
                    transposes(x2, x2T_ps)
                    pe.wait_ge(x2T_done, c * 2 + 2)
                    for b in range(BATCH):
                        lo = 6 if b % 2 == 0 else 4
                        if b >= 2:
                            pe.wait_ge(kvq_done, c * 2 * BATCH + 2 * (b - 1))
                        for n, (a, z) in enumerate(((0, 512), (512, 768))):
                            for k in range(KD):
                                ins = nc.tensor.matmul(bank[lo + n][:, 0:z - a], wide_b[:, k, b * P:b * P + P],
                                                       wkvq[:, k, a:z], start=(k == 0), stop=(k == KD - 1))
                        ins.then_inc(kvq_ps, 1)

                def mix_transposes(c, scan):
                    pe.wait_ge(ln3_done, c + 1)
                    if scan:
                        pe.wait_ge(kvq_done, (c + 2) * 2 * BATCH)
                    transposes(x3, x3T_ps)

                def mix_in(c):
                    pe.wait_ge(mixk_done, c * 2 + 2)
                    for m in range(KD):
                        for k in range(KD):
                            ins = nc.tensor.matmul(bank[4 + m][:], wk[:, k, m * P:m * P + P], wide_a[:, k, :],
                                                   start=(k == 0), stop=(k == KD - 1))
                        ins.then_inc(dk_ps, 1)
                    pe.wait_ge(mixr_done, c * 2 + 2)
                    for b in range(BATCH):
                        for k in range(KD):
                            ins = nc.tensor.matmul(bank[6 + b // 2][:, (b % 2) * DIM:(b % 2) * DIM + DIM],
                                                   wide_b[:, k, b * P:b * P + P], wr[:, k, :],
                                                   start=(k == 0), stop=(k == KD - 1))
                        if b % 2:
                            ins.then_inc(dr_ps, 1)

                def mix_out(c):
                    pe.wait_ge(kact_done, c * 2 + 2)
                    for b in range(BATCH):
                        for k in range(KD):
                            ins = nc.tensor.matmul(bank[4 + b // 2][:, (b % 2) * DIM:(b % 2) * DIM + DIM],
                                                   wide_a[:, k, b * P:b * P + P], wv[:, k, :],
                                                   start=(k == 0), stop=(k == KD - 1))
                        if b % 2:
                            ins.then_inc(dv_ps, 1)

                def body(i, ffn, scan, mix, more):
                    if ffn:
                        up(i, scan)
                    if scan:
                        scan_inputs(i - 1)
                    for m in range(KH):
                        if ffn:
                            hidden(i, m, h1, hid_a, (h0_done, g1_done), h1_ps)
                        if mix and m == 1:
                            mix_transposes(i - 2, scan)
                        if mix and m == 3:
                            mix_in(i - 2)
                        if mix and m == 6:
                            mix_out(i - 2)
                    for m in range(KH):
                        if ffn:
                            hidden(i, m, h2, hid_b, (g1_done, g2_done), h2_ps)
                        if more and m == 6:
                            if mix:
                                pe.wait_ge(gated4, (i - 2) * 2 + 2)
                            elif scan:
                                pe.wait_ge(kvq_done, i * 2 * BATCH)
                            x1_transposed(i + 1)
                    if ffn:
                        down(i)

                x1_transposed(0)
                schedule(pe, body)

            @block.scalar
            def _(act):
                act.wait_ge(ffn_in, 16 * N_FFN_IN)
                act.wait_ge(prep, 9)

                def evacuate(dst, c, ps, done):
                    for k in range(KD):
                        act.wait_ge(ps, c * 2 + k + 1)
                        nc.scalar.copy(dst[:, k, :], bank[4 + k][:]).then_inc(done, 1)

                def scan_tanh(c, t):
                    for hf in range(2):
                        act.wait_ge(pre_tanh, c * 8 + 2 * t + hf + 1)
                        half = S[:, hf * HALF:hf * HALF + HALF, :, :].rearrange("p n i j -> p (n i j)")
                        nc.scalar.activation(half, half, ACT.Tanh).then_inc(post_tanh, 1)

                def body(i, ffn, scan, mix, more):
                    c = i - 1
                    d = i - 2
                    if ffn:
                        for m in range(KH):
                            act.wait_ge(w12_ps, i * KH + m + 1)
                            if m >= 2:
                                act.wait_ge(h0_done, i * KH + m - 1)
                            nc.scalar.activation(th[:, m % 2, :], bank[2 * (m % 2)][:], ACT.Tanh,
                                                 scale=s1half[:, m:m + 1]).then_inc(th_done, 1)
                    if scan:
                        evacuate(wide_b, c, x2T_ps, x2T_done)
                        for b in range(BATCH):
                            lo = 6 if b % 2 == 0 else 4
                            act.wait_ge(kvq_ps, c * BATCH + b + 1)
                            nc.scalar.copy(kvq[:, b, 0:512], bank[lo][:]).then_inc(kvq_done, 1)
                            nc.scalar.copy(kvq[:, b, 512:768], bank[lo + 1][:, 0:DIM]).then_inc(kvq_done, 1)
                        act.wait_ge(kvq_done, (c + 1) * 2 * BATCH)
                        nc.scalar.activation(tmp[:, 0:HALF, :, :].rearrange("p n i j -> p (n i j)").rearrange(
                            "p (b d) -> p b d", b=BATCH), kvq[:, :, 0:DIM], ACT.Square).then_inc(ksq_done, 1)
                    for m in range(KH):
                        if ffn:
                            act.wait_ge(h1_ps, i * KH + m + 1)
                            nc.scalar.activation(hid_b[:, m, :], bank[m % 4][:], ACT.Gelu,
                                                 scale=hs1[:, m:m + 1]).then_inc(g1_done, 1)
                        if scan and m == 0:
                            scan_tanh(c, 0)
                        if mix and m == 1:
                            nc.scalar.copy(x3T[:, :, :, 0], x3T[:, :, :, P]).then_inc(x3T_col, 1)
                            act.wait_ge(x3T_col, d + 1)
                            for k in range(KD):
                                act.wait_ge(x3T_ps, d * 2 + k + 1)
                                nc.scalar.copy(x3T[:, k, :, 1:P + 1], bank[4 + k][:].rearrange("p (b n) -> p b n", b=BATCH)
                                               ).then_inc(x3T_done, 1)
                            act.wait_ge(x3T_done, d * 2 + 2)
                            for dst, nu in ((wide_a, nu_k), (wide_b, nu_r)):
                                for k in range(KD):
                                    nc.scalar.activation(dst[:, k, :].rearrange("p (b n) -> p b n", b=BATCH),
                                                         x3T[:, k, :, 0:P], ACT.Copy,
                                                         scale=nu[:, k:k + 1]).then_inc(part_done, 1)
                        if scan and m == 3:
                            scan_tanh(c, 1)
                        if mix and m == 4:
                            act.wait_ge(dk_ps, d * 2 + 2)
                            for k in range(KD):
                                nc.scalar.activation(wide_a[:, k, :], bank[4 + k][:], ACT.Relu).then_inc(relu_done, 1)
                            act.wait_ge(relu_done, d * 2 + 2)
                            for k in range(KD):
                                nc.scalar.activation(wide_a[:, k, :], wide_a[:, k, :], ACT.Square).then_inc(kact_done, 1)
                            if not (isinstance(i, int) and i == 2):
                                act.wait_ge(out_done, (i - 2) * 16)
                            for n in range(2):
                                act.wait_ge(dr_ps, d * 2 + n + 1)
                                nc.scalar.activation(y4[:, 2 * n:2 * n + 2, :],
                                                     bank[6 + n][:].rearrange("p (b d) -> p b d", b=2),
                                                     ACT.Tanh, scale=0.5).then_inc(sig_done, 1)
                        if scan and m == 6:
                            scan_tanh(c, 2)
                    for m in range(KH):
                        if ffn:
                            act.wait_ge(h2_ps, i * KH + m + 1)
                            nc.scalar.activation(hid_a[:, m, :], bank[m % 4][:], ACT.Gelu,
                                                 scale=hs2[:, m:m + 1]).then_inc(g2_done, 1)
                        if scan and m == 1:
                            scan_tanh(c, 3)
                        if scan and m == 4:
                            act.wait_ge(sq_done, (c + 1) * 2 * BATCH)
                            nc.scalar.activation(tmp[:, 0:HALF, :, :].rearrange("p n i j -> p (n i j)"),
                                                 Sq[:].rearrange("p b d -> p (b d)"), ACT.Tanh,
                                                 scale=0.5).then_inc(sq_tanh, 1)
                        if more and m == 6:
                            evacuate(wide_a, i + 1, x1T_ps, x1T_done)

                evacuate(wide_a, 0, x1T_ps, x1T_done)
                schedule(act, body)

            @block.gpsimd
            def _(pool):
                def root(dst, src, n, expo, ready, done, c):
                    pool.wait_ge(ready, c + 1)
                    nc.gpsimd.tensor_tensor(dst, src, expo[:, 0:n], ALU.pow).then_inc(done, 1)

                def body(i, ffn, scan, mix, more):
                    flat = norm[:].rearrange("p b n -> p (b n)")
                    if scan:
                        root(flat, flat, BATCH * NB, half_pow, nsum, nroot, i - 1)
                    if mix:
                        root(rstd4[:], mv4[:, :, 1], BATCH, inv_pow, ve4, rs4, i - 2)
                    if scan:
                        root(rstd3[:], mv3[:, :, 1], BATCH, inv_pow, ve3, rs3, i - 1)
                    if ffn:
                        root(rstd2[:], mv2[:, :, 1], BATCH, inv_pow, ve2, rs2, i)

                schedule(pool, body)

            @block.vector
            def _(dve):
                dve.wait_ge(ffn_in, 16 * N_FFN_IN)
                nc.vector.tensor_scalar(s1half[:], s1[:], 0.5, None, ALU.mult).then_inc(prep, 1)
                nc.vector.tensor_tensor(s12half[:], s1[:], s2[:], ALU.mult).then_inc(prep, 1)
                dve.wait_ge(prep, 2)
                nc.vector.tensor_scalar(s12half[:], s12half[:], 0.5, None, ALU.mult).then_inc(prep, 1)
                nc.vector.tensor_scalar(nu_r[:], mu_r[:], -1.0, 1.0, ALU.mult, ALU.add).then_inc(prep, 1)
                nc.vector.tensor_scalar(nu_k[:], mu_k[:], -1.0, 1.0, ALU.mult, ALU.add).then_inc(prep, 1)
                for k in range(KD):
                    for col in (0, P):
                        nc.vector.memset(x3T[:, k, :, col], 0.0).then_inc(prep, 1)
                dve.wait_ge(prep, 9)
                ln2, ln3, ln4 = (Steps(dve, ln2_steps, N_LN2), Steps(dve, ln3_steps, N_LN3),
                                 Steps(dve, ln4_steps, N_LN4))
                scan = Steps(dve, scan_steps, N_SCAN)
                kb4 = kvq[:, :, 0:DIM].rearrange("p b (n j) -> p b n j", j=BS)

                def product(c, m):
                    dve.wait_ge(th_done, c * KH + m + 1)
                    nc.vector.scalar_tensor_tensor(out=th[:, m % 2, :], in0=th[:, m % 2, :], scalar=1.0,
                                                   in1=bank[2 * (m % 2)][:], op0=ALU.add,
                                                   op1=ALU.mult).then_inc(prod_mid, 1)
                    dve.wait_ge(prod_mid, c * KH + m + 1)
                    nc.vector.scalar_tensor_tensor(out=hid_a[:, m, :], in0=bank[2 * (m % 2) + 1][:],
                                                   scalar=s12half[:, m:m + 1], in1=th[:, m % 2, :],
                                                   op0=ALU.mult, op1=ALU.mult).then_inc(h0_done, 1)

                def key_norms(c):
                    scan.begin(c)
                    flat = norm[:].rearrange("p b n -> p (b n)")
                    dve.wait_ge(ksq_done, c + 1)
                    nc.vector.tensor_reduce(flat, tmp[:, 0:HALF, :, :].rearrange("p n i j -> p (n i) j"),
                                            AX_X, ALU.add).then_inc(nsum, 1)
                    dve.wait_ge(nroot, c + 1)
                    scan.done(nc.vector.tensor_scalar(flat, flat, 1e-6, None, ALU.add))
                    scan.wait()
                    scan.done(nc.vector.reciprocal(flat, flat))
                    scan.wait()
                    for hf in range(2):
                        b2 = slice(2 * hf, 2 * hf + 2)
                        scan.done(nc.vector.tensor_tensor(kb4[:, b2], kb4[:, b2],
                                                          norm[:, b2, :].unsqueeze(3).broadcast_to([P, 2, NB, BS]),
                                                          ALU.mult))
                    scan.wait()

                def parts(t, hf):
                    n0 = hf * HALF
                    k, v, q = (kvq[:, t, a * DIM + n0 * BS:a * DIM + (n0 + HALF) * BS].rearrange(
                        "p (n j) -> p n j", j=BS) for a in range(3))
                    return k, v, q, S[:, n0:n0 + HALF], tmp[:, n0:n0 + HALF]

                def along_j(x):
                    return x.unsqueeze(2).broadcast_to([P, HALF, BS, BS])

                def along_i(x):
                    return x.unsqueeze(3).broadcast_to([P, HALF, BS, BS])

                def first_update(c):
                    for hf in range(2):
                        k, v, q, s, _ = parts(0, hf)
                        nc.vector.tensor_tensor(s, along_i(v), along_j(k), ALU.mult).then_inc(pre_tanh, 1)

                def read_out(c, t, hf):
                    k, v, q, s, w = parts(t, hf)
                    dve.wait_ge(post_tanh, c * 8 + 2 * t + hf + 1)
                    scan.done(nc.vector.tensor_tensor(w, s, along_j(q), ALU.mult))
                    scan.wait()
                    nc.vector.tensor_reduce(Sq[:, t, hf * HALF * BS:(hf + 1) * HALF * BS].rearrange(
                        "p (n i) -> p n i", i=BS), w, AX_X, ALU.add).then_inc(sq_done, 1)

                def update(c, t, hf):
                    k, v, q, s, w = parts(t, hf)
                    dl = delta[:, hf * HALF:hf * HALF + HALF, :]
                    dve.wait_ge(sq_done, c * 2 * BATCH + 2 * (t - 1) + hf + 1)
                    scan.done(nc.vector.tensor_tensor(w, s, along_j(k), ALU.mult))
                    scan.wait()
                    scan.done(nc.vector.tensor_reduce(dl, w, AX_X, ALU.add))
                    scan.wait()
                    scan.done(nc.vector.tensor_tensor(dl, v, dl, ALU.subtract))
                    scan.wait()
                    scan.done(nc.vector.tensor_tensor(w, along_i(dl), along_j(k), ALU.mult))
                    scan.wait()
                    nc.vector.tensor_tensor(s, s, w, ALU.add).then_inc(pre_tanh, 1)

                def scan_step(c, t):
                    for hf in range(2):
                        read_out(c, t, hf)
                        if t + 1 < BATCH:
                            update(c, t + 1, hf)

                def scan_out(c):
                    scan.end()
                    ln3.begin(c)
                    dve.wait_ge(sq_tanh, c + 1)
                    sqf = Sq[:].rearrange("p b d -> p (b d)")
                    thf = tmp[:, 0:HALF, :, :].rearrange("p n i j -> p (n i j)")
                    x3f = x3[:].rearrange("p b d -> p (b d)")
                    ln3.done(nc.vector.scalar_tensor_tensor(out=x3f, in0=thf, scalar=1.0, in1=sqf,
                                                            op0=ALU.add, op1=ALU.mult))
                    ln3.wait()
                    ln3.done(nc.vector.scalar_tensor_tensor(out=x3f, in0=x3f, scalar=0.5, in1=sqf,
                                                            op0=ALU.mult, op1=ALU.mult))
                    ln3.wait()
                    ln3.done(nc.vector.tensor_tensor(x3[:], x3[:], x2[:], ALU.add))
                    layernorm(dve, ln3, x3, mv3, rstd3, ve3, rs3, c, ln3_done)
                    ln3.end()

                def mix_inputs(d):
                    for n, (dst, mu, done) in enumerate(((wide_a, mu_k, mixk_done), (wide_b, mu_r, mixr_done))):
                        for k in range(KD):
                            dve.wait_ge(part_done, d * 4 + 2 * n + k + 1)
                            w = dst[:, k, :].rearrange("p (b n) -> p b n", b=BATCH)
                            nc.vector.scalar_tensor_tensor(out=w, in0=x3T[:, k, :, 1:P + 1], scalar=mu[:, k:k + 1],
                                                           in1=w, op0=ALU.mult, op1=ALU.add).then_inc(done, 1)

                def mix_result(d):
                    ln4.begin(d)
                    for n in range(2):
                        dve.wait_ge(dv_ps, d * 2 + n + 1)
                        dve.wait_ge(sig_done, d * 2 + n + 1)
                        w = y4[:, 2 * n:2 * n + 2, :]
                        nc.vector.scalar_tensor_tensor(out=w, in0=w, scalar=1.0,
                                                       in1=bank[4 + n][:].rearrange("p (b d) -> p b d", b=2),
                                                       op0=ALU.add, op1=ALU.mult).then_inc(gated4, 1)
                    dve.wait_ge(gated4, d * 2 + 2)
                    yf, xf = y4[:].rearrange("p b d -> p (b d)"), x3[:].rearrange("p b d -> p (b d)")
                    ln4.done(nc.vector.scalar_tensor_tensor(out=yf, in0=yf, scalar=0.5, in1=xf,
                                                            op0=ALU.mult, op1=ALU.add))
                    layernorm(dve, ln4, y4, mv4, rstd4, ve4, rs4, d, ln4_done)
                    ln4.end()

                def ffn_out(c):
                    ln2.begin(c)
                    dve.wait_ge(x1res_in, (c + 1) * 16)
                    for n in range(2):
                        dve.wait_ge(w3_ps, c * 2 + n + 1)
                        nc.vector.tensor_tensor(x2[:, 2 * n:2 * n + 2, :],
                                                bank[n][:].rearrange("p (b d) -> p b d", b=2),
                                                s3[:].unsqueeze(1).broadcast_to([P, 2, DIM]),
                                                ALU.mult).then_inc(scaled_done, 1)
                    for n in range(2):
                        dve.wait_ge(scaled_done, c * 2 + n + 1)
                        w = x2[:, 2 * n:2 * n + 2, :]
                        nc.vector.tensor_tensor(w, w, x1res[:, 2 * n:2 * n + 2, :], ALU.add).then_inc(r2_done, 1)
                    dve.wait_ge(r2_done, c * 2 + 2)
                    layernorm(dve, ln2, x2, mv2, rstd2, ve2, rs2, c, ln2_done)
                    ln2.end()

                def body(i, ffn, has_scan, mix, more):
                    c, d = i - 1, i - 2
                    if ffn:
                        for m in range(KH):
                            product(i, m)
                    if has_scan:
                        key_norms(c)
                        first_update(c)
                    if mix:
                        mix_inputs(d)
                    if has_scan:
                        scan_step(c, 0)
                        scan_step(c, 1)
                    if mix:
                        mix_result(d)
                    if has_scan:
                        scan_step(c, 2)
                        scan_step(c, 3)
                        scan_out(c)
                    if ffn:
                        ffn_out(i)

                schedule(dve, body)


def tables():
    import numpy as np

    pos = np.arange(LENGTH, dtype=np.float64)
    half = HEAD // 2
    base = (np.arange(0, HEAD, 2) + 0.4 * HEAD) / (1.4 * HEAD)
    scale = base[None, :] ** (pos[:, None] / 512.0)
    freq = 1.0 / 10000.0 ** (np.arange(half) / half)
    angle = (pos[:, None].astype(np.float32) * freq[None, :].astype(np.float32)).astype(np.float64)
    sign = np.tile([-1.0, 1.0], half)
    gammas = 1.0 - np.exp(np.linspace(np.log(1.0 / 32.0), np.log(1.0 / 512.0), HEADS))
    local = (np.arange(LENGTH) % P).astype(np.float64)
    rope = np.empty((LENGTH, 2, 2, HEADS, HEAD))
    for n, (s, power) in enumerate(((scale, local), (1.0 / scale, -local))):
        decay = gammas[None, :] ** power[:, None]
        for m, trig in enumerate((np.cos(angle), np.sin(angle))):
            row = np.repeat(trig * s, 2, axis=1) * (sign if m else 1.0)
            rope[:, m, n] = decay[:, :, None] * row[:, None, :]
    rope = rope.reshape(CHUNKS, P, 2, 2 * DIM)
    causal = np.triu(np.ones((P, P)))
    across = np.zeros((P, GROUPS, P))
    for g in range(GROUPS):
        for j in range(PER_GROUP):
            r = slice(j * HEAD, (j + 1) * HEAD)
            across[r, g, r] = gammas[g * PER_GROUP + j] ** P
    return {n: np.ascontiguousarray(a, dtype=np.float32) for n, a in
            dict(rope=rope, causal=causal, ident=np.eye(P), decay=across).items()}


def kernel(**inputs):
    import numpy as np
    import concourse.bacc as bacc
    from concourse.bass_utils import run_bass_kernel_spmd as run

    a = {n: np.asarray(x) for n, x in inputs.items()}

    def tiles(w):
        return w.reshape(-1, P, w.shape[1]).transpose(1, 0, 2)

    def columns(w):
        return w.reshape(-1, P).T

    X = a["L0_attn_X"]
    heads = [a[f"L0_attn_W_{n}"].transpose(1, 0, 2).reshape(DIM, DIM) for n in "QKV"]
    arrays = tables()
    arrays.update(
        xT=X.transpose(2, 0, 1).reshape(KD, P, BATCH, LENGTH).transpose(1, 0, 2, 3),
        x=X.reshape(BATCH, CHUNKS, P, DIM),
        wa=tiles(np.concatenate([*heads, a["L0_attn_W_G"]], axis=1)),
        wo=tiles(a["L0_attn_W_O"]),
        gnw=a["L0_attn_gn_weight"][None, :], gnb=a["L0_attn_gn_bias"][None, :],
        w1=tiles(a["L0_ffn_w1_w"].T), w2=tiles(a["L0_ffn_w2_w"].T),
        h1=tiles(a["L0_ffn_h1_w"].T), h2=tiles(a["L0_ffn_h2_w"].T), w3=tiles(a["L0_ffn_w3_w"].T),
        s1=columns(a["L0_ffn_w1_s"]), s2=columns(a["L0_ffn_w2_s"]),
        hs1=columns(a["L0_ffn_h1_s"]), hs2=columns(a["L0_ffn_h2_s"]), s3=a["L0_ffn_w3_s"][None, :],
        wkvq=tiles(np.concatenate([a["L1_attn_W_k"].T, a["L1_attn_W_v"].T, a["L1_attn_W_q"].T], axis=1)),
        wr=tiles(a["L1_ffn_W_r"].T), wk=tiles(a["L1_ffn_W_k"].T), wv=tiles(a["L1_ffn_W_v"].T),
        mur=columns(a["L1_ffn_mu_r"]), muk=columns(a["L1_ffn_mu_k"]),
    )
    arrays = {n: np.ascontiguousarray(x) for n, x in arrays.items()}
    nc = bacc.Bacc("TRN2", target_bir_lowering=False, num_devices=1)
    t = {n: nc.dram_tensor(f"{n}_dram", x.shape, mybir.dt.from_np(x.dtype), kind="ExternalInput").ap()
         for n, x in arrays.items()}
    t_out = nc.dram_tensor("out_dram", (BATCH, LENGTH, DIM), F32, kind="ExternalOutput").ap()
    t_x1 = nc.dram_tensor("x1_dram", (CHUNKS, P, BATCH, DIM), F32, kind="Internal").ap()
    build(nc, t["xT"], t["x"], t["rope"], t["causal"], t["ident"], t["decay"], t["wa"], t["wo"],
          t["gnw"], t["gnb"], t["w1"], t["w2"], t["h1"], t["h2"], t["w3"], t["s1"], t["s2"],
          t["hs1"], t["hs2"], t["s3"], t["wkvq"], t["wr"], t["wk"], t["wv"], t["mur"], t["muk"],
          t_out, t_x1)
    r = run(nc, [{f"{n}_dram": x for n, x in arrays.items()}], core_ids=[0])
    return r.results[0]["out_dram"]
```

```python
from contextlib import ExitStack

import concourse.bass as bass
from concourse import mybir

F32 = mybir.dt.float32
F32R = mybir.dt.float32r
I32 = mybir.dt.int32
ALU = mybir.AluOpType
ACT = mybir.ActivationFunctionType
AX_X = mybir.AxisListType.X

P = 128
BATCH, LENGTH, DIM = 4, 1024, 256
HEADS, HEAD = 8, 32
GROUPS, PER_GROUP = 2, 4
CHUNKS = LENGTH // P
KD = DIM // P
HID = 1024
KH = HID // P
NB, BS = 32, 8
HALF = NB // 2
TOK = BATCH * P
EPS = 1e-5
COL_W1, COL_W2 = 0, KD * HID
COL_H1 = 2 * KD * HID
COL_H2 = COL_H1 + KH * HID
COL_W3 = COL_H2 + KH * HID
FFN_COLS = COL_W3 + KH * DIM
RING = 4
LOOKS = 6
LOOK_STEP = 3752
LOOK_COLS = FFN_COLS - (LOOKS - 1) * LOOK_STEP


class Steps:

    def __init__(self, eng, sem, per_chunk):
        self.eng, self.sem, self.per_chunk = eng, sem, per_chunk

    def begin(self, c):
        self.c, self.k = c, 0

    def done(self, ins):
        ins.then_inc(self.sem, 1)
        self.k += 1

    def wait(self):
        self.eng.wait_ge(self.sem, self.c * self.per_chunk + self.k)

    def end(self):
        assert self.k == self.per_chunk, (self.k, self.per_chunk)


def build(nc, xT_d, x_d, rope_d, causal_d, ident_d, decay_d, wa_d, wo_d, gnw_d, gnb_d,
          ffn_d, s1_d, s2_d, hs1_d, hs2_d, s3_d, wkvq_d,
          wr_d, wk_d, wv_d, mur_d, muk_d, out_d, x1_d, ffn_s):
    top = ExitStack()

    def sb(ctx, name, shape, dtype=F32):
        return ctx.enter_context(nc.sbuf_tensor(name, shape, dtype))

    def sem(ctx, name):
        return ctx.enter_context(nc.semaphore(name))

    with top:
        bank = [top.enter_context(nc.psum_tensor(f"bank{n}", [P, 512], F32)) for n in range(8)]

        ident = sb(top, "ident", [P, P])
        inv_pow = sb(top, "inv_pow", [P, BATCH * HEADS])
        wkvq = sb(top, "wkvq", [P, KD, 3 * DIM])
        wr = sb(top, "wr", [P, KD, DIM])
        wk = sb(top, "wk", [P, KD, DIM])
        wv = sb(top, "wv", [P, KD, DIM])
        s1 = sb(top, "s1", [P, KH])
        s2 = sb(top, "s2", [P, KH])
        hs1 = sb(top, "hs1", [P, KH])
        hs2 = sb(top, "hs2", [P, KH])
        s1half = sb(top, "s1half", [P, KH])
        s12half = sb(top, "s12half", [P, KH])
        s3 = sb(top, "s3", [P, DIM])
        mu_r = sb(top, "mu_r", [P, KD])
        mu_k = sb(top, "mu_k", [P, KD])
        nu_r = sb(top, "nu_r", [P, KD])
        nu_k = sb(top, "nu_k", [P, KD])
        stats = sb(top, "stats", [P, BATCH, 6])
        spread = sb(top, "spread", [P, BATCH])
        low_sum = sb(top, "low_sum", [P, LOOKS + 2])
        low_all = sb(top, "low_all", [P, 1])
        low_max = sb(top, "low_max", [P, 1])
        wide_flag = sb(top, "wide_flag", [P, 1], I32)
        ffn_in = sem(top, "ffn_in")
        w123_in = sem(top, "w123_in")
        pow_ready = sem(top, "pow_ready")

        def layernorm(dve, steps, r, mv, rstd, ve_ready, rstd_ready, c, done_sem):
            steps.wait()
            for b in range(BATCH):
                ins = nc.vector.bn_stats(out=stats[:, b, :], in_=r[:, b, :])
            steps.done(ins)
            steps.wait()
            nc.vector.tensor_tensor(mv[:, :, 0], stats[:, :, 1], stats[:, :, 4], ALU.add)
            nc.vector.tensor_tensor(spread[:], stats[:, :, 1], stats[:, :, 4], ALU.subtract)
            steps.done(nc.vector.tensor_tensor(mv[:, :, 1], stats[:, :, 2], stats[:, :, 5], ALU.add))
            steps.wait()
            nc.vector.tensor_scalar(mv[:, :, 0], mv[:, :, 0], 0.5, None, ALU.mult)
            nc.vector.tensor_tensor(spread[:], spread[:], spread[:], ALU.mult)
            steps.done(nc.vector.tensor_scalar(mv[:, :, 1], mv[:, :, 1], 1.0 / DIM, EPS, ALU.mult, ALU.add))
            steps.wait()
            nc.vector.scalar_tensor_tensor(out=mv[:, :, 1], in0=spread[:], scalar=0.25, in1=mv[:, :, 1],
                                           op0=ALU.mult, op1=ALU.add).then_inc(ve_ready, 1)
            dve.wait_ge(rstd_ready, c + 1)
            for b in range(BATCH):
                ins = nc.vector.tensor_scalar(r[:, b, :], r[:, b, :], mv[:, b, 0:1], rstd[:, b:b + 1],
                                              ALU.subtract, ALU.mult)
            ins.then_inc(done_sem, 1)

        narrow = ExitStack()
        w1r = sb(narrow, "w1r", [P, KD, HID], F32R)
        w2r = sb(narrow, "w2r", [P, KD, HID], F32R)
        w3r = sb(narrow, "w3r", [P, KH, DIM], F32R)

        with ExitStack() as ctx:
            xT = sb(ctx, "xT", [P, KD, BATCH, P])
            xtok = sb(ctx, "xtok", [P, BATCH, DIM])
            rope = sb(ctx, "rope", [P, 2, 2 * DIM])
            causal = sb(ctx, "causal", [P, P])
            decay = sb(ctx, "decay", [P, GROUPS, P])
            wa = sb(ctx, "wa", [P, KD, 4 * DIM])
            wo = sb(ctx, "wo", [P, KD, DIM])
            gnw = sb(ctx, "gnw", [P, DIM])
            gnb = sb(ctx, "gnb", [P, DIM])
            qk = sb(ctx, "qk", [P, BATCH, 2 * DIM])
            turned = sb(ctx, "turned", [P, 2 * DIM])
            qkT = sb(ctx, "qkT", [P, BATCH, 4, P])
            v = sb(ctx, "v", [P, BATCH, DIM])
            gate = sb(ctx, "gate", [P, 2, BATCH, DIM])
            probs = sb(ctx, "probs", [P, PER_GROUP, 2, GROUPS, P])
            state = sb(ctx, "state", [P, BATCH, GROUPS, P])
            mean = sb(ctx, "mean", [P, BATCH, HEADS])
            var = sb(ctx, "var", [P, BATCH, HEADS])
            rgn = sb(ctx, "rgn", [P, BATCH, HEADS])
            y = sb(ctx, "y", [P, BATCH, DIM])
            ysq = sb(ctx, "ysq", [P, BATCH, DIM])
            zT = sb(ctx, "zT", [P, KD, TOK])
            r1 = sb(ctx, "r1", [P, BATCH, DIM])
            look = sb(ctx, "look", [P, LOOK_COLS])
            mv1 = sb(ctx, "mv1", [P, BATCH, 2])
            rstd1 = sb(ctx, "rstd1", [P, BATCH])

            const_in = sem(ctx, "const_in")
            xT_in = sem(ctx, "xT_in")
            xtok_in = sem(ctx, "xtok_in")
            rope_in = sem(ctx, "rope_in")
            x1_out = sem(ctx, "x1_out")
            proj_done = sem(ctx, "proj_done")
            v_done = sem(ctx, "v_done")
            tanh_done = sem(ctx, "tanh_done")
            gate_done = sem(ctx, "gate_done")
            rope_done = sem(ctx, "rope_done")
            turn_done = sem(ctx, "turn_done")
            t_done = sem(ctx, "t_done")
            qkT_done = sem(ctx, "qkT_done")
            scores_done = sem(ctx, "scores_done")
            probs_done = sem(ctx, "probs_done")
            y_done = sem(ctx, "y_done")
            mean_done = sem(ctx, "mean_done")
            centre_done = sem(ctx, "centre_done")
            sum_done = sem(ctx, "sum_done")
            state_done = sem(ctx, "state_done")
            ysq_done = sem(ctx, "ysq_done")
            gn_ve = sem(ctx, "gn_ve")
            gn_rstd = sem(ctx, "gn_rstd")
            z_done = sem(ctx, "z_done")
            zt_ps = sem(ctx, "zt_ps")
            zT_done = sem(ctx, "zT_done")
            wo_ps = sem(ctx, "wo_ps")
            r1_done = sem(ctx, "r1_done")
            ve1 = sem(ctx, "ve1")
            rs1 = sem(ctx, "rs1")
            ln1_done = sem(ctx, "ln1_done")
            gn_steps = sem(ctx, "gn_steps")
            copy_in = sem(ctx, "copy_in")
            look_in = sem(ctx, "look_in")
            low_bits = sem(ctx, "low_bits")
            low_added = sem(ctx, "low_added")
            low_done = sem(ctx, "low_done")
            low_reduced = sem(ctx, "low_reduced")
            flag_done = sem(ctx, "flag_done")
            N_GN = 7
            N_CONST = 7

            block = ctx.enter_context(nc.Block())

            @block.sync
            def _(sp):
                x_view = x_d.rearrange("b c p d -> p c b d")
                sp.dma_start(xT[:], xT_d[:, :, :, 0:P]).then_inc(xT_in, 16)
                sp.dma_start(wa[:], wa_d).then_inc(const_in, 16)
                sp.dma_start(rope[:], rope_d[0]).then_inc(rope_in, 16)
                sp.dma_start(ident[:], ident_d).then_inc(const_in, 16)
                sp.dma_start(causal[:], causal_d).then_inc(const_in, 16)
                sp.dma_start(xtok[:], x_view[:, 0]).then_inc(xtok_in, 16)
                sp.dma_start(decay[:], decay_d).then_inc(const_in, 16)
                sp.dma_start(gnw[:], gnw_d.broadcast_to([P, DIM])).then_inc(const_in, 16)
                sp.dma_start(gnb[:], gnb_d.broadcast_to([P, DIM])).then_inc(const_in, 16)
                sp.dma_start(wo[:], wo_d).then_inc(const_in, 16)

                def loads(c):
                    sp.wait_ge(proj_done, c * BATCH)
                    sp.dma_start(xT[:], xT_d[:, :, :, bass.ts(c, P)]).then_inc(xT_in, 16)
                    sp.wait_ge(rope_done, c * BATCH)
                    sp.dma_start(rope[:], rope_d[bass.ds(c, 1)].rearrange("o p a d -> (o p) a d")).then_inc(rope_in, 16)

                def loads_late(c):
                    sp.wait_ge(r1_done, c * 2)
                    sp.dma_start(xtok[:], x_rows(c)).then_inc(xtok_in, 16)
                    sp.wait_ge(ln1_done, c)
                    sp.dma_start(x1_rows(c - 1), r1[:]).then_inc(x1_out, 16)

                def x_rows(c):
                    return x_view[:, bass.ds(c, 1)].rearrange("p o b d -> p (o b) d")

                def x1_rows(c):
                    return x1_d[bass.ds(c, 1)].rearrange("o p b d -> (o p) b d")

                loads(1)
                sp.dma_start(ffn_s, ffn_d).then_inc(copy_in, 16)
                for dst, src in ((wkvq, wkvq_d), (wr, wr_d), (wk, wk_d), (wv, wv_d), (s1, s1_d),
                                 (s2, s2_d), (hs1, hs1_d), (hs2, hs2_d), (mu_r, mur_d), (mu_k, muk_d)):
                    sp.dma_start(dst[:], src).then_inc(ffn_in, 16)
                sp.dma_start(s3[:], s3_d.broadcast_to([P, DIM])).then_inc(ffn_in, 16)

                def look_at(c):
                    if not isinstance(c, int):
                        sp.wait_ge(low_added, c - 1)
                    sp.dma_start(look[:], ffn_d[:, bass.ds((c - 1) * LOOK_STEP, LOOK_COLS)]).then_inc(look_in, 16)

                look_at(1)
                loads_late(1)
                with sp.Fori(2, LOOKS + 1) as c:
                    loads(c)
                    look_at(c)
                    loads_late(c)
                sp.wait_ge(copy_in, 16)
                for dst, col in ((w1r, COL_W1), (w2r, COL_W2), (w3r, COL_W3)):
                    n = dst.shape[1] * dst.shape[2]
                    sp.dma_start(dst[:].bitcast(F32).rearrange("p k n -> p (k n)"),
                                 ffn_s[:, col:col + n]).then_inc(w123_in, 16)
                loads(CHUNKS - 1)
                loads_late(CHUNKS - 1)
                sp.wait_ge(ln1_done, CHUNKS)
                sp.dma_start(x1_rows(CHUNKS - 1), r1[:]).then_inc(x1_out, 16)
                sp.wait_ge(x1_out, 16 * CHUNKS)

            @block.tensor
            def _(pe):
                pe.wait_ge(const_in, 16 * N_CONST)

                def project(c, b):
                    if b == 0:
                        pe.wait_ge(xT_in, (c + 1) * 16)
                    if not (isinstance(c, int) and c == 0 and b == 0):
                        pe.wait_ge(rope_done, c * BATCH + b)
                        pe.wait_ge(v_done, c * BATCH + b)
                        pe.wait_ge(gate_done, c * BATCH + b)
                    for half in range(2):
                        for k in range(KD):
                            ins = nc.tensor.matmul(bank[half][:], xT[:, k, b, :],
                                                   wa[:, k, half * 512:half * 512 + 512],
                                                   start=(k == 0), stop=(k == KD - 1))
                    ins.then_inc(proj_done, 1)

                def turn(c, b, first):
                    pe.wait_ge(rope_done, c * BATCH + b + 1)
                    if not first and b >= 2:
                        pe.wait_ge(r1_done, c * 2 + b - 3)
                    for t in range(4):
                        ins = nc.tensor.transpose(bank[4 + b][:, t * P:t * P + P],
                                                  qk[:, b, t * P:t * P + P], ident[:])
                    ins.then_inc(t_done, 1)

                def scores(c, r):
                    pe.wait_ge(qkT_done, c * BATCH + BATCH)
                    if r == 1:
                        pe.wait_ge(probs_done, c * 8 + 4)
                    for b2 in range(2):
                        for g in range(GROUPS):
                            for j in range(PER_GROUP):
                                rows = slice(HEAD * j, HEAD * j + HEAD)
                                col = (b2 * GROUPS + g) * P
                                ins = nc.tensor.matmul(bank[4 + j][:, col:col + P],
                                                       qkT[rows, 2 * r + b2, 2 + g, :],
                                                       qkT[rows, 2 * r + b2, g, :], start=True, stop=True)
                    ins.then_inc(scores_done, 1)

                def outputs(c, b):
                    if b % 2 == 0:
                        pe.wait_ge(probs_done, c * 8 + 4 * (b // 2) + 4)
                        pe.wait_ge(v_done, c * BATCH + BATCH)
                    pe.wait_ge(state_done, c * BATCH + b + 3)
                    pb = bank[2 + b % 2]
                    for g in range(GROUPS):
                        nc.tensor.matmul(pb[:, g * P:g * P + P], qkT[:, b, g, :], state[:, b, g, :],
                                         start=True, stop=False, skip_group_check=True)
                        for j in range(PER_GROUP):
                            h = g * PER_GROUP + j
                            nc.tensor.matmul(pb[:, h * HEAD:h * HEAD + HEAD], probs[:, j, b % 2, g, :],
                                             v[:, b, h * HEAD:h * HEAD + HEAD], start=False,
                                             stop=(j == PER_GROUP - 1), skip_group_check=True)
                    for g in range(GROUPS):
                        ins = nc.tensor.matmul(pb[:, DIM + g * P:DIM + g * P + P],
                                               qk[:, b, DIM + g * P:DIM + g * P + P],
                                               v[:, b, g * P:g * P + P], start=True, stop=True)
                    ins.then_inc(y_done, 1)

                def out_product(c):
                    pe.wait_ge(z_done, c + 1)
                    for k in range(KD):
                        for b in range(BATCH):
                            ins = nc.tensor.transpose(bank[4 + k][:, b * P:b * P + P],
                                                      y[:, b, k * P:k * P + P], ident[:])
                        ins.then_inc(zt_ps, 1)
                    pe.wait_ge(zT_done, c * 2 + 2)
                    for b in range(BATCH):
                        for k in range(KD):
                            ins = nc.tensor.matmul(bank[6 + b // 2][:, (b % 2) * DIM:(b % 2) * DIM + DIM],
                                                   zT[:, k, b * P:b * P + P], wo[:, k, :],
                                                   start=(k == 0), stop=(k == KD - 1))
                        if b % 2:
                            ins.then_inc(wo_ps, 1)

                def body(c, last=False):
                    scores(c, 0)
                    if not last:
                        project(c + 1, 0)
                    outputs(c, 0)
                    outputs(c, 1)
                    scores(c, 1)
                    if not last:
                        project(c + 1, 1)
                    outputs(c, 2)
                    outputs(c, 3)
                    if not last:
                        project(c + 1, 2)
                        project(c + 1, 3)
                    out_product(c)
                    if not last:
                        for b in range(BATCH):
                            turn(c + 1, b, False)

                for b in range(BATCH):
                    project(0, b)
                for b in range(BATCH):
                    turn(0, b, True)
                body(0)
                with pe.Fori(1, CHUNKS - 1, 2) as c:
                    body(c)
                    body(c + 1)
                body(CHUNKS - 1, last=True)

            @block.scalar
            def _(act):
                def value_gate(c, b, parity, first):
                    act.wait_ge(proj_done, c * BATCH + b + 1)
                    if not first:
                        act.wait_ge(y_done, (c - 1) * BATCH + b + 1)
                    nc.scalar.copy(v[:, b, :], bank[1][:, 0:DIM]).then_inc(v_done, 1)
                    nc.scalar.activation(gate[:, parity, b, :], bank[1][:, DIM:2 * DIM], ACT.Tanh,
                                         scale=0.5).then_inc(tanh_done, 1)

                def square(c, b):
                    act.wait_ge(centre_done, c * BATCH + b + 1)
                    nc.scalar.activation(ysq[:, b, :], y[:, b, :], ACT.Square).then_inc(ysq_done, 1)

                def z_transposed(c):
                    for k in range(KD):
                        act.wait_ge(zt_ps, c * 2 + k + 1)
                        nc.scalar.copy(zT[:, k, :], bank[4 + k][:]).then_inc(zT_done, 1)

                def turned_out(c):
                    for b in range(BATCH):
                        act.wait_ge(t_done, c * BATCH + b + 1)
                        nc.scalar.copy(qkT[:, b, :, :], bank[4 + b][:].rearrange("p (t n) -> p t n", t=4)
                                       ).then_inc(qkT_done, 1)

                def add_low_bits(c):
                    act.wait_ge(low_bits, c)
                    nc.scalar.activation(look[:], look[:].bitcast(I32), ACT.Copy,
                                         accum_out=low_sum[:, bass.ds(c, 1)]).then_inc(low_added, 1)

                def body(c, parity, last=False):
                    nxt = 1 - parity
                    if not last:
                        value_gate(c + 1, 0, nxt, False)
                    square(c, 0)
                    square(c, 1)
                    if not last:
                        value_gate(c + 1, 1, nxt, False)
                    square(c, 2)
                    square(c, 3)
                    if not last:
                        value_gate(c + 1, 2, nxt, False)
                        value_gate(c + 1, 3, nxt, False)
                    z_transposed(c)
                    if not last:
                        turned_out(c + 1)
                    if not (isinstance(c, int)):
                        add_low_bits(c)

                for b in range(BATCH):
                    value_gate(0, b, 0, True)
                turned_out(0)
                body(0, 0)
                with act.Fori(1, CHUNKS - 1, 2) as c:
                    body(c, 1)
                    body(c + 1, 0)
                body(CHUNKS - 1, 1, last=True)

            @block.gpsimd
            def _(pool):
                nc.gpsimd.memset(inv_pow[:], -0.5).then_inc(pow_ready, 1)
                pool.wait_ge(pow_ready, 1)

                def body(c):
                    pool.wait_ge(gn_ve, c + 1)
                    nc.gpsimd.tensor_tensor(rgn[:].rearrange("p b h -> p (b h)"), var[:].rearrange("p b h -> p (b h)"),
                                            inv_pow[:, 0:BATCH * HEADS], ALU.pow).then_inc(gn_rstd, 1)
                    pool.wait_ge(ve1, c + 1)
                    nc.gpsimd.tensor_tensor(rstd1[:], mv1[:, :, 1], inv_pow[:, 0:BATCH], ALU.pow).then_inc(rs1, 1)

                with pool.Fori(0, CHUNKS) as c:
                    body(c)
                pool.wait_ge(low_done, 1)
                nc.gpsimd.partition_all_reduce(low_max[:], low_all[:], P, bass.bass_isa.ReduceOp.max
                                               ).then_inc(low_reduced, 1)

            @block.vector
            def _(dve):
                for b in range(BATCH):
                    nc.vector.memset(state[:, b, :, :], 0.0).then_inc(state_done, 1)
                dve.wait_ge(const_in, 16 * N_CONST)
                steps = Steps(dve, gn_steps, N_GN)

                def rotate(c, b, parity, first):
                    if b == 0:
                        dve.wait_ge(rope_in, (c + 1) * 16)
                    dve.wait_ge(proj_done, c * BATCH + b + 1)
                    if not first:
                        dve.wait_ge(y_done, (c - 1) * BATCH + b + 1)
                    raw = bank[0][:].rearrange("p (e two) -> p e two", two=2)
                    sin = rope[:, 1, :].rearrange("p (e two) -> p e two", two=2)
                    tur = turned[:].rearrange("p (e two) -> p e two", two=2)
                    nc.vector.tensor_tensor(qk[:, b, :], bank[0][:], rope[:, 0, :], ALU.mult)
                    nc.vector.tensor_tensor(tur[:, :, 0], raw[:, :, 1], sin[:, :, 0], ALU.mult)
                    nc.vector.tensor_tensor(tur[:, :, 1], raw[:, :, 0], sin[:, :, 1], ALU.mult).then_inc(turn_done, 1)
                    dve.wait_ge(turn_done, c * BATCH + b + 1)
                    nc.vector.tensor_tensor(qk[:, b, :], qk[:, b, :], turned[:], ALU.add).then_inc(rope_done, 1)
                    dve.wait_ge(tanh_done, c * BATCH + b + 1)
                    nc.vector.scalar_tensor_tensor(out=gate[:, parity, b, :], in0=gate[:, parity, b, :], scalar=1.0,
                                                   in1=bank[1][:, DIM:2 * DIM], op0=ALU.add,
                                                   op1=ALU.mult).then_inc(gate_done, 1)

                def masked(c, r):
                    dve.wait_ge(scores_done, c * 2 + r + 1)
                    for j in range(PER_GROUP):
                        nc.vector.tensor_tensor(
                            probs[:, j, :, :, :].rearrange("p b g n -> p (b g) n"),
                            bank[4 + j][:].rearrange("p (x n) -> p x n", n=P),
                            causal[:].unsqueeze(1).broadcast_to([P, 4, P]), ALU.mult).then_inc(probs_done, 1)

                def collect(c, b):
                    dve.wait_ge(y_done, c * BATCH + b + 1)
                    pb = bank[2 + b % 2]
                    y3 = pb[:, 0:DIM].rearrange("p (h e) -> p h e", e=HEAD)
                    nc.vector.tensor_reduce(mean[:, b, :], y3, AX_X, ALU.add).then_inc(mean_done, 1)
                    st = state[:, b, :, :].rearrange("p g e -> p (g e)")
                    nc.vector.tensor_tensor(st, st, pb[:, DIM:2 * DIM], ALU.add).then_inc(sum_done, 1)
                    dve.wait_ge(mean_done, c * 2 * BATCH + 2 * b + 1)
                    nc.vector.tensor_scalar(mean[:, b, :], mean[:, b, :], 1.0 / HEAD, None, ALU.mult).then_inc(mean_done, 1)
                    dve.wait_ge(sum_done, c * BATCH + b + 1)
                    dve.wait_ge(mean_done, c * 2 * BATCH + 2 * b + 2)
                    nc.vector.tensor_tensor(y[:, b, :].rearrange("p (h e) -> p h e", e=HEAD), y3,
                                            mean[:, b, :].unsqueeze(2).broadcast_to([P, HEADS, HEAD]),
                                            ALU.subtract).then_inc(centre_done, 1)
                    nc.vector.tensor_tensor(st, st, decay[:].rearrange("p g e -> p (g e)"),
                                            ALU.mult).then_inc(state_done, 1)

                def variance(c):
                    dve.wait_ge(ysq_done, c * BATCH + BATCH)
                    vflat = var[:].rearrange("p b h -> p (b h)")
                    steps.done(nc.vector.tensor_reduce(vflat, ysq[:].rearrange("p b (h e) -> p (b h) e", e=HEAD),
                                                       AX_X, ALU.add))
                    steps.wait()
                    nc.vector.tensor_scalar(vflat, vflat, 1.0 / HEAD, EPS, ALU.mult, ALU.add).then_inc(gn_ve, 1)

                def gated(c, parity):
                    dve.wait_ge(gn_rstd, c + 1)
                    yh = y[:].rearrange("p b (h e) -> p (b h) e", e=HEAD)
                    dve.wait_ge(centre_done, c * BATCH + BATCH)
                    steps.done(nc.vector.tensor_tensor(
                        yh, yh, rgn[:].rearrange("p b h -> p (b h)").unsqueeze(2).broadcast_to([P, BATCH * HEADS, HEAD]),
                        ALU.mult))
                    steps.wait()
                    steps.done(nc.vector.tensor_tensor(y[:], y[:], gnw[:].unsqueeze(1).broadcast_to([P, BATCH, DIM]), ALU.mult))
                    steps.wait()
                    steps.done(nc.vector.tensor_tensor(y[:], y[:], gnb[:].unsqueeze(1).broadcast_to([P, BATCH, DIM]), ALU.add))
                    steps.wait()
                    dve.wait_ge(gate_done, c * BATCH + BATCH)
                    nc.vector.scalar_tensor_tensor(out=y[:].rearrange("p b d -> p (b d)"),
                                                   in0=gate[:, parity, :, :].rearrange("p b d -> p (b d)"), scalar=0.5,
                                                   in1=y[:].rearrange("p b d -> p (b d)"), op0=ALU.mult,
                                                   op1=ALU.mult).then_inc(z_done, 1)

                def residual(c, first):
                    dve.wait_ge(xtok_in, (c + 1) * 16)
                    if not first:
                        dve.wait_ge(x1_out, c * 16)
                    for n in range(2):
                        dve.wait_ge(wo_ps, c * 2 + n + 1)
                        nc.vector.tensor_tensor(r1[:, 2 * n:2 * n + 2, :],
                                                bank[6 + n][:].rearrange("p (b d) -> p b d", b=2),
                                                xtok[:, 2 * n:2 * n + 2, :], ALU.add).then_inc(r1_done, 1)
                    dve.wait_ge(r1_done, c * 2 + 2)
                    layernorm(dve, steps, r1, mv1, rstd1, ve1, rs1, c, ln1_done)
                    steps.end()

                def body(c, parity, first=False, last=False):
                    steps.begin(c)
                    masked(c, 0)
                    if not last:
                        rotate(c + 1, 0, 1 - parity, False)
                    collect(c, 0)
                    collect(c, 1)
                    masked(c, 1)
                    if not last:
                        rotate(c + 1, 1, 1 - parity, False)
                    collect(c, 2)
                    collect(c, 3)
                    variance(c)
                    if not last:
                        rotate(c + 1, 2, 1 - parity, False)
                    gated(c, parity)
                    if not last:
                        rotate(c + 1, 3, 1 - parity, False)
                    if not isinstance(c, int):
                        dve.wait_ge(look_in, c * 16)
                        w = look[:].bitcast(I32)
                        nc.vector.tensor_scalar(w, w, 0xFFF, None, ALU.bitwise_and).then_inc(low_bits, 1)
                    residual(c, first)

                for b in range(BATCH):
                    rotate(0, b, 0, True)
                body(0, 0, first=True)
                with dve.Fori(1, CHUNKS - 1, 2) as c:
                    body(c, 1)
                    body(c + 1, 0)
                body(CHUNKS - 1, 1, last=True)
                dve.wait_ge(low_added, LOOKS)
                nc.vector.tensor_reduce(low_all[:], low_sum[:, 1:LOOKS + 1], AX_X, ALU.add).then_inc(low_done, 1)
                dve.wait_ge(low_reduced, 1)
                nc.vector.tensor_scalar(wide_flag[:], low_max[:], 0.0, None, ALU.is_gt).then_inc(flag_done, 1)
                dve.wait_ge(flag_done, 1)

        def shared(ctx):
            t = {}
            for name, shape in (
                    ("x1in", [P, BATCH, DIM]),
                    ("x1res", [P, BATCH, DIM]),
                    ("wide_a", [P, KD, TOK]),
                    ("wide_b", [P, KD, TOK]),
                    ("x2", [P, BATCH, DIM]),
                    ("x2res", [P, BATCH, DIM]),
                    ("kvq", [P, BATCH, 3 * DIM]),
                    ("S", [P, NB, BS, BS]),
                    ("tmp", [P, NB, BS, BS]),
                    ("norm", [P, BATCH, NB]),
                    ("root", [P, BATCH, NB]),
                    ("newton", [P, BATCH, NB]),
                    ("delta", [P, NB, BS]),
                    ("Sq", [P, BATCH, DIM]),
                    ("x3", [P, BATCH, DIM]),
                    ("x3T", [P, KD, BATCH, P + 1]),
                    ("y4", [P, BATCH, DIM]),
                    ("mv2", [P, BATCH, 2]), ("rstd2", [P, BATCH]),
                    ("mv3", [P, BATCH, 2]), ("rstd3", [P, BATCH]),
                    ("mv4", [P, BATCH, 2]), ("rstd4", [P, BATCH])):
                t[name] = sb(ctx, f"{name}_{len(made)}", shape)
            made.append(t)
            return t

        made = []
        with ExitStack() as ctx:
            tn = shared(ctx)
            tn["x1hi"] = sb(ctx, "x1hi", [P, KD, TOK], F32R)
            tn["x1lo"] = sb(ctx, "x1lo", [P, KD, TOK], F32R)
            tn["whole"] = sb(ctx, "whole", [P, 4, TOK])
            tn["a_hi"] = sb(ctx, "a_hi", [P, KH, TOK], F32R)
            tn["a_lo"] = sb(ctx, "a_lo", [P, KH, TOK], F32R)
            tn["b_hi"] = sb(ctx, "b_hi", [P, KH, TOK], F32R)
            tn["b_lo"] = sb(ctx, "b_lo", [P, KH, TOK], F32R)
            tn["ring"] = sb(ctx, "ring", [P, RING, KH, P], F32R)
        narrow.close()
        with ExitStack() as ctx:
            tw = shared(ctx)
            tw["a"] = sb(ctx, "hid_a", [P, KH, TOK])
            tw["b"] = sb(ctx, "hid_b", [P, KH, TOK])
            tw["ffn"] = sb(ctx, "ffn_w", [P, FFN_COLS])

        with ExitStack() as ctx:
            sem2 = lambda name: sem(ctx, name)
            x1in_in, x1res_in, out_done = sem2("x1in_in"), sem2("x1res_in"), sem2("out_done")
            wide_in = sem2("wide_in")
            ring_in = [sem2(f"ring_in{n}") for n in range(RING)]
            prep = sem2("prep")
            x1T_ps, x1T_done, x1lo_done = sem2("x1T_ps"), sem2("x1T_done"), sem2("x1lo_done")
            w12_ps, th_done, prod_mid, prod_done = sem2("w12_ps"), sem2("th_done"), sem2("prod_mid"), sem2("prod_done")
            hid_ps, act_done = sem2("hid_ps"), sem2("act_done")
            hi_done, lo_done = sem2("hi_done"), sem2("lo_done")
            w3_ps, scaled_done, r2_done = sem2("w3_ps"), sem2("scaled_done"), sem2("r2_done")
            ve2, rs2, ln2_steps, ln2_done = sem2("ve2"), sem2("rs2"), sem2("ln2_steps"), sem2("ln2_done")
            x2T_ps, x2T_done, kvq_ps, kvq_done = sem2("x2T_ps"), sem2("x2T_done"), sem2("kvq_ps"), sem2("kvq_done")
            ksq_done = sem2("ksq_done")
            scan_steps, tail_steps, x2_kept = sem2("scan_steps"), sem2("tail_steps"), sem2("x2_kept")
            pre_tanh, post_tanh = sem2("pre_tanh"), sem2("post_tanh")
            sq_done, sq_tanh = sem2("sq_done"), sem2("sq_tanh")
            ve3, rs3, ln3_steps, ln3_done = sem2("ve3"), sem2("rs3"), sem2("ln3_steps"), sem2("ln3_done")
            x3T_ps, x3T_col, x3T_done = sem2("x3T_ps"), sem2("x3T_col"), sem2("x3T_done")
            part_done, mixk_done, mixr_done = sem2("part_done"), sem2("mixk_done"), sem2("mixr_done")
            dk_ps, relu_done, kact_done = sem2("dk_ps"), sem2("relu_done"), sem2("kact_done")
            dr_ps, sig_done, dv_ps, gated4 = sem2("dr_ps"), sem2("sig_done"), sem2("dv_ps"), sem2("gated4")
            ve4, rs4, ln4_steps, ln4_done = sem2("ve4"), sem2("rs4"), sem2("ln4_steps"), sem2("ln4_done")
            N_FFN_IN = 11
            N_LN2, N_LN3, N_LN4 = 3, 6, 4
            N_NORM = 16
            N_SCAN = N_NORM + 2 * (BATCH - 1) + 2 * 4 * (BATCH - 1)
            N_TAIL = 2

            def pair(m):
                return (6, 4, 2, 6, 4, 0, 2, 0)[m]
            SPLITS = 3 * KH

            def schedule(eng, body):
                for i in range(3):
                    body(i, True, i >= 1, i >= 2, i + 1 < CHUNKS)
                with eng.Fori(3, CHUNKS - 1) as i:
                    body(i, True, True, True, True)
                body(CHUNKS - 1, True, True, True, False)
                body(CHUNKS, False, True, True, False)
                body(CHUNKS + 1, False, False, True, False)

            def sync_program(sp, narrow_w):
                t = tn if narrow_w else tw

                def x1_rows(c):
                    return x1_d[bass.ds(c, 1)].rearrange("o p b d -> (o p) b d")

                def ring_load(c, n, free=None):
                    if free is not None:
                        sp.wait_ge(hid_ps, free)
                    sp.dma_start(t["ring"][:, n % RING].bitcast(F32).rearrange("p k n -> p (k n)"),
                                 ffn_s[:, COL_H1 + n * HID:COL_H1 + (n + 1) * HID]).then_inc(ring_in[n % RING], 16)

                out_view = out_d.rearrange("b (c p) d -> p c b d", p=P)
                sp.dma_start(t["x1in"][:], x1_rows(0)).then_inc(x1in_in, 16)
                sp.dma_start(t["x1res"][:], x1_rows(0)).then_inc(x1res_in, 16)
                if narrow_w:
                    for n in range(RING):
                        ring_load(0, n)
                else:
                    sp.dma_start(t["ffn"][:], ffn_d).then_inc(wide_in, 16)

                def body(i, ffn, scan, mix, more):
                    if more:
                        sp.wait_ge(x1T_ps, i * 2 + 2)
                        sp.dma_start(t["x1in"][:], x1_rows(i + 1)).then_inc(x1in_in, 16)
                    if scan and ffn:
                        sp.wait_ge(r2_done, i * 2)
                        sp.dma_start(t["x1res"][:], x1_rows(i)).then_inc(x1res_in, 16)
                    if ffn and narrow_w:
                        for n in range(RING, 2 * KH):
                            ring_load(i, n, i * 2 * KH + n - RING + 1)
                    if mix:
                        sp.wait_ge(ln4_done, i - 1)
                        sp.dma_start(out_view[:, bass.ds(i - 2, 1)].rearrange("p o b d -> p (o b) d"),
                                     t["y4"][:]).then_inc(out_done, 16)
                    if more and narrow_w:
                        for n in range(RING):
                            ring_load(i + 1, n, i * 2 * KH + 2 * KH - RING + n + 1)

                schedule(sp, body)
                sp.wait_ge(out_done, 16 * CHUNKS)

            def tensor_program(pe, narrow_w):
                t = tn if narrow_w else tw
                wide_a, wide_b, x2, x3 = t["wide_a"], t["wide_b"], t["x2"], t["x3"]
                pe.wait_ge(ffn_in, 16 * N_FFN_IN)
                if narrow_w:
                    pe.wait_ge(w123_in, 16 * 3)
                else:
                    pe.wait_ge(wide_in, 16)

                def weight(col, k, n, a, z):
                    return t["ffn"][:, col + k * n + a:col + k * n + z]

                def transposes(src, lo, ps):
                    for k in range(KD):
                        for b in range(BATCH):
                            ins = nc.tensor.transpose(bank[lo + k][:, b * P:b * P + P], src[:, b, k * P:k * P + P],
                                                      ident[:])
                        ins.then_inc(ps, 1)

                def x1_transposed(c):
                    pe.wait_ge(x1in_in, (c + 1) * 16)
                    transposes(t["x1in"], 6, x1T_ps)

                def product(out, pairs, first=True, last=True):
                    for n, (a, b) in enumerate(pairs):
                        ins = nc.tensor.matmul(out, a, b, start=(first and n == 0), stop=(last and n == len(pairs) - 1))
                    return ins

                def up(c, tiles, first=False):
                    if tiles[0] == 0:
                        pe.wait_ge(x1T_done, c * 2 + 2)
                        if narrow_w:
                            pe.wait_ge(x1lo_done, c * 2 + 2)
                    for m in tiles:
                        before = {3: 0, 4: 1, 6: 2, 7: 5}
                        if m in before:
                            pe.wait_ge(prod_done, c * KH + before[m] + 1)
                        elif m == 1 and not (isinstance(c, int) and c < 3):
                            pe.wait_ge(gated4, (c - 2) * 2)
                        elif m == 5 and not first:
                            pe.wait_ge(scaled_done, c * 2)
                        elif m == 2 and not (isinstance(c, int) and c == 0):
                            if narrow_w:
                                pe.wait_ge(hi_done, c * SPLITS)
                            else:
                                pe.wait_ge(act_done, c * 2 * KH)
                        cols = slice(m * P, m * P + P)
                        for n in range(2):
                            if narrow_w:
                                w = (w1r, w2r)[n]
                                pairs = [(w[:, k, cols], x[:, k, :]) for k in range(KD) for x in (t["x1hi"], t["x1lo"])]
                            else:
                                pairs = [(weight((COL_W1, COL_W2)[n], k, HID, m * P, m * P + P), wide_a[:, k, :])
                                         for k in range(KD)]
                            ins = product(bank[pair(m) + n][:], pairs)
                        ins.then_inc(w12_ps, 1)

                def hidden(c, layer, m):
                    n = layer * KH + m
                    if not narrow_w:
                        if m == 0 and layer == 0:
                            pe.wait_ge(prod_done, c * KH + KH)
                        if m == 0 and layer == 1:
                            pe.wait_ge(act_done, c * 2 * KH + KH)
                        if n >= 4:
                            pe.wait_ge(act_done, c * 2 * KH + n - 3)
                        src = t["ab"[layer]]
                        ins = product(bank[m % 4][:],
                                      [(weight(COL_H1, n * KH + k, P, 0, P), src[:, k, :]) for k in range(KH)])
                        ins.then_inc(hid_ps, 1)
                        return
                    pe.wait_ge(ring_in[n % RING], c * (2 * KH // RING) * 16 + (n // RING + 1) * 16)
                    if n >= 4:
                        pe.wait_ge(hi_done, c * SPLITS + KH + n - 3)
                    else:
                        pe.wait_ge(prod_done, c * KH + KH)
                    hi, lo = (t["a_hi"], t["a_lo"]) if layer == 0 else (t["b_hi"], t["b_lo"])
                    w = t["ring"][:, n % RING]
                    if m == 0:
                        for k in range(KH):
                            pe.wait_ge(hi_done, c * SPLITS + layer * KH + k + 1)
                            product(bank[0][:], [(w[:, k, :], hi[:, k, :])], first=(k == 0), last=False)
                        pe.wait_ge(lo_done, c * SPLITS + layer * KH + KH)
                        ins = product(bank[0][:], [(w[:, k, :], lo[:, k, :]) for k in range(KH)], first=False)
                    else:
                        ins = product(bank[m % 4][:], [(w[:, k, :], x[:, k, :]) for k in range(KH) for x in (hi, lo)])
                    ins.then_inc(hid_ps, 1)

                def down(c):
                    if narrow_w:
                        pe.wait_ge(hi_done, c * SPLITS + 3 * KH)
                        pe.wait_ge(lo_done, c * SPLITS + 3 * KH)
                    else:
                        pe.wait_ge(act_done, c * 2 * KH + 2 * KH)
                    for b in range(BATCH):
                        rows = slice(b * P, b * P + P)
                        if narrow_w:
                            pairs = [(x[:, k, rows], w3r[:, k, :]) for k in range(KH) for x in (t["a_hi"], t["a_lo"])]
                        else:
                            pairs = [(t["a"][:, k, rows], weight(COL_W3, k, DIM, 0, DIM)) for k in range(KH)]
                        ins = product(bank[b // 2][:, (b % 2) * DIM:(b % 2) * DIM + DIM], pairs)
                        if b % 2:
                            ins.then_inc(w3_ps, 1)

                def scan_inputs(c):
                    pe.wait_ge(x2T_done, c * 2 + 2)
                    for b in range(BATCH):
                        lo = 4 if b % 2 == 0 else 6
                        if b >= 2:
                            pe.wait_ge(kvq_done, c * 2 * BATCH + 2 * (b - 1))
                        for n, (a, z) in enumerate(((0, 512), (512, 768))):
                            ins = product(bank[lo + n][:, 0:z - a],
                                          [(wide_b[:, k, b * P:b * P + P], wkvq[:, k, a:z]) for k in range(KD)])
                        ins.then_inc(kvq_ps, 1)

                def by_row(src, w, lo, ps):
                    for b in range(BATCH):
                        ins = product(bank[lo + b // 2][:, (b % 2) * DIM:(b % 2) * DIM + DIM],
                                      [(src[:, k, b * P:b * P + P], w[:, k, :]) for k in range(KD)])
                        if b % 2:
                            ins.then_inc(ps, 1)

                def mix_in(c):
                    pe.wait_ge(mixk_done, c * 2 + 2)
                    for m in range(KD):
                        product(bank[4 + m][:], [(wk[:, k, m * P:m * P + P], wide_a[:, k, :]) for k in range(KD)]
                                ).then_inc(dk_ps, 1)
                    pe.wait_ge(mixr_done, c * 2 + 2)
                    by_row(wide_b, wr, 6, dr_ps)

                def body(i, ffn, scan, mix, more):
                    c, d = i - 1, i - 2
                    if ffn:
                        up(i, range(3, KH - 1), first=not scan)
                    if scan:
                        pe.wait_ge(ln2_done, c + 1)
                        if ffn:
                            pe.wait_ge(prod_done, i * KH + 4)
                        transposes(x2, 6, x2T_ps)
                    if ffn:
                        up(i, [KH - 1])
                    if scan:
                        if ffn:
                            pe.wait_ge(prod_done, i * KH + 5)
                        scan_inputs(c)
                    if ffn:
                        hidden(i, 0, 0)
                    if mix:
                        pe.wait_ge(ln3_done, d + 1)
                        if scan:
                            pe.wait_ge(kvq_done, c * 2 * BATCH + 6)
                        transposes(x3, 4, x3T_ps)
                    if ffn:
                        for m in range(1, KH):
                            hidden(i, 0, m)
                    if mix:
                        mix_in(d)
                    if ffn:
                        hidden(i, 1, 0)
                    if mix:
                        pe.wait_ge(kact_done, d * 2 + 2)
                        by_row(wide_a, wv, 4, dv_ps)
                    if ffn:
                        hidden(i, 1, 1)
                        if more:
                            if mix:
                                pe.wait_ge(sig_done, d * 2 + 2)
                            elif scan:
                                pe.wait_ge(kvq_done, i * 2 * BATCH)
                            x1_transposed(i + 1)
                        for m in range(2, KH):
                            hidden(i, 1, m)
                        if more:
                            up(i + 1, range(3))
                        down(i)

                x1_transposed(0)
                up(0, range(3))
                schedule(pe, body)

            def scalar_program(act, narrow_w):
                t = tn if narrow_w else tw
                wide_a, wide_b, S, tmp, kvq, x2 = t["wide_a"], t["wide_b"], t["S"], t["tmp"], t["kvq"], t["x2"]
                x3T, y4 = t["x3T"], t["y4"]
                act.wait_ge(ffn_in, 16 * N_FFN_IN)
                act.wait_ge(prep, 9)

                def evacuate(dst, lo, c, ps, done):
                    for k in range(KD):
                        act.wait_ge(ps, c * 2 + k + 1)
                        nc.scalar.copy(dst[:, k, :], bank[lo + k][:]).then_inc(done, 1)

                def scan_tanh(c, n, hf):
                    act.wait_ge(pre_tanh, c * 8 + 2 * n + hf + 1)
                    half = S[:, hf * HALF:hf * HALF + HALF, :, :].rearrange("p n i j -> p (n i j)")
                    nc.scalar.activation(half, half, ACT.Tanh).then_inc(post_tanh, 1)

                def product_hi(c, m):
                    act.wait_ge(prod_done, c * KH + m + 1)
                    nc.scalar.copy(t["a_hi"][:, m, :], t["whole"][:, m % 4, :]).then_inc(hi_done, 1)

                def gelu(c, layer, m):
                    n = layer * KH + m
                    act.wait_ge(hid_ps, c * 2 * KH + n + 1)
                    scale = (hs1, hs2)[layer][:, m:m + 1]
                    if not narrow_w:
                        nc.scalar.activation(t["ba"[layer]][:, m, :], bank[m % 4][:], ACT.Gelu,
                                             scale=scale).then_inc(act_done, 1)
                        return
                    act.wait_ge(lo_done, c * SPLITS + KH + n - 3)
                    nc.scalar.activation(t["whole"][:, m % 4, :], bank[m % 4][:], ACT.Gelu, scale=scale).then_inc(act_done, 1)
                    nc.scalar.activation((t["b_hi"], t["a_hi"])[layer][:, m, :], bank[m % 4][:], ACT.Gelu,
                                         scale=scale).then_inc(hi_done, 1)

                def body(i, ffn, scan, mix, more):
                    c, d = i - 1, i - 2
                    started = isinstance(i, int) and i == 0
                    if ffn:
                        for m in range(KH):
                            if not narrow_w:
                                if m == 0 and not started:
                                    act.wait_ge(w3_ps, i * 2)
                                dst = t["a"][:, m, :]
                            else:
                                if m >= 4 or not started:
                                    act.wait_ge(lo_done, i * SPLITS + m - 3)
                                dst = t["whole"][:, m % 4, :]
                            act.wait_ge(w12_ps, i * KH + m + 1)
                            nc.scalar.activation(dst, bank[pair(m)][:], ACT.Tanh, scale=s1half[:, m:m + 1]
                                                 ).then_inc(th_done, 1)
                            if narrow_w and m == 2:
                                if not started:
                                    act.wait_ge(w3_ps, i * 2)
                                product_hi(i, 0)
                                product_hi(i, 1)
                            if narrow_w and m >= 3:
                                product_hi(i, m - 1)
                            if scan and m == KH - 2:
                                evacuate(wide_b, 6, c, x2T_ps, x2T_done)
                        if narrow_w:
                            product_hi(i, KH - 1)
                    elif scan:
                        evacuate(wide_b, 6, c, x2T_ps, x2T_done)

                    def silu_tanh():
                        act.wait_ge(sq_done, (d + 1) * 2 * BATCH)
                        nc.scalar.activation(tmp[:, 0:HALF, :, :].rearrange("p n i j -> p (n i j)"),
                                             t["Sq"][:].rearrange("p b d -> p (b d)"), ACT.Tanh,
                                             scale=0.5).then_inc(sq_tanh, 1)

                    def kvq_out(b):
                        lo = 4 if b % 2 == 0 else 6
                        act.wait_ge(kvq_ps, c * BATCH + b + 1)
                        if mix:
                            act.wait_ge(sq_done, (c - 1) * 2 * BATCH + 2 * b + 2)
                        nc.scalar.copy(kvq[:, b, 0:512], bank[lo][:]).then_inc(kvq_done, 1)
                        nc.scalar.copy(kvq[:, b, 512:768], bank[lo + 1][:, 0:DIM]).then_inc(kvq_done, 1)

                    def part(dst, nu):
                        for k in range(KD):
                            nc.scalar.activation(dst[:, k, :].rearrange("p (b n) -> p b n", b=BATCH),
                                                 x3T[:, k, :, 0:P], ACT.Copy, scale=nu[:, k:k + 1]).then_inc(part_done, 1)

                    def mix_parts():
                        nc.scalar.copy(x3T[:, :, :, 0], x3T[:, :, :, P]).then_inc(x3T_col, 1)
                        act.wait_ge(x3T_col, d + 1)
                        for k in range(KD):
                            act.wait_ge(x3T_ps, d * 2 + k + 1)
                            nc.scalar.copy(x3T[:, k, :, 1:P + 1], bank[4 + k][:].rearrange("p (b n) -> p b n", b=BATCH)
                                           ).then_inc(x3T_done, 1)
                        act.wait_ge(x3T_done, d * 2 + 2)
                        if not (isinstance(i, int) and i == 2):
                            act.wait_ge(dv_ps, d * 2)
                        part(wide_a, nu_k)
                        part(wide_b, nu_r)

                    if scan:
                        kvq_out(0)
                        kvq_out(1)
                    if mix:
                        silu_tanh()
                    if scan:
                        kvq_out(2)
                        kvq_out(3)
                        act.wait_ge(kvq_done, (c + 1) * 2 * BATCH)
                        if mix:
                            act.wait_ge(ln3_steps, (c - 1) * N_LN3 + 3)
                        nc.scalar.activation(tmp[:, 0:HALF, :, :].rearrange("p n i j -> p (n i j)").rearrange(
                            "p (b d) -> p b d", b=BATCH), kvq[:, :, 0:DIM], ACT.Square).then_inc(ksq_done, 1)

                    for n in range(2 * KH):
                        if ffn:
                            gelu(i, n // KH, n % KH)
                        if n == 0:
                            if mix:
                                mix_parts()
                            if scan:
                                nc.scalar.copy(t["x2res"][:], x2[:]).then_inc(x2_kept, 1)
                        if scan:
                            if n == 2:
                                scan_tanh(c, 0, 0)
                                scan_tanh(c, 0, 1)
                            if n in (5, 7, 9, 12, 14):
                                half = (5, 7, 0, 9, 12, 14).index(n)
                                scan_tanh(c, 1 + half // 2, half % 2)
                        if n == KH - 1:
                            if mix:
                                act.wait_ge(dk_ps, d * 2 + 2)
                                for k in range(KD):
                                    nc.scalar.activation(wide_a[:, k, :], bank[4 + k][:], ACT.Relu).then_inc(relu_done, 1)
                                act.wait_ge(relu_done, d * 2 + 2)
                                for k in range(KD):
                                    nc.scalar.activation(wide_a[:, k, :], wide_a[:, k, :], ACT.Square).then_inc(kact_done, 1)
                                if not (isinstance(i, int) and i == 2):
                                    act.wait_ge(out_done, (i - 2) * 16)
                                for r in range(2):
                                    act.wait_ge(dr_ps, d * 2 + r + 1)
                                    nc.scalar.activation(y4[:, 2 * r:2 * r + 2, :],
                                                         bank[6 + r][:].rearrange("p (b d) -> p b d", b=2),
                                                         ACT.Tanh, scale=0.5).then_inc(sig_done, 1)
                            if scan:
                                scan_tanh(c, 2, 0)
                        if more and n == KH + 1:
                            evacuate(t["x1hi"] if narrow_w else wide_a, 6, i + 1, x1T_ps, x1T_done)

                evacuate(t["x1hi"] if narrow_w else wide_a, 6, 0, x1T_ps, x1T_done)
                schedule(act, body)

            def gpsimd_program(pool, narrow_w):
                t = tn if narrow_w else tw

                def root(dst, src, n, expo, ready, done, c):
                    pool.wait_ge(ready, c + 1)
                    nc.gpsimd.tensor_tensor(dst, src, expo[:, 0:n], ALU.pow).then_inc(done, 1)

                def low_part(layer, m, c):
                    hi, lo = (t["b_hi"], t["b_lo"]) if layer == 1 else (t["a_hi"], t["a_lo"])
                    pool.wait_ge(hi_done, c * SPLITS + layer * KH + m + 1)
                    nc.gpsimd.tensor_tensor(lo[:, m, :], t["whole"][:, m % 4, :], hi[:, m, :].bitcast(F32),
                                            ALU.subtract).then_inc(lo_done, 1)

                def body(i, ffn, scan, mix, more):
                    if scan:
                        root(t["rstd2"][:], t["mv2"][:, :, 1], BATCH, inv_pow, ve2, rs2, i - 1)
                    if ffn and narrow_w:
                        for m in range(KH):
                            low_part(0, m, i)
                    if mix:
                        root(t["rstd3"][:], t["mv3"][:, :, 1], BATCH, inv_pow, ve3, rs3, i - 2)
                    for n in range(2 * KH):
                        if ffn and narrow_w:
                            low_part(1 + n // KH, n % KH, i)
                        if mix and n == KH + 1:
                            root(t["rstd4"][:], t["mv4"][:, :, 1], BATCH, inv_pow, ve4, rs4, i - 2)

                schedule(pool, body)

            def vector_program(dve, narrow_w):
                t = tn if narrow_w else tw
                wide_a, wide_b, S, tmp, kvq = t["wide_a"], t["wide_b"], t["S"], t["tmp"], t["kvq"]
                x3T, y4, x2, x3, Sq, delta = t["x3T"], t["y4"], t["x2"], t["x3"], t["Sq"], t["delta"]
                dve.wait_ge(ffn_in, 16 * N_FFN_IN)
                nc.vector.tensor_scalar(s1half[:], s1[:], 0.5, None, ALU.mult).then_inc(prep, 1)
                nc.vector.tensor_tensor(s12half[:], s1[:], s2[:], ALU.mult).then_inc(prep, 1)
                dve.wait_ge(prep, 2)
                nc.vector.tensor_scalar(s12half[:], s12half[:], 0.5, None, ALU.mult).then_inc(prep, 1)
                nc.vector.tensor_scalar(nu_r[:], mu_r[:], -1.0, 1.0, ALU.mult, ALU.add).then_inc(prep, 1)
                nc.vector.tensor_scalar(nu_k[:], mu_k[:], -1.0, 1.0, ALU.mult, ALU.add).then_inc(prep, 1)
                for k in range(KD):
                    for col in (0, P):
                        nc.vector.memset(x3T[:, k, :, col], 0.0).then_inc(prep, 1)
                dve.wait_ge(prep, 9)
                ln2, ln3, ln4 = (Steps(dve, ln2_steps, N_LN2), Steps(dve, ln3_steps, N_LN3),
                                 Steps(dve, ln4_steps, N_LN4))
                scan, tail = Steps(dve, scan_steps, N_SCAN), Steps(dve, tail_steps, N_TAIL)
                kb4 = kvq[:, :, 0:DIM].rearrange("p b (n j) -> p b n j", j=BS)

                def x1_low(c):
                    for k in range(KD):
                        dve.wait_ge(x1T_done, c * 2 + k + 1)
                        nc.vector.tensor_tensor(t["x1lo"][:, k, :], bank[6 + k][:], t["x1hi"][:, k, :].bitcast(F32),
                                                ALU.subtract).then_inc(x1lo_done, 1)

                def product(c, m):
                    w = t["whole"][:, m % 4, :] if narrow_w else t["a"][:, m, :]
                    dve.wait_ge(th_done, c * KH + m + 1)
                    nc.vector.scalar_tensor_tensor(out=w, in0=w, scalar=1.0, in1=bank[pair(m)][:], op0=ALU.add,
                                                   op1=ALU.mult).then_inc(prod_mid, 1)
                    dve.wait_ge(prod_mid, c * KH + m + 1)
                    nc.vector.scalar_tensor_tensor(out=w, in0=bank[pair(m) + 1][:],
                                                   scalar=s12half[:, m:m + 1], in1=w,
                                                   op0=ALU.mult, op1=ALU.mult).then_inc(prod_done, 1)

                def key_norms(c):
                    scan.begin(c)
                    x, y, z = (t[n][:].rearrange("p b n -> p (b n)") for n in ("norm", "root", "newton"))
                    dve.wait_ge(ksq_done, c + 1)
                    scan.done(nc.vector.tensor_reduce(x, tmp[:, 0:HALF, :, :].rearrange("p n i j -> p (n i) j"),
                                                      AX_X, ALU.add))
                    scan.wait()
                    scan.done(nc.vector.tensor_scalar(y.bitcast(I32), x.bitcast(I32), 1, None, ALU.arith_shift_right))
                    scan.wait()
                    scan.done(nc.vector.tensor_scalar(y.bitcast(I32), y.bitcast(I32), -1, 0x5F3759DF,
                                                      ALU.mult, ALU.add))
                    for step in range(3):
                        scan.wait()
                        if step:
                            pass
                        scan.done(nc.vector.tensor_tensor(z, y, y, ALU.mult))
                        scan.wait()
                        scan.done(nc.vector.scalar_tensor_tensor(out=z, in0=z, scalar=-0.5, in1=x,
                                                                 op0=ALU.mult, op1=ALU.mult))
                        scan.wait()
                        scan.done(nc.vector.scalar_tensor_tensor(out=y, in0=z, scalar=1.5, in1=y,
                                                                 op0=ALU.add, op1=ALU.mult))
                    scan.wait()
                    scan.done(nc.vector.tensor_tensor(x, x, y, ALU.mult))
                    scan.wait()
                    nc.vector.tensor_scalar(x, x, 1e-6, None, ALU.add).then_inc(scan.sem, 1)
                    scan.k += 1
                    scan.wait()
                    scan.done(nc.vector.reciprocal(x, x))
                    scan.wait()
                    scan.done(nc.vector.tensor_tensor(kb4, kb4, t["norm"][:].unsqueeze(3).broadcast_to(
                        [P, BATCH, NB, BS]), ALU.mult))
                    scan.wait()
                    assert scan.k == N_NORM, scan.k

                def parts(s, hf):
                    n0 = hf * HALF
                    k, v, q = (kvq[:, s, a * DIM + n0 * BS:a * DIM + (n0 + HALF) * BS].rearrange(
                        "p (n j) -> p n j", j=BS) for a in range(3))
                    return k, v, q, S[:, n0:n0 + HALF], tmp[:, n0:n0 + HALF]

                def along_j(x):
                    return x.unsqueeze(2).broadcast_to([P, HALF, BS, BS])

                def along_i(x):
                    return x.unsqueeze(3).broadcast_to([P, HALF, BS, BS])

                def first_update(c):
                    for hf in range(2):
                        k, v, q, s, _ = parts(0, hf)
                        nc.vector.tensor_tensor(s, along_i(v), along_j(k), ALU.mult).then_inc(pre_tanh, 1)

                def read_out(c, s, hf, steps):
                    k, v, q, st, w = parts(s, hf)
                    dve.wait_ge(post_tanh, c * 8 + 2 * s + hf + 1)
                    steps.done(nc.vector.tensor_tensor(w, st, along_j(q), ALU.mult))
                    steps.wait()
                    nc.vector.tensor_reduce(Sq[:, s, hf * HALF * BS:(hf + 1) * HALF * BS].rearrange(
                        "p (n i) -> p n i", i=BS), w, AX_X, ALU.add).then_inc(sq_done, 1)

                def update(c, s, hf):
                    k, v, q, st, w = parts(s, hf)
                    dl = delta[:, hf * HALF:hf * HALF + HALF, :]
                    dve.wait_ge(sq_done, c * 2 * BATCH + 2 * (s - 1) + hf + 1)
                    scan.done(nc.vector.tensor_tensor(w, st, along_j(k), ALU.mult))
                    scan.wait()
                    scan.done(nc.vector.tensor_reduce(dl, w, AX_X, ALU.add))
                    scan.wait()
                    scan.done(nc.vector.tensor_tensor(dl, v, dl, ALU.subtract))
                    scan.wait()
                    scan.done(nc.vector.tensor_tensor(w, along_i(dl), along_j(k), ALU.mult))
                    scan.wait()
                    nc.vector.tensor_tensor(st, st, w, ALU.add).then_inc(pre_tanh, 1)

                def scan_step(c, s):
                    for hf in range(2):
                        read_out(c, s, hf, scan)
                        update(c, s + 1, hf)

                def scan_out(c):
                    tail.begin(c)
                    for hf in range(2):
                        read_out(c, BATCH - 1, hf, tail)
                    tail.end()
                    ln3.begin(c)
                    dve.wait_ge(sq_tanh, c + 1)
                    dve.wait_ge(x2_kept, c + 1)
                    sqf = Sq[:].rearrange("p b d -> p (b d)")
                    thf = tmp[:, 0:HALF, :, :].rearrange("p n i j -> p (n i j)")
                    x3f = x3[:].rearrange("p b d -> p (b d)")
                    ln3.done(nc.vector.scalar_tensor_tensor(out=x3f, in0=thf, scalar=1.0, in1=sqf,
                                                            op0=ALU.add, op1=ALU.mult))
                    ln3.wait()
                    ln3.done(nc.vector.scalar_tensor_tensor(out=x3f, in0=x3f, scalar=0.5, in1=sqf,
                                                            op0=ALU.mult, op1=ALU.mult))
                    ln3.wait()
                    ln3.done(nc.vector.tensor_tensor(x3[:], x3[:], t["x2res"][:], ALU.add))
                    layernorm(dve, ln3, x3, t["mv3"], t["rstd3"], ve3, rs3, c, ln3_done)
                    ln3.end()

                def mix_inputs(d, n, dst, mu, done):
                    for k in range(KD):
                        dve.wait_ge(part_done, d * 4 + 2 * n + k + 1)
                        w = dst[:, k, :].rearrange("p (b n) -> p b n", b=BATCH)
                        nc.vector.scalar_tensor_tensor(out=w, in0=x3T[:, k, :, 1:P + 1], scalar=mu[:, k:k + 1],
                                                       in1=w, op0=ALU.mult, op1=ALU.add).then_inc(done, 1)

                def mix_result(d):
                    ln4.begin(d)
                    for n in range(2):
                        dve.wait_ge(dv_ps, d * 2 + n + 1)
                        dve.wait_ge(sig_done, d * 2 + n + 1)
                        w = y4[:, 2 * n:2 * n + 2, :]
                        nc.vector.scalar_tensor_tensor(out=w, in0=w, scalar=1.0,
                                                       in1=bank[4 + n][:].rearrange("p (b d) -> p b d", b=2),
                                                       op0=ALU.add, op1=ALU.mult).then_inc(gated4, 1)
                    dve.wait_ge(gated4, d * 2 + 2)
                    yf, xf = y4[:].rearrange("p b d -> p (b d)"), x3[:].rearrange("p b d -> p (b d)")
                    ln4.done(nc.vector.scalar_tensor_tensor(out=yf, in0=yf, scalar=0.5, in1=xf,
                                                            op0=ALU.mult, op1=ALU.add))
                    layernorm(dve, ln4, y4, t["mv4"], t["rstd4"], ve4, rs4, d, ln4_done)
                    ln4.end()

                def ffn_out(c):
                    ln2.begin(c)
                    dve.wait_ge(x1res_in, (c + 1) * 16)
                    for n in range(2):
                        dve.wait_ge(w3_ps, c * 2 + n + 1)
                        nc.vector.tensor_tensor(x2[:, 2 * n:2 * n + 2, :],
                                                bank[n][:].rearrange("p (b d) -> p b d", b=2),
                                                s3[:].unsqueeze(1).broadcast_to([P, 2, DIM]),
                                                ALU.mult).then_inc(scaled_done, 1)
                    for n in range(2):
                        dve.wait_ge(scaled_done, c * 2 + n + 1)
                        w = x2[:, 2 * n:2 * n + 2, :]
                        nc.vector.tensor_tensor(w, w, t["x1res"][:, 2 * n:2 * n + 2, :], ALU.add).then_inc(r2_done, 1)
                    dve.wait_ge(r2_done, c * 2 + 2)
                    layernorm(dve, ln2, x2, t["mv2"], t["rstd2"], ve2, rs2, c, ln2_done)
                    ln2.end()

                def body(i, ffn, has_scan, mix, more):
                    c, d = i - 1, i - 2
                    if has_scan:
                        ffn_out(c)
                    if ffn:
                        for m in range(3, KH):
                            product(i, m)
                    if mix:
                        scan_out(d)
                    if has_scan:
                        key_norms(c)
                        first_update(c)
                    if mix:
                        mix_inputs(d, 0, wide_a, mu_k, mixk_done)
                        mix_inputs(d, 1, wide_b, mu_r, mixr_done)
                    if has_scan:
                        scan_step(c, 0)
                        scan_step(c, 1)
                    if mix:
                        mix_result(d)
                    if more and narrow_w:
                        x1_low(i + 1)
                    if has_scan:
                        scan_step(c, 2)
                        scan.end()
                    if more:
                        for m in range(3):
                            product(i + 1, m)

                if narrow_w:
                    x1_low(0)
                for m in range(3):
                    product(0, m)
                schedule(dve, body)

            block = ctx.enter_context(nc.Block())

            @block.sync
            def _(sp):
                flag = sp.value_load(wide_flag[0:1, 0:1], min_val=0, max_val=1)
                with sp.If(flag > 0):
                    sync_program(sp, False)
                with sp.Else():
                    sync_program(sp, True)

            @block.tensor
            def _(pe):
                flag = pe.value_load(wide_flag[0:1, 0:1], min_val=0, max_val=1)
                with pe.If(flag > 0):
                    tensor_program(pe, False)
                with pe.Else():
                    tensor_program(pe, True)

            @block.scalar
            def _(act):
                flag = act.value_load(wide_flag[0:1, 0:1], min_val=0, max_val=1)
                with act.If(flag > 0):
                    scalar_program(act, False)
                with act.Else():
                    scalar_program(act, True)

            @block.gpsimd
            def _(pool):
                flag = pool.value_load(wide_flag[0:1, 0:1], min_val=0, max_val=1)
                with pool.If(flag > 0):
                    gpsimd_program(pool, False)
                with pool.Else():
                    gpsimd_program(pool, True)

            @block.vector
            def _(dve):
                flag = dve.value_load(wide_flag[0:1, 0:1], min_val=0, max_val=1)
                with dve.If(flag > 0):
                    vector_program(dve, False)
                with dve.Else():
                    vector_program(dve, True)


def tables():
    import numpy as np

    pos = np.arange(LENGTH, dtype=np.float64)
    half = HEAD // 2
    base = (np.arange(0, HEAD, 2) + 0.4 * HEAD) / (1.4 * HEAD)
    scale = base[None, :] ** (pos[:, None] / 512.0)
    freq = 1.0 / 10000.0 ** (np.arange(half) / half)
    angle = (pos[:, None].astype(np.float32) * freq[None, :].astype(np.float32)).astype(np.float64)
    sign = np.tile([-1.0, 1.0], half)
    gammas = 1.0 - np.exp(np.linspace(np.log(1.0 / 32.0), np.log(1.0 / 512.0), HEADS))
    local = (np.arange(LENGTH) % P).astype(np.float64)
    rope = np.empty((LENGTH, 2, 2, HEADS, HEAD))
    for n, (s, power) in enumerate(((scale, local), (1.0 / scale, -local))):
        decay = gammas[None, :] ** power[:, None]
        for m, trig in enumerate((np.cos(angle), np.sin(angle))):
            row = np.repeat(trig * s, 2, axis=1) * (sign if m else 1.0)
            rope[:, m, n] = decay[:, :, None] * row[:, None, :]
    rope = rope.reshape(CHUNKS, P, 2, 2 * DIM)
    causal = np.triu(np.ones((P, P)))
    across = np.zeros((P, GROUPS, P))
    for g in range(GROUPS):
        for j in range(PER_GROUP):
            r = slice(j * HEAD, (j + 1) * HEAD)
            across[r, g, r] = gammas[g * PER_GROUP + j] ** P
    return {n: np.ascontiguousarray(a, dtype=np.float32) for n, a in
            dict(rope=rope, causal=causal, ident=np.eye(P), decay=across).items()}


def kernel(**inputs):
    import numpy as np
    import concourse.bacc as bacc
    from concourse.bass_utils import run_bass_kernel_spmd as run

    a = {n: np.asarray(x) for n, x in inputs.items()}

    def tiles(w):
        return w.reshape(-1, P, w.shape[1]).transpose(1, 0, 2)

    def columns(w):
        return w.reshape(-1, P).T

    def by_output_tile(w):
        return w.reshape(KH, P, KH, P).transpose(1, 2, 0, 3).reshape(P, -1)

    X = a["L0_attn_X"]
    heads = [a[f"L0_attn_W_{n}"].transpose(1, 0, 2).reshape(DIM, DIM) for n in "QKV"]
    arrays = tables()
    arrays.update(
        xT=X.transpose(2, 0, 1).reshape(KD, P, BATCH, LENGTH).transpose(1, 0, 2, 3),
        x=X.reshape(BATCH, CHUNKS, P, DIM),
        wa=tiles(np.concatenate([*heads, a["L0_attn_W_G"]], axis=1)),
        wo=tiles(a["L0_attn_W_O"]),
        gnw=a["L0_attn_gn_weight"][None, :], gnb=a["L0_attn_gn_bias"][None, :],
        ffn=np.concatenate([
            tiles(a["L0_ffn_w1_w"].T).reshape(P, -1), tiles(a["L0_ffn_w2_w"].T).reshape(P, -1),
            by_output_tile(a["L0_ffn_h1_w"].T), by_output_tile(a["L0_ffn_h2_w"].T),
            tiles(a["L0_ffn_w3_w"].T).reshape(P, -1)], axis=1),
        s1=columns(a["L0_ffn_w1_s"]), s2=columns(a["L0_ffn_w2_s"]),
        hs1=columns(a["L0_ffn_h1_s"]), hs2=columns(a["L0_ffn_h2_s"]), s3=a["L0_ffn_w3_s"][None, :],
        wkvq=tiles(np.concatenate([a["L1_attn_W_k"].T, a["L1_attn_W_v"].T, a["L1_attn_W_q"].T], axis=1)),
        wr=tiles(a["L1_ffn_W_r"].T), wk=tiles(a["L1_ffn_W_k"].T), wv=tiles(a["L1_ffn_W_v"].T),
        mur=columns(a["L1_ffn_mu_r"]), muk=columns(a["L1_ffn_mu_k"]),
    )
    arrays = {n: np.ascontiguousarray(x) for n, x in arrays.items()}
    nc = bacc.Bacc("TRN2", target_bir_lowering=False, num_devices=1)
    t = {n: nc.dram_tensor(f"{n}_dram", x.shape, mybir.dt.from_np(x.dtype), kind="ExternalInput").ap()
         for n, x in arrays.items()}
    t_out = nc.dram_tensor("out_dram", (BATCH, LENGTH, DIM), F32, kind="ExternalOutput").ap()
    t_x1 = nc.dram_tensor("x1_dram", (CHUNKS, P, BATCH, DIM), F32, kind="Internal").ap()
    t_ffn = nc.dram_tensor("ffn_copy_dram", (P, FFN_COLS), F32, kind="Internal").ap()
    build(nc, t["xT"], t["x"], t["rope"], t["causal"], t["ident"], t["decay"], t["wa"], t["wo"],
          t["gnw"], t["gnb"], t["ffn"], t["s1"], t["s2"],
          t["hs1"], t["hs2"], t["s3"], t["wkvq"], t["wr"], t["wk"], t["wv"], t["mur"], t["muk"],
          t_out, t_x1, t_ffn)
    r = run(nc, [{f"{n}_dram": x for n, x in arrays.items()}], core_ids=[0])
    return r.results[0]["out_dram"]
```

```python
from contextlib import ExitStack

import concourse.bass as bass
from concourse import mybir

F32 = mybir.dt.float32
F32R = mybir.dt.float32r
I32 = mybir.dt.int32
ALU = mybir.AluOpType
ACT = mybir.ActivationFunctionType
AX_X = mybir.AxisListType.X

P = 128
BATCH, LENGTH, DIM = 4, 1024, 256
HEADS, HEAD = 8, 32
GROUPS, PER_GROUP = 2, 4
CHUNKS = LENGTH // P
KD = DIM // P
HID = 1024
KH = HID // P
NB, BS = 32, 8
HALF = NB // 2
TOK = BATCH * P
EPS = 1e-5
COL_W1, COL_W2 = 0, KD * HID
COL_W3 = 2 * KD * HID
COL_H1 = COL_W3 + KH * DIM
COL_H2 = COL_H1 + KH * HID
FFN_COLS = COL_H2 + KH * HID
RING = 4
PIECE = FFN_COLS // CHUNKS
PAIRS = (6, 4, 2, 6, 4, 0, 2, 4)
KVQ_BANKS = (0, 6, 4, 6)


class Steps:

    def __init__(self, eng, sem, per_chunk):
        self.eng, self.sem, self.per_chunk = eng, sem, per_chunk

    def begin(self, c):
        self.c, self.k = c, 0

    def done(self, ins):
        ins.then_inc(self.sem, 1)
        self.k += 1

    def wait(self):
        self.eng.wait_ge(self.sem, self.c * self.per_chunk + self.k)

    def end(self):
        assert self.k == self.per_chunk, (self.k, self.per_chunk)


def build(nc, xT_d, x_d, rope_d, causal_d, ident_d, decay_d, wa_d, wo_d, gnw_d, gnb_d,
          ffn_d, s1_d, s2_d, hs1_d, hs2_d, s3_d, wkvq_d,
          wr_d, wk_d, wv_d, mur_d, muk_d, out_d, x1_d, ffn_s):
    top = ExitStack()

    def sb(ctx, name, shape, dtype=F32):
        return ctx.enter_context(nc.sbuf_tensor(name, shape, dtype))

    def sem(ctx, name):
        return ctx.enter_context(nc.semaphore(name))

    with top:
        bank = [top.enter_context(nc.psum_tensor(f"bank{n}", [P, 512], F32)) for n in range(8)]

        ident = sb(top, "ident", [P, P])
        inv_pow = sb(top, "inv_pow", [P, BATCH])
        wkvq = sb(top, "wkvq", [P, KD, 3 * DIM])
        wr = sb(top, "wr", [P, KD, DIM])
        wk = sb(top, "wk", [P, KD, DIM])
        wv = sb(top, "wv", [P, KD, DIM])
        s1 = sb(top, "s1", [P, KH])
        s2 = sb(top, "s2", [P, KH])
        hs1 = sb(top, "hs1", [P, KH])
        hs2 = sb(top, "hs2", [P, KH])
        s1half = sb(top, "s1half", [P, KH])
        s12half = sb(top, "s12half", [P, KH])
        s3 = sb(top, "s3", [P, DIM])
        mu_r = sb(top, "mu_r", [P, KD])
        mu_k = sb(top, "mu_k", [P, KD])
        nu_r = sb(top, "nu_r", [P, KD])
        nu_k = sb(top, "nu_k", [P, KD])
        stats = sb(top, "stats", [P, BATCH, 6])
        spread = sb(top, "spread", [P, BATCH])
        low_sum = sb(top, "low_sum", [P, CHUNKS])
        low_all = sb(top, "low_all", [P, 1])
        low_max = sb(top, "low_max", [P, 1])
        wide_flag = sb(top, "wide_flag", [P, 1], I32)
        x1in = sb(top, "x1in", [P, BATCH, DIM])
        x1res = sb(top, "x1res", [P, BATCH, DIM])
        y4 = sb(top, "y4", [P, BATCH, DIM])
        x1_out = [sem(top, f"x1_out{n}") for n in range(2)]
        x1in_in = sem(top, "x1in_in")
        x1res_in = sem(top, "x1res_in")
        ffn_in = sem(top, "ffn_in")
        w123_in = sem(top, "w123_in")
        pow_ready = sem(top, "pow_ready")

        def row_stats(steps, r, rows):
            for b in rows:
                ins = nc.vector.bn_stats(out=stats[:, b, :], in_=r[:, b, :])
            steps.done(ins)

        def layernorm(dve, steps, r, mv, rstd, ve_ready, rstd_ready, c, done_sem, meanwhile=None,
                      have_stats=False):
            if not have_stats:
                steps.wait()
                row_stats(steps, r, range(BATCH))
            steps.wait()
            nc.vector.tensor_tensor(mv[:, :, 0], stats[:, :, 1], stats[:, :, 4], ALU.add)
            nc.vector.tensor_tensor(spread[:], stats[:, :, 1], stats[:, :, 4], ALU.subtract)
            steps.done(nc.vector.tensor_tensor(mv[:, :, 1], stats[:, :, 2], stats[:, :, 5], ALU.add))
            steps.wait()
            nc.vector.tensor_scalar(mv[:, :, 0], mv[:, :, 0], 0.5, None, ALU.mult)
            nc.vector.tensor_tensor(spread[:], spread[:], spread[:], ALU.mult)
            steps.done(nc.vector.tensor_scalar(mv[:, :, 1], mv[:, :, 1], 1.0 / DIM, EPS, ALU.mult, ALU.add))
            steps.wait()
            nc.vector.scalar_tensor_tensor(out=mv[:, :, 1], in0=spread[:], scalar=0.25, in1=mv[:, :, 1],
                                           op0=ALU.mult, op1=ALU.add).then_inc(ve_ready, 1)
            if meanwhile is not None:
                meanwhile()
            dve.wait_ge(rstd_ready, c + 1)
            for b in range(BATCH):
                ins = nc.vector.tensor_scalar(r[:, b, :], r[:, b, :], mv[:, b, 0:1], rstd[:, b:b + 1],
                                              ALU.subtract, ALU.mult)
            ins.then_inc(done_sem, 1)

        def inverse_root(steps, x, y, z):
            steps.wait()
            steps.done(nc.vector.tensor_scalar(y.bitcast(I32), x.bitcast(I32), 1, None, ALU.arith_shift_right))
            steps.wait()
            steps.done(nc.vector.tensor_scalar(y.bitcast(I32), y.bitcast(I32), -1, 0x5F3759DF, ALU.mult, ALU.add))
            for _ in range(3):
                steps.wait()
                steps.done(nc.vector.tensor_tensor(z, y, y, ALU.mult))
                steps.wait()
                steps.done(nc.vector.scalar_tensor_tensor(out=z, in0=z, scalar=-0.5, in1=x,
                                                          op0=ALU.mult, op1=ALU.mult))
                steps.wait()
                steps.done(nc.vector.scalar_tensor_tensor(out=y, in0=z, scalar=1.5, in1=y,
                                                          op0=ALU.add, op1=ALU.mult))

        narrow = ExitStack()
        w1r = sb(narrow, "w1r", [P, KD, HID], F32R)
        w2r = sb(narrow, "w2r", [P, KD, HID], F32R)
        w3r = sb(narrow, "w3r", [P, KH, DIM], F32R)

        with ExitStack() as ctx:
            xT = sb(ctx, "xT", [P, 2, KD, BATCH, P])
            xtok = sb(ctx, "xtok", [P, 2, BATCH, DIM])
            rope = sb(ctx, "rope", [P, 2, 2, 2 * DIM])
            causal = sb(ctx, "causal", [P, P])
            decay = sb(ctx, "decay", [P, GROUPS, P])
            wa = sb(ctx, "wa", [P, KD, 4 * DIM])
            wo = sb(ctx, "wo", [P, KD, DIM])
            gnw = sb(ctx, "gnw", [P, DIM])
            gnb = sb(ctx, "gnb", [P, DIM])
            qk = sb(ctx, "qk", [P, 2, BATCH, 2 * DIM])
            turned = sb(ctx, "turned", [P, 2 * DIM])
            qkT = sb(ctx, "qkT", [P, 2, BATCH, 4, P])
            v = sb(ctx, "v", [P, 2, BATCH, DIM])
            gate = sb(ctx, "gate", [P, 2, BATCH, DIM])
            gate_b = sb(ctx, "gate_b", [P, BATCH, DIM])
            probs = sb(ctx, "probs", [P, 2, PER_GROUP, 2, GROUPS, P])
            state = sb(ctx, "state", [P, BATCH, GROUPS, P])
            update = sb(ctx, "update", [P, 2, GROUPS, P])
            mean = sb(ctx, "mean", [P, BATCH, HEADS])
            var = sb(ctx, "var", [P, BATCH, HEADS])
            rgn = sb(ctx, "rgn", [P, BATCH, HEADS])
            newton1 = sb(ctx, "newton1", [P, BATCH, HEADS])
            y = sb(ctx, "y", [P, BATCH, DIM])
            ysq = sb(ctx, "ysq", [P, BATCH, DIM])
            zT = sb(ctx, "zT", [P, KD, TOK])
            r1 = (sb(ctx, "r1", [P, BATCH, DIM]), y4)
            look = sb(ctx, "look", [P, PIECE])
            mv1 = sb(ctx, "mv1", [P, BATCH, 2])
            rstd1 = sb(ctx, "rstd1", [P, BATCH])

            const_in = sem(ctx, "const_in")
            wa_in = [sem(ctx, f"wa_in{n}") for n in range(2)]
            xT_in = [sem(ctx, f"xT_in{n}") for n in range(2)]
            xtok_in = [sem(ctx, f"xtok_in{n}") for n in range(2)]
            rope_in = [sem(ctx, f"rope_in{n}") for n in range(2)]
            proj_done = sem(ctx, "proj_done")
            v_done = sem(ctx, "v_done")
            tanh_done = sem(ctx, "tanh_done")
            gate_done = sem(ctx, "gate_done")
            gn_halved = sem(ctx, "gn_halved")
            gw_done = sem(ctx, "gw_done")
            rope_done = sem(ctx, "rope_done")
            turn_done = sem(ctx, "turn_done")
            t_done = sem(ctx, "t_done")
            qkT_done = sem(ctx, "qkT_done")
            scores_done = sem(ctx, "scores_done")
            probs_done = sem(ctx, "probs_done")
            y_done = sem(ctx, "y_done")
            mean_done = sem(ctx, "mean_done")
            centre_done = sem(ctx, "centre_done")
            update_out = sem(ctx, "update_out")
            sum_done = sem(ctx, "sum_done")
            state_done = sem(ctx, "state_done")
            ysq_done = sem(ctx, "ysq_done")
            z_done = sem(ctx, "z_done")
            zt_ps = sem(ctx, "zt_ps")
            zT_done = sem(ctx, "zT_done")
            wo_ps = sem(ctx, "wo_ps")
            r1_done = sem(ctx, "r1_done")
            ve1 = sem(ctx, "ve1")
            rs1 = sem(ctx, "rs1")
            ln1_done = sem(ctx, "ln1_done")
            gn_steps = [sem(ctx, f"gn_steps{n}") for n in range(2)]
            ln1_steps = sem(ctx, "ln1_steps")
            copy_in = sem(ctx, "copy_in")
            look_in = sem(ctx, "look_in")
            low_bits = sem(ctx, "low_bits")
            low_added = sem(ctx, "low_added")
            low_done = sem(ctx, "low_done")
            low_reduced = sem(ctx, "low_reduced")
            flag_done = sem(ctx, "flag_done")
            N_GN, N_LN1 = 15, 3
            N_CONST = 6

            def loaded(c, parity):
                return (c - parity) * 8 + 16

            def banks_of(n, b):
                return bank[2 * b:2 * b + 2] if isinstance(n, int) and n == 0 else bank[0:2]

            def schedule1(eng, body):
                body(0, 0, False, True, True, True)
                body(1, 1, True, True, True, True)
                with eng.Fori(2, CHUNKS - 3, 2) as c:
                    body(c, 0, True, True, True, True)
                    body(c + 1, 1, True, True, True, True)
                body(CHUNKS - 2, 0, True, True, True, False)
                body(CHUNKS - 1, 1, True, True, False, False)
                body(CHUNKS, 0, True, False, False, False)

            block = ctx.enter_context(nc.Block())

            @block.sync
            def _(sp):
                x_view = x_d.rearrange("b c p d -> p c b d")

                def xT_load(c, parity):
                    sp.dma_start(xT[:, parity], xT_d[:, :, :, bass.ts(c, P)]).then_inc(xT_in[parity], 16)

                def rope_load(c, parity):
                    sp.dma_start(rope[:, parity], rope_d[bass.ds(c, 1)].rearrange("o p a d -> (o p) a d")
                                 ).then_inc(rope_in[parity], 16)

                def xtok_load(c, parity):
                    sp.dma_start(xtok[:, parity], x_view[:, bass.ds(c, 1)].rearrange("p o b d -> p (o b) d")
                                 ).then_inc(xtok_in[parity], 16)

                xT_load(0, 0)
                for n in range(2):
                    sp.dma_start(wa[:, :, n * 512:n * 512 + 512], wa_d[:, :, n * 512:n * 512 + 512]
                                 ).then_inc(wa_in[n], 16)
                rope_load(0, 0)
                sp.dma_start(ident[:], ident_d).then_inc(const_in, 16)
                sp.dma_start(causal[:], causal_d).then_inc(const_in, 16)
                xT_load(1, 1)
                rope_load(1, 1)
                sp.dma_start(decay[:], decay_d).then_inc(const_in, 16)
                sp.dma_start(gnw[:], gnw_d.broadcast_to([P, DIM])).then_inc(const_in, 16)
                sp.dma_start(gnb[:], gnb_d.broadcast_to([P, DIM])).then_inc(const_in, 16)
                sp.dma_start(wo[:], wo_d).then_inc(const_in, 16)
                xtok_load(0, 0)
                xtok_load(1, 1)

                def store(c, parity):
                    sp.wait_ge(ln1_done, c + 1)
                    sp.dma_start(x1_d[bass.ds(c, 1)].rearrange("o p b d -> (o p) b d"), r1[parity][:]
                                 ).then_inc(x1_out[parity], 16)

                def copy_piece(c):
                    cols = bass.ds(c * PIECE, PIECE)
                    sp.dma_start(ffn_s[:, cols], ffn_d[:, cols]).then_inc(copy_in, 16)

                def body(c, parity, more_x):
                    if more_x:
                        sp.wait_ge(proj_done, (c + 1) * BATCH)
                        xT_load(c + 2, parity)
                        sp.wait_ge(rope_done, (c + 1) * BATCH)
                        rope_load(c + 2, parity)
                    if not (isinstance(c, int) and c < 2):
                        store(c - 2, parity)
                    if not (isinstance(c, int) and c == 0):
                        sp.wait_ge(r1_done, c * 2)
                        xtok_load(c + 1, 1 - parity)
                    copy_piece(c)

                body(0, 0, True)
                body(1, 1, True)
                with sp.Fori(2, CHUNKS - 3, 2) as c:
                    body(c, 0, True)
                    body(c + 1, 1, True)
                sp.wait_ge(copy_in, (CHUNKS - 2) * 16)
                for dst, col in ((w1r, COL_W1), (w2r, COL_W2), (w3r, COL_W3)):
                    n = dst.shape[1] * dst.shape[2]
                    sp.dma_start(dst[:].bitcast(F32).rearrange("p k n -> p (k n)"),
                                 ffn_s[:, col:col + n]).then_inc(w123_in, 16)
                for dst, src in ((wkvq, wkvq_d), (wr, wr_d), (wk, wk_d), (wv, wv_d), (s1, s1_d),
                                 (s2, s2_d), (hs1, hs1_d), (hs2, hs2_d), (mu_r, mur_d), (mu_k, muk_d)):
                    sp.dma_start(dst[:], src).then_inc(ffn_in, 16)
                sp.dma_start(s3[:], s3_d.broadcast_to([P, DIM])).then_inc(ffn_in, 16)
                body(CHUNKS - 2, 0, False)
                copy_piece(CHUNKS - 1)
                sp.wait_ge(x1_out[0], 16 * (CHUNKS - 2) // 2)
                sp.dma_start(x1in[:], x1_d[0]).then_inc(x1in_in, 16)
                sp.dma_start(x1res[:], x1_d[0]).then_inc(x1res_in, 16)
                for c in range(CHUNKS - 3, CHUNKS):
                    store(c, c % 2)
                sp.wait_ge(copy_in, 16 * CHUNKS)
                sp.wait_ge(x1_out[0], 16 * (CHUNKS // 2))

            @block.tensor
            def _(pe):
                def project(n, parity, b):
                    if b == 0:
                        pe.wait_ge(xT_in[parity], loaded(n, parity))
                    if not (isinstance(n, int) and n == 0):
                        pe.wait_ge(rope_done, n * BATCH + b)
                        pe.wait_ge(v_done, n * BATCH + b)
                        pe.wait_ge(gate_done, n * BATCH + b)
                    for half in range(2):
                        if isinstance(n, int) and n == 0 and b == 0:
                            pe.wait_ge(wa_in[half], 16)
                        for k in range(KD):
                            ins = nc.tensor.matmul(banks_of(n, b)[half][:], xT[:, parity, k, b, :],
                                                   wa[:, k, half * 512:half * 512 + 512],
                                                   start=(k == 0), stop=(k == KD - 1))
                    ins.then_inc(proj_done, 1)

                def turn(n, parity, b):
                    pe.wait_ge(rope_done, n * BATCH + b + 1)
                    if not (isinstance(n, int) and n == 0):
                        pe.wait_ge(probs_done, n * 8)
                    elif b == 0:
                        pe.wait_ge(v_done, BATCH)
                        pe.wait_ge(gate_done, BATCH)
                        pe.wait_ge(rope_done, BATCH)
                    for t in range(4):
                        ins = nc.tensor.transpose(bank[4 + b][:, t * P:t * P + P],
                                                  qk[:, parity, b, t * P:t * P + P], ident[:])
                    ins.then_inc(t_done, 1)

                def scores(c, parity, r):
                    if r == 0:
                        pe.wait_ge(qkT_done, c * BATCH + BATCH)
                    else:
                        pe.wait_ge(probs_done, c * 8 + 4)
                    for b2 in range(2):
                        for g in range(GROUPS):
                            for j in range(PER_GROUP):
                                rows = slice(HEAD * j, HEAD * j + HEAD)
                                col = (b2 * GROUPS + g) * P
                                ins = nc.tensor.matmul(bank[4 + j][:, col:col + P],
                                                       qkT[rows, parity, 2 * r + b2, 2 + g, :],
                                                       qkT[rows, parity, 2 * r + b2, g, :], start=True, stop=True)
                    ins.then_inc(scores_done, 1)

                def outputs(c, parity, b, follow):
                    pe.wait_ge(v_done, c * BATCH + b + 1)
                    pe.wait_ge(state_done, c * BATCH + b + 1)
                    if follow:
                        if b < 2:
                            pe.wait_ge(zT_done, (c - 1) * 2 + b + 1)
                        else:
                            pe.wait_ge(r1_done, (c - 1) * 2 + b - 1)
                    elif b >= 2:
                        pe.wait_ge(centre_done, c * BATCH + b - 1)
                        pe.wait_ge(update_out, c * BATCH + b - 1)
                    pb = bank[2 + b % 2]
                    for g in range(GROUPS):
                        nc.tensor.matmul(pb[:, DIM + g * P:DIM + g * P + P],
                                               qk[:, parity, b, DIM + g * P:DIM + g * P + P],
                                               v[:, parity, b, g * P:g * P + P], start=True, stop=True)
                    for g in range(GROUPS):
                        nc.tensor.matmul(pb[:, g * P:g * P + P], qkT[:, parity, b, g, :], state[:, b, g, :],
                                         start=True, stop=False, skip_group_check=True)
                        for j in range(PER_GROUP):
                            h = g * PER_GROUP + j
                            if g == 0 and b % 2 == 0:
                                pe.wait_ge(probs_done, c * 8 + 4 * (b // 2) + j + 1)
                            ins = nc.tensor.matmul(pb[:, h * HEAD:h * HEAD + HEAD], probs[:, b // 2, j, b % 2, g, :],
                                             v[:, parity, b, h * HEAD:h * HEAD + HEAD], start=False,
                                             stop=(j == PER_GROUP - 1), skip_group_check=True)
                    ins.then_inc(y_done, 1)

                def turn_z(c):
                    pe.wait_ge(z_done, c * 2 + 2)
                    pe.wait_ge(update_out, (c + 1) * BATCH)
                    for k in range(KD):
                        for b in range(BATCH):
                            ins = nc.tensor.transpose(bank[2 + k][:, b * P:b * P + P],
                                                      y[:, b, k * P:k * P + P], ident[:])
                        ins.then_inc(zt_ps, 1)

                def out_product(c, attend):
                    pe.wait_ge(zT_done, c * 2 + 2)
                    if attend:
                        pe.wait_ge(centre_done, (c + 1) * BATCH + 2)
                        pe.wait_ge(update_out, (c + 1) * BATCH + 2)
                    for b in range(BATCH):
                        for k in range(KD):
                            ins = nc.tensor.matmul(bank[2 + b // 2][:, (b % 2) * DIM:(b % 2) * DIM + DIM],
                                                   zT[:, k, b * P:b * P + P], wo[:, k, :],
                                                   start=(k == 0), stop=(k == KD - 1))
                        if b % 2:
                            ins.then_inc(wo_ps, 1)

                def body(c, parity, follow, attend, more, more2):
                    n, other = c + 1, 1 - parity
                    if attend:
                        scores(c, parity, 0)
                    if more:
                        project(n, other, 1)
                    if follow:
                        turn_z(c - 1)
                    if attend:
                        outputs(c, parity, 0, follow)
                    if more:
                        project(n, other, 2)
                    if attend:
                        outputs(c, parity, 1, follow)
                        scores(c, parity, 1)
                    if follow:
                        out_product(c - 1, attend)
                    if more:
                        project(n, other, 3)
                    if attend:
                        outputs(c, parity, 2, follow)
                    if more:
                        for b in range(BATCH):
                            turn(n, other, b)
                    if more2:
                        project(c + 2, parity, 0)
                    if attend:
                        outputs(c, parity, 3, follow)

                for b in range(BATCH):
                    project(0, 0, b)
                project(1, 1, 0)
                pe.wait_ge(const_in, 16 * N_CONST)
                for b in range(BATCH):
                    turn(0, 0, b)
                schedule1(pe, body)

            @block.scalar
            def _(act):
                def value_gate(n, parity, b):
                    act.wait_ge(proj_done, n * BATCH + b + 1)
                    pb = banks_of(n, b)[1]
                    nc.scalar.copy(v[:, parity, b, :], pb[:, 0:DIM]).then_inc(v_done, 1)
                    if b % 2 == 0 and not (isinstance(n, int) and n < 2):
                        act.wait_ge(z_done, (n - 2) * 2 + b // 2 + 1)
                    nc.scalar.activation(gate[:, parity, b, :], pb[:, DIM:2 * DIM], ACT.Tanh,
                                         scale=0.5).then_inc(tanh_done, 1)

                def update_copy(c, b):
                    act.wait_ge(centre_done, c * BATCH + b + 1)
                    if not (isinstance(c, int) and c == 0 and b < 2):
                        act.wait_ge(sum_done, c * BATCH + b - 1)
                    nc.scalar.copy(update[:, b % 2, :, :].rearrange("p g e -> p (g e)"),
                                   bank[2 + b % 2][:, DIM:2 * DIM]).then_inc(update_out, 1)

                def square(c, b):
                    update_copy(c, b)
                    nc.scalar.activation(ysq[:, b, :], y[:, b, :], ACT.Square).then_inc(ysq_done, 1)

                def z_out(c):
                    for k in range(KD):
                        act.wait_ge(zt_ps, c * 2 + k + 1)
                        nc.scalar.copy(zT[:, k, :], bank[2 + k][:]).then_inc(zT_done, 1)

                def turned_out(n, parity, b):
                    act.wait_ge(t_done, n * BATCH + b + 1)
                    nc.scalar.copy(qkT[:, parity, b, :, :], bank[4 + b][:].rearrange("p (t n) -> p t n", t=4)
                                   ).then_inc(qkT_done, 1)

                def look_load(c):
                    act.dma_start(look[:], ffn_d[:, bass.ds(c * PIECE, PIECE)]).then_inc(look_in, 16)

                def add_low_bits(c):
                    act.wait_ge(low_bits, c + 1)
                    nc.scalar.activation(look[:], look[:].bitcast(I32), ACT.Copy,
                                         accum_out=low_sum[:, bass.ds(c, 1)]).then_inc(low_added, 1)

                def body(c, parity, follow, attend, more, more2):
                    n, other = c + 1, 1 - parity
                    if more:
                        value_gate(n, other, 1)
                    if follow:
                        z_out(c - 1)
                    if attend:
                        square(c, 0)
                    if more:
                        value_gate(n, other, 2)
                    if attend:
                        square(c, 1)
                    if more:
                        value_gate(n, other, 3)
                        for b in range(BATCH):
                            turned_out(n, other, b)
                    if attend:
                        square(c, 2)
                    if more2:
                        value_gate(c + 2, parity, 0)
                    if attend:
                        square(c, 3)
                        add_low_bits(c)
                        if more:
                            act.wait_ge(low_added, c + 1)
                            look_load(c + 1)

                for b in range(BATCH):
                    value_gate(0, 0, b)
                look_load(0)
                value_gate(1, 1, 0)
                for b in range(BATCH):
                    turned_out(0, 0, b)
                schedule1(act, body)

            @block.gpsimd
            def _(pool):
                nc.gpsimd.memset(inv_pow[:], -0.5).then_inc(pow_ready, 1)
                for b in range(BATCH):
                    nc.gpsimd.memset(state[:, b, :, :], 0.0).then_inc(state_done, 1)
                pool.wait_ge(pow_ready, 1)
                pool.wait_ge(state_done, BATCH)
                pool.wait_ge(const_in, 16 * N_CONST)
                pool.wait_ge(gn_halved, 2)

                def gate_norm(c, parity, h):
                    rows = slice(2 * h, 2 * h + 2)
                    pool.wait_ge(gate_done, c * BATCH + 2 * h + 2)
                    if not (isinstance(c, int) and c == 0):
                        pool.wait_ge(z_done, (c - 1) * 2 + h + 1)
                    nc.gpsimd.tensor_tensor(gate_b[:, rows], gate[:, parity, rows],
                                            gnb[:].unsqueeze(1).broadcast_to([P, 2, DIM]), ALU.mult).then_inc(gw_done, 1)
                    pool.wait_ge(gw_done, c * 4 + 2 * h + 1)
                    nc.gpsimd.tensor_tensor(gate[:, parity, rows], gate[:, parity, rows],
                                            gnw[:].unsqueeze(1).broadcast_to([P, 2, DIM]),
                                            ALU.mult).then_inc(gw_done, 1)

                def move_state(c, b):
                    pool.wait_ge(update_out, c * BATCH + b + 1)
                    st = state[:, b, :, :].rearrange("p g e -> p (g e)")
                    nc.gpsimd.tensor_tensor(st, st, update[:, b % 2, :, :].rearrange("p g e -> p (g e)"),
                                            ALU.add).then_inc(sum_done, 1)
                    pool.wait_ge(sum_done, c * BATCH + b + 1)
                    nc.gpsimd.tensor_tensor(st, st, decay[:].rearrange("p g e -> p (g e)"),
                                            ALU.mult).then_inc(state_done, 1)

                def root(c):
                    pool.wait_ge(ve1, c + 1)
                    nc.gpsimd.tensor_tensor(rstd1[:], mv1[:, :, 1], inv_pow[:, 0:BATCH], ALU.pow).then_inc(rs1, 1)

                def body(c, parity, follow, attend, more, more2):
                    if attend:
                        gate_norm(c, parity, 0)
                    if not attend:
                        pool.wait_ge(low_done, 1)
                        nc.gpsimd.partition_all_reduce(low_max[:], low_all[:], P, bass.bass_isa.ReduceOp.max
                                                       ).then_inc(low_reduced, 1)
                    if follow and not (isinstance(c, int) and c == 1):
                        root(c - 2)
                    if attend:
                        move_state(c, 0)
                        move_state(c, 1)
                        gate_norm(c, parity, 1)
                    else:
                        root(c - 1)
                    if attend:
                        move_state(c, 2)
                        move_state(c, 3)

                schedule1(pool, body)

            @block.vector
            def _(dve):
                norms = [Steps(dve, gn_steps[h], N_GN) for h in range(2)]
                ln1 = Steps(dve, ln1_steps, N_LN1)

                def rotate(n, parity, b):
                    if b == 0:
                        dve.wait_ge(rope_in[parity], loaded(n, parity))
                    dve.wait_ge(proj_done, n * BATCH + b + 1)
                    pb = banks_of(n, b)
                    raw = pb[0][:].rearrange("p (e two) -> p e two", two=2)
                    sin = rope[:, parity, 1, :].rearrange("p (e two) -> p e two", two=2)
                    tur = turned[:].rearrange("p (e two) -> p e two", two=2)
                    q = qk[:, parity, b, :]
                    nc.vector.tensor_tensor(q, pb[0][:], rope[:, parity, 0, :], ALU.mult)
                    if not (isinstance(n, int) and n == 0 and b == 0):
                        dve.wait_ge(rope_done, n * BATCH + b)
                    nc.vector.tensor_tensor(tur[:, :, 0], raw[:, :, 1], sin[:, :, 0], ALU.mult)
                    nc.vector.tensor_tensor(tur[:, :, 1], raw[:, :, 0], sin[:, :, 1], ALU.mult).then_inc(turn_done, 1)
                    dve.wait_ge(turn_done, n * BATCH + b + 1)
                    nc.vector.tensor_tensor(q, q, turned[:], ALU.add).then_inc(rope_done, 1)
                    dve.wait_ge(tanh_done, n * BATCH + b + 1)
                    nc.vector.scalar_tensor_tensor(out=gate[:, parity, b, :], in0=gate[:, parity, b, :], scalar=1.0,
                                                   in1=pb[1][:, DIM:2 * DIM], op0=ALU.add,
                                                   op1=ALU.mult).then_inc(gate_done, 1)

                def masked(c, r):
                    dve.wait_ge(scores_done, c * 2 + r + 1)
                    for j in range(PER_GROUP):
                        nc.vector.tensor_tensor(
                            probs[:, r, j, :, :, :].rearrange("p b g n -> p (b g) n"),
                            bank[4 + j][:].rearrange("p (x n) -> p x n", n=P),
                            causal[:].unsqueeze(1).broadcast_to([P, 4, P]), ALU.mult).then_inc(probs_done, 1)

                def centre(c, b):
                    dve.wait_ge(y_done, c * BATCH + b + 1)
                    y3 = bank[2 + b % 2][:, 0:DIM].rearrange("p (h e) -> p h e", e=HEAD)
                    nc.vector.tensor_reduce(mean[:, b, :], y3, AX_X, ALU.add).then_inc(mean_done, 1)
                    dve.wait_ge(mean_done, c * BATCH + b + 1)
                    nc.vector.scalar_tensor_tensor(out=y[:, b, :].rearrange("p (h e) -> p h e", e=HEAD),
                                                   in0=mean[:, b, :].unsqueeze(2).broadcast_to([P, HEADS, HEAD]),
                                                   scalar=-1.0 / HEAD, in1=y3, op0=ALU.mult,
                                                   op1=ALU.add).then_inc(centre_done, 1)

                def gated(c, parity, h):
                    steps = norms[h]
                    steps.begin(c)
                    rows = slice(2 * h, 2 * h + 2)
                    dve.wait_ge(ysq_done, c * BATCH + 2 * h + 2)
                    vflat, rflat, nflat = (x[:, rows].rearrange("p b h -> p (b h)") for x in (var, rgn, newton1))
                    steps.done(nc.vector.tensor_reduce(vflat, ysq[:, rows].rearrange("p b (h e) -> p (b h) e", e=HEAD),
                                                       AX_X, ALU.add))
                    steps.wait()
                    steps.done(nc.vector.tensor_scalar(vflat, vflat, 1.0 / HEAD, EPS, ALU.mult, ALU.add))
                    inverse_root(steps, vflat, rflat, nflat)
                    steps.wait()
                    yh = y[:, rows].rearrange("p b (h e) -> p (b h) e", e=HEAD)
                    steps.done(nc.vector.tensor_tensor(
                        yh, yh, rflat.unsqueeze(2).broadcast_to([P, 2 * HEADS, HEAD]), ALU.mult))
                    steps.wait()
                    dve.wait_ge(gw_done, c * 4 + 2 * h + 2)
                    steps.done(nc.vector.tensor_tensor(y[:, rows], y[:, rows], gate[:, parity, rows], ALU.mult))
                    steps.wait()
                    nc.vector.tensor_tensor(y[:, rows], y[:, rows], gate_b[:, rows], ALU.add).then_inc(z_done, 1)
                    steps.end()

                def residual(c, parity):
                    dve.wait_ge(xtok_in[parity], loaded(c, parity))
                    if not (isinstance(c, int) and c < 2):
                        dve.wait_ge(x1_out[parity], (c - parity) * 8)
                    for n in range(2):
                        dve.wait_ge(wo_ps, c * 2 + n + 1)
                        nc.vector.tensor_tensor(r1[parity][:, 2 * n:2 * n + 2, :],
                                                bank[2 + n][:].rearrange("p (b d) -> p b d", b=2),
                                                xtok[:, parity, 2 * n:2 * n + 2, :], ALU.add).then_inc(r1_done, 1)

                def norm(c, parity):
                    ln1.begin(c)
                    dve.wait_ge(r1_done, c * 2 + 2)
                    layernorm(dve, ln1, r1[parity], mv1, rstd1, ve1, rs1, c, ln1_done)
                    ln1.end()

                def low_part_of_words(c):
                    dve.wait_ge(look_in, (c + 1) * 16)
                    w = look[:].bitcast(I32)
                    nc.vector.tensor_scalar(w, w, 0xFFF, None, ALU.bitwise_and).then_inc(low_bits, 1)

                def body(c, parity, follow, attend, more, more2):
                    n, other = c + 1, 1 - parity
                    if follow:
                        gated(c - 1, other, 1)
                    if not attend:
                        dve.wait_ge(low_added, CHUNKS)
                        nc.vector.tensor_reduce(low_all[:], low_sum[:], AX_X, ALU.add).then_inc(low_done, 1)
                    if attend:
                        masked(c, 0)
                    if more:
                        rotate(n, other, 1)
                    if attend:
                        centre(c, 0)
                    if follow and not (isinstance(c, int) and c == 1):
                        norm(c - 2, parity)
                    if more:
                        rotate(n, other, 2)
                    if attend:
                        centre(c, 1)
                        gated(c, parity, 0)
                        masked(c, 1)
                    if follow:
                        residual(c - 1, other)
                    if more:
                        rotate(n, other, 3)
                    if attend:
                        low_part_of_words(c)
                        centre(c, 2)
                    else:
                        dve.wait_ge(low_reduced, 1)
                        nc.vector.tensor_scalar(wide_flag[:], low_max[:], 0.0, None, ALU.is_gt).then_inc(flag_done, 1)
                        norm(c - 1, other)
                    if more2:
                        rotate(c + 2, parity, 0)
                    if attend:
                        centre(c, 3)

                for b in range(BATCH):
                    rotate(0, 0, b)
                rotate(1, 1, 0)
                dve.wait_ge(const_in, 16 * N_CONST)
                nc.vector.tensor_scalar(gnw[:], gnw[:], 0.5, None, ALU.mult).then_inc(gn_halved, 1)
                nc.vector.tensor_scalar(gnb[:], gnb[:], 0.5, None, ALU.mult).then_inc(gn_halved, 1)
                schedule1(dve, body)
                dve.wait_ge(flag_done, 1)

        def shared(ctx):
            t = {"x1in": x1in, "x1res": x1res, "y4": y4}
            for name, shape in (
                    ("wide_a", [P, KD, TOK]),
                    ("wide_b", [P, KD, TOK]),
                    ("x2", [P, BATCH, DIM]),
                    ("x2res", [P, BATCH, DIM]),
                    ("kvq", [P, BATCH, 3 * DIM]),
                    ("S", [P, NB, BS, BS]),
                    ("tmp", [P, NB, BS, BS]),
                    ("norm", [P, BATCH, NB]),
                    ("root", [P, BATCH, NB]),
                    ("newton", [P, BATCH, NB]),
                    ("delta", [P, NB, BS]),
                    ("Sq", [P, BATCH, DIM]),
                    ("x3", [P, BATCH, DIM]),
                    ("x3T", [P, KD, BATCH, P + 1]),
                    ("mv2", [P, BATCH, 2]), ("rstd2", [P, BATCH]),
                    ("mv3", [P, BATCH, 2]), ("rstd3", [P, BATCH]),
                    ("mv4", [P, BATCH, 2]), ("rstd4", [P, BATCH])):
                t[name] = sb(ctx, f"{name}_{len(made)}", shape)
            made.append(t)
            return t

        made = []
        with ExitStack() as ctx:
            tn = shared(ctx)
            tn["x1hi"] = sb(ctx, "x1hi", [P, KD, TOK], F32R)
            tn["x1lo"] = sb(ctx, "x1lo", [P, KD, TOK], F32R)
            tn["whole"] = sb(ctx, "whole", [P, 4, TOK])
            tn["a_hi"] = sb(ctx, "a_hi", [P, KH, TOK], F32R)
            tn["a_lo"] = sb(ctx, "a_lo", [P, KH, TOK], F32R)
            tn["b_hi"] = sb(ctx, "b_hi", [P, KH, TOK], F32R)
            tn["b_lo"] = sb(ctx, "b_lo", [P, KH, TOK], F32R)
            tn["ring"] = sb(ctx, "ring", [P, RING, KH, P], F32R)
            tn["spare"] = tn["whole"]
        narrow.close()
        with ExitStack() as ctx:
            tw = shared(ctx)
            tw["a"] = sb(ctx, "hid_a", [P, KH, TOK])
            tw["b"] = sb(ctx, "hid_b", [P, KH, TOK])
            tw["spare"] = tw["a"]
            tw["ffn"] = sb(ctx, "ffn_w", [P, FFN_COLS])

        with ExitStack() as ctx:
            sem2 = lambda name: sem(ctx, name)
            out_done = sem2("out_done")
            wide_in = sem2("wide_in")
            ring_in = [sem2(f"ring_in{n}") for n in range(RING)]
            prep = sem2("prep")
            x1T_ps, x1T_done, x1lo_done = sem2("x1T_ps"), sem2("x1T_done"), sem2("x1lo_done")
            w12_ps, th_done, prod_mid, prod_done = sem2("w12_ps"), sem2("th_done"), sem2("prod_mid"), sem2("prod_done")
            hid_ps, act_done = sem2("hid_ps"), sem2("act_done")
            hi_done, lo_done = sem2("hi_done"), sem2("lo_done")
            w3_ps, scaled_done, r2_done = sem2("w3_ps"), sem2("scaled_done"), sem2("r2_done")
            ve2, rs2, ln2_steps, ln2_done = sem2("ve2"), sem2("rs2"), sem2("ln2_steps"), sem2("ln2_done")
            x2T_ps, x2T_done, kvq_ps, kvq_done = sem2("x2T_ps"), sem2("x2T_done"), sem2("kvq_ps"), sem2("kvq_done")
            ksq_done = sem2("ksq_done")
            scan_steps, tail_steps, x2_kept = sem2("scan_steps"), sem2("tail_steps"), sem2("x2_kept")
            pre_tanh, post_tanh = sem2("pre_tanh"), sem2("post_tanh")
            sq_done, sq_tanh = sem2("sq_done"), sem2("sq_tanh")
            delta_ready, outer_done, readq_done = sem2("delta_ready"), sem2("outer_done"), sem2("readq_done")
            ve3, rs3, ln3_steps, ln3_done = sem2("ve3"), sem2("rs3"), sem2("ln3_steps"), sem2("ln3_done")
            x3T_ps, x3T_col, x3T_done = sem2("x3T_ps"), sem2("x3T_col"), sem2("x3T_done")
            part_done, mixk_done, mixr_done = sem2("part_done"), sem2("mixk_done"), sem2("mixr_done")
            dk_ps, relu_done, kact_done = sem2("dk_ps"), sem2("relu_done"), sem2("kact_done")
            dr_ps, sig_done, dv_ps, gated4 = sem2("dr_ps"), sem2("sig_done"), sem2("dv_ps"), sem2("gated4")
            ve4, rs4, ln4_steps, ln4_done = sem2("ve4"), sem2("rs4"), sem2("ln4_steps"), sem2("ln4_done")
            N_FFN_IN = 11
            N_LN2, N_LN3, N_LN4 = 4, 6, 4
            N_NORM = 16
            N_SCAN = N_NORM + 2 * (BATCH - 1) + 2 * 4 * (BATCH - 1)
            N_TAIL = 2

            def bank_of(n):
                return bank[(n if n < KH else n + 2) % 4]

            def read_before(n):
                return n - 2 if n in (KH, KH + 1) else n - 6 if n in (KH + 2, KH + 3) else n - 4

            def pair(m):
                return PAIRS[m]
            SPLITS = 3 * KH

            def half_blocks(t, s, hf):
                n0 = hf * HALF
                k, v, q = (t["kvq"][:, s, a * DIM + n0 * BS:a * DIM + (n0 + HALF) * BS].rearrange(
                    "p (n j) -> p n j", j=BS) for a in range(3))
                return k, v, q, t["S"][:, n0:n0 + HALF], t["delta"][:, n0:n0 + HALF, :]

            def along_j(x):
                return x.unsqueeze(2).broadcast_to([P, HALF, BS, BS])

            def along_i(x):
                return x.unsqueeze(3).broadcast_to([P, HALF, BS, BS])

            def last_buffers(t, hf):
                sq = (t["x1in"], t["x1res"])[hf][:].rearrange("p b d -> p (b d)").rearrange(
                    "p (n i j) -> p n i j", i=BS, j=BS)
                outer = t["spare"][:].rearrange("p m n -> p (m n)")[:, hf * HALF * BS * BS:(hf + 1) * HALF * BS * BS].rearrange(
                    "p (n i j) -> p n i j", i=BS, j=BS)
                return sq, outer

            def schedule(eng, body):
                for i in range(3):
                    body(i, True, i >= 1, i >= 2, i + 1 < CHUNKS)
                with eng.Fori(3, CHUNKS - 1) as i:
                    body(i, True, True, True, True)
                body(CHUNKS - 1, True, True, True, False)
                body(CHUNKS, False, True, True, False)
                body(CHUNKS + 1, False, False, True, False)

            def sync_program(sp, narrow_w):
                t = tn if narrow_w else tw

                def x1_rows(c):
                    return x1_d[bass.ds(c, 1)].rearrange("o p b d -> (o p) b d")

                def ring_load(c, n, free=None):
                    if free is not None:
                        sp.wait_ge(hid_ps, free)
                    sp.dma_start(t["ring"][:, n % RING].bitcast(F32).rearrange("p k n -> p (k n)"),
                                 ffn_s[:, COL_H1 + n * HID:COL_H1 + (n + 1) * HID]).then_inc(ring_in[n % RING], 16)

                out_view = out_d.rearrange("b (c p) d -> p c b d", p=P)
                if narrow_w:
                    for n in range(RING):
                        ring_load(0, n)
                else:
                    sp.dma_start(t["ffn"][:], ffn_d).then_inc(wide_in, 16)

                sp.wait_ge(x1_out[1], 16 * (CHUNKS // 2))

                def body(i, ffn, scan, mix, more):
                    if more:
                        sp.wait_ge(x1T_ps, i * 2 + 2)
                        sp.dma_start(t["x1in"][:], x1_rows(i + 1)).then_inc(x1in_in, 16)
                    if scan and ffn:
                        sp.wait_ge(r2_done, i * 2)
                        sp.dma_start(t["x1res"][:], x1_rows(i)).then_inc(x1res_in, 16)
                    if ffn and narrow_w:
                        for n in range(RING, 2 * KH):
                            ring_load(i, n, i * 2 * KH + n - RING + 1)
                    if mix:
                        sp.wait_ge(ln4_done, i - 1)
                        sp.dma_start(out_view[:, bass.ds(i - 2, 1)].rearrange("p o b d -> p (o b) d"),
                                     t["y4"][:]).then_inc(out_done, 16)
                    if more and narrow_w:
                        for n in range(RING):
                            ring_load(i + 1, n, i * 2 * KH + 2 * KH - RING + n + 1)

                schedule(sp, body)
                sp.wait_ge(out_done, 16 * CHUNKS)

            def tensor_program(pe, narrow_w):
                t = tn if narrow_w else tw
                wide_a, wide_b, x2, x3 = t["wide_a"], t["wide_b"], t["x2"], t["x3"]
                pe.wait_ge(ffn_in, 16 * N_FFN_IN)
                if narrow_w:
                    pe.wait_ge(w123_in, 16 * 3)
                else:
                    pe.wait_ge(wide_in, 16)

                def weight(col, k, n, a, z):
                    return t["ffn"][:, col + k * n + a:col + k * n + z]

                def transposes(src, lo, ps):
                    for k in range(KD):
                        for b in range(BATCH):
                            ins = nc.tensor.transpose(bank[lo + k][:, b * P:b * P + P], src[:, b, k * P:k * P + P],
                                                      ident[:])
                        ins.then_inc(ps, 1)

                def x1_transposed(c):
                    pe.wait_ge(x1in_in, (c + 1) * 16)
                    transposes(t["x1in"], 6, x1T_ps)

                def product(out, pairs, first=True, last=True):
                    for n, (a, b) in enumerate(pairs):
                        ins = nc.tensor.matmul(out, a, b, start=(first and n == 0), stop=(last and n == len(pairs) - 1))
                    return ins

                def up(c, tiles, first=False):
                    if tiles[0] == 0:
                        pe.wait_ge(x1T_done, c * 2 + 2)
                        if narrow_w:
                            pe.wait_ge(x1lo_done, c * 2 + 2)
                    for m in tiles:
                        before = {3: 0, 4: 1, 6: 2, 7: 4}
                        if m in before:
                            pe.wait_ge(prod_done, c * KH + before[m] + 1)
                        elif m == 1 and not (isinstance(c, int) and c < 3):
                            pe.wait_ge(gated4, (c - 2) * 2)
                        elif m == 5 and not first:
                            pe.wait_ge(scaled_done, c * 2)
                        elif m == 2 and not (isinstance(c, int) and c == 0):
                            if narrow_w:
                                pe.wait_ge(hi_done, c * SPLITS - 2)
                            else:
                                pe.wait_ge(act_done, c * 2 * KH - 2)
                        cols = slice(m * P, m * P + P)
                        for n in range(2):
                            if narrow_w:
                                w = (w1r, w2r)[n]
                                pairs = [(w[:, k, cols], x[:, k, :]) for k in range(KD) for x in (t["x1hi"], t["x1lo"])]
                            else:
                                pairs = [(weight((COL_W1, COL_W2)[n], k, HID, m * P, m * P + P), wide_a[:, k, :])
                                         for k in range(KD)]
                            ins = product(bank[pair(m) + n][:], pairs)
                        ins.then_inc(w12_ps, 1)

                def hidden(c, layer, m):
                    n = layer * KH + m
                    if not narrow_w:
                        if m == 0 and layer == 0:
                            pe.wait_ge(prod_done, c * KH + KH)
                        if m == 0 and layer == 1:
                            pe.wait_ge(act_done, c * 2 * KH + KH)
                        if n >= 4:
                            pe.wait_ge(act_done, c * 2 * KH + read_before(n) + 1)
                        src = t["ab"[layer]]
                        ins = product(bank_of(n)[:],
                                      [(weight(COL_H1, n * KH + k, P, 0, P), src[:, k, :]) for k in range(KH)])
                        ins.then_inc(hid_ps, 1)
                        return
                    pe.wait_ge(ring_in[n % RING], c * (2 * KH // RING) * 16 + (n // RING + 1) * 16)
                    if n >= 4:
                        pe.wait_ge(hi_done, c * SPLITS + KH + read_before(n) + 1)
                    else:
                        pe.wait_ge(prod_done, c * KH + KH)
                    hi, lo = (t["a_hi"], t["a_lo"]) if layer == 0 else (t["b_hi"], t["b_lo"])
                    w = t["ring"][:, n % RING]
                    if m == 0:
                        for k in range(KH):
                            pe.wait_ge(hi_done, c * SPLITS + layer * KH + k + 1)
                            product(bank_of(n)[:], [(w[:, k, :], hi[:, k, :])], first=(k == 0), last=False)
                        pe.wait_ge(lo_done, c * SPLITS + layer * KH + KH)
                        ins = product(bank_of(n)[:], [(w[:, k, :], lo[:, k, :]) for k in range(KH)], first=False)
                    else:
                        ins = product(bank_of(n)[:], [(w[:, k, :], x[:, k, :]) for k in range(KH) for x in (hi, lo)])
                    ins.then_inc(hid_ps, 1)

                def down(c):
                    if narrow_w:
                        pe.wait_ge(hi_done, c * SPLITS + 3 * KH)
                        pe.wait_ge(lo_done, c * SPLITS + 3 * KH)
                    else:
                        pe.wait_ge(act_done, c * 2 * KH + 2 * KH)
                    for b in range(BATCH):
                        rows = slice(b * P, b * P + P)
                        if narrow_w:
                            pairs = [(x[:, k, rows], w3r[:, k, :]) for k in range(KH) for x in (t["a_hi"], t["a_lo"])]
                        else:
                            pairs = [(t["a"][:, k, rows], weight(COL_W3, k, DIM, 0, DIM)) for k in range(KH)]
                        ins = product(bank[b // 2][:, (b % 2) * DIM:(b % 2) * DIM + DIM], pairs)
                        if b % 2:
                            ins.then_inc(w3_ps, 1)

                def scan_inputs(c, ffn):
                    pe.wait_ge(x2T_done, c * 2 + 2)
                    for b in range(BATCH):
                        lo = KVQ_BANKS[b]
                        if ffn and b in (0, 2):
                            pe.wait_ge(prod_done, (c + 1) * KH + (6, 0, 8)[b])
                        elif b == 3:
                            pe.wait_ge(kvq_done, c * 2 * BATCH + 4)
                        for n, (a, z) in enumerate(((0, 512), (512, 768))):
                            ins = product(bank[lo + n][:, 0:z - a],
                                          [(wide_b[:, k, b * P:b * P + P], wkvq[:, k, a:z]) for k in range(KD)])
                        ins.then_inc(kvq_ps, 1)

                def by_row(src, w, lo, ps):
                    for b in range(BATCH):
                        ins = product(bank[lo + b // 2][:, (b % 2) * DIM:(b % 2) * DIM + DIM],
                                      [(src[:, k, b * P:b * P + P], w[:, k, :]) for k in range(KD)])
                        if b % 2:
                            ins.then_inc(ps, 1)

                def mix_in(c):
                    pe.wait_ge(mixk_done, c * 2 + 2)
                    for m in range(KD):
                        product(bank[4 + m][:], [(wk[:, k, m * P:m * P + P], wide_a[:, k, :]) for k in range(KD)]
                                ).then_inc(dk_ps, 1)
                    pe.wait_ge(mixr_done, c * 2 + 2)
                    by_row(wide_b, wr, 6, dr_ps)

                def body(i, ffn, scan, mix, more):
                    c, d = i - 1, i - 2
                    if ffn:
                        up(i, range(3, KH - 1), first=not scan)
                    if scan:
                        pe.wait_ge(ln2_done, c + 1)
                        if ffn:
                            pe.wait_ge(prod_done, i * KH + 4)
                        transposes(x2, 6, x2T_ps)
                    if ffn:
                        up(i, [KH - 1])
                    if scan:
                        scan_inputs(c, ffn)
                    if ffn:
                        if scan:
                            pe.wait_ge(kvq_done, c * 2 * BATCH + 2)
                        hidden(i, 0, 0)
                        hidden(i, 0, 1)
                    if mix:
                        pe.wait_ge(ln3_done, d + 1)
                        if scan:
                            pe.wait_ge(kvq_done, c * 2 * BATCH + 6)
                        transposes(x3, 4, x3T_ps)
                    if ffn:
                        for m in range(2, KH):
                            hidden(i, 0, m)
                    if mix:
                        mix_in(d)
                    if ffn:
                        hidden(i, 1, 0)
                    if mix:
                        pe.wait_ge(kact_done, d * 2 + 2)
                        by_row(wide_a, wv, 4, dv_ps)
                    if ffn:
                        hidden(i, 1, 1)
                        if more:
                            if mix:
                                pe.wait_ge(sig_done, d * 2 + 2)
                            elif scan:
                                pe.wait_ge(kvq_done, i * 2 * BATCH)
                            x1_transposed(i + 1)
                        for m in range(2, KH):
                            hidden(i, 1, m)
                        if more:
                            up(i + 1, range(3))
                        down(i)

                x1_transposed(0)
                up(0, range(3))
                schedule(pe, body)

            def scalar_program(act, narrow_w):
                t = tn if narrow_w else tw
                wide_a, wide_b, S, tmp, kvq, x2 = t["wide_a"], t["wide_b"], t["S"], t["tmp"], t["kvq"], t["x2"]
                x3T, y4 = t["x3T"], t["y4"]
                act.wait_ge(ffn_in, 16 * N_FFN_IN)
                act.wait_ge(prep, 9)

                def evacuate(dst, lo, c, ps, done):
                    for k in range(KD):
                        act.wait_ge(ps, c * 2 + k + 1)
                        nc.scalar.copy(dst[:, k, :], bank[lo + k][:]).then_inc(done, 1)

                def scan_tanh(c, n, hf):
                    act.wait_ge(pre_tanh, c * 8 + 2 * n + hf + 1)
                    half = S[:, hf * HALF:hf * HALF + HALF, :, :].rearrange("p n i j -> p (n i j)")
                    nc.scalar.activation(half, half, ACT.Tanh).then_inc(post_tanh, 1)

                def product_hi(c, m):
                    act.wait_ge(prod_done, c * KH + m + 1)
                    nc.scalar.copy(t["a_hi"][:, m, :], t["whole"][:, m % 4, :]).then_inc(hi_done, 1)

                def gelu(c, layer, m):
                    n = layer * KH + m
                    act.wait_ge(hid_ps, c * 2 * KH + n + 1)
                    scale = (hs1, hs2)[layer][:, m:m + 1]
                    if not narrow_w:
                        nc.scalar.activation(t["ba"[layer]][:, m, :], bank_of(n)[:], ACT.Gelu,
                                             scale=scale).then_inc(act_done, 1)
                        return
                    act.wait_ge(lo_done, c * SPLITS + KH + n - 3)
                    nc.scalar.activation(t["whole"][:, m % 4, :], bank_of(n)[:], ACT.Gelu, scale=scale).then_inc(act_done, 1)
                    nc.scalar.activation((t["b_hi"], t["a_hi"])[layer][:, m, :], bank_of(n)[:], ACT.Gelu,
                                         scale=scale).then_inc(hi_done, 1)

                def body(i, ffn, scan, mix, more):
                    c, d = i - 1, i - 2
                    started = isinstance(i, int) and i == 0
                    if ffn:
                        for m in range(KH):
                            if not narrow_w:
                                if m == 0 and not started:
                                    act.wait_ge(w3_ps, i * 2)
                                dst = t["a"][:, m, :]
                            else:
                                if m >= 4 or not started:
                                    act.wait_ge(lo_done, i * SPLITS + m - 3)
                                dst = t["whole"][:, m % 4, :]
                            act.wait_ge(w12_ps, i * KH + m + 1)
                            nc.scalar.activation(dst, bank[pair(m)][:], ACT.Tanh, scale=s1half[:, m:m + 1]
                                                 ).then_inc(th_done, 1)
                            if narrow_w and m == 2:
                                if not started:
                                    act.wait_ge(w3_ps, i * 2)
                                product_hi(i, 0)
                                product_hi(i, 1)
                            if narrow_w and m >= 3:
                                product_hi(i, m - 1)
                            if scan and m == KH - 2:
                                evacuate(wide_b, 6, c, x2T_ps, x2T_done)
                        if narrow_w:
                            product_hi(i, KH - 1)
                    elif scan:
                        evacuate(wide_b, 6, c, x2T_ps, x2T_done)

                    def silu_tanh():
                        act.wait_ge(sq_done, (d + 1) * 2 * BATCH)
                        nc.scalar.activation(tmp[:, 0:HALF, :, :].rearrange("p n i j -> p (n i j)"),
                                             t["Sq"][:].rearrange("p b d -> p (b d)"), ACT.Tanh,
                                             scale=0.5).then_inc(sq_tanh, 1)

                    def kvq_out(b):
                        lo = KVQ_BANKS[b]
                        act.wait_ge(kvq_ps, c * BATCH + b + 1)
                        if mix:
                            act.wait_ge(sq_done, (c - 1) * 2 * BATCH + 2 * b + 2)
                        nc.scalar.copy(kvq[:, b, 0:512], bank[lo][:]).then_inc(kvq_done, 1)
                        nc.scalar.copy(kvq[:, b, 512:768], bank[lo + 1][:, 0:DIM]).then_inc(kvq_done, 1)

                    def part(dst, nu):
                        for k in range(KD):
                            nc.scalar.activation(dst[:, k, :].rearrange("p (b n) -> p b n", b=BATCH),
                                                 x3T[:, k, :, 0:P], ACT.Copy, scale=nu[:, k:k + 1]).then_inc(part_done, 1)

                    def mix_parts():
                        nc.scalar.copy(x3T[:, :, :, 0], x3T[:, :, :, P]).then_inc(x3T_col, 1)
                        act.wait_ge(x3T_col, d + 1)
                        for k in range(KD):
                            act.wait_ge(x3T_ps, d * 2 + k + 1)
                            nc.scalar.copy(x3T[:, k, :, 1:P + 1], bank[4 + k][:].rearrange("p (b n) -> p b n", b=BATCH)
                                           ).then_inc(x3T_done, 1)
                        act.wait_ge(x3T_done, d * 2 + 2)
                        if not (isinstance(i, int) and i == 2):
                            act.wait_ge(dv_ps, d * 2)
                        part(wide_a, nu_k)
                        part(wide_b, nu_r)

                    if mix and not ffn:
                        silu_tanh()
                    if scan:
                        kvq_out(0)
                        kvq_out(1)
                    if mix and ffn:
                        silu_tanh()
                    if scan:
                        kvq_out(2)
                        kvq_out(3)
                        act.wait_ge(kvq_done, (c + 1) * 2 * BATCH)
                        if mix:
                            act.wait_ge(ln3_steps, (c - 1) * N_LN3 + 3)
                        nc.scalar.activation(tmp[:, 0:HALF, :, :].rearrange("p n i j -> p (n i j)").rearrange(
                            "p (b d) -> p b d", b=BATCH), kvq[:, :, 0:DIM], ACT.Square).then_inc(ksq_done, 1)

                    for n in range(2 * KH):
                        if ffn:
                            gelu(i, n // KH, n % KH)
                        if n == 1:
                            if mix:
                                mix_parts()
                            if scan:
                                nc.scalar.copy(t["x2res"][:], x2[:]).then_inc(x2_kept, 1)
                        if scan:
                            if n == 2:
                                scan_tanh(c, 0, 0)
                                scan_tanh(c, 0, 1)
                            if n in (5, 7, 9, 14, 15):
                                half = (5, 7, 0, 9, 14, 15).index(n)
                                scan_tanh(c, 1 + half // 2, half % 2)
                        if n == KH - 1:
                            if mix:
                                act.wait_ge(dk_ps, d * 2 + 2)
                                for k in range(KD):
                                    nc.scalar.activation(wide_a[:, k, :], bank[4 + k][:], ACT.Relu).then_inc(relu_done, 1)
                                act.wait_ge(relu_done, d * 2 + 2)
                                for k in range(KD):
                                    nc.scalar.activation(wide_a[:, k, :], wide_a[:, k, :], ACT.Square).then_inc(kact_done, 1)
                                if isinstance(i, int) and i == 2:
                                    act.wait_ge(x1_out[1], 16 * (CHUNKS // 2))
                                else:
                                    act.wait_ge(out_done, (i - 2) * 16)
                                for r in range(2):
                                    act.wait_ge(dr_ps, d * 2 + r + 1)
                                    nc.scalar.activation(y4[:, 2 * r:2 * r + 2, :],
                                                         bank[6 + r][:].rearrange("p (b d) -> p b d", b=2),
                                                         ACT.Tanh, scale=0.5).then_inc(sig_done, 1)
                            if scan:
                                scan_tanh(c, 2, 0)
                        if more and n == KH + 1:
                            evacuate(t["x1hi"] if narrow_w else wide_a, 6, i + 1, x1T_ps, x1T_done)

                evacuate(t["x1hi"] if narrow_w else wide_a, 6, 0, x1T_ps, x1T_done)
                schedule(act, body)

            def gpsimd_program(pool, narrow_w):
                t = tn if narrow_w else tw

                def root(dst, src, n, expo, ready, done, c):
                    pool.wait_ge(ready, c + 1)
                    nc.gpsimd.tensor_tensor(dst, src, expo[:, 0:n], ALU.pow).then_inc(done, 1)

                def help_step(c, s):
                    for hf in range(2):
                        q, st = half_blocks(t, s, hf)[2:4]
                        k, _, _, _, dl = half_blocks(t, s + 1, hf)
                        sq, outer = last_buffers(t, hf)
                        pool.wait_ge(post_tanh, c * 8 + 2 * s + hf + 1)
                        if s:
                            pool.wait_ge(sq_done, c * 8 + 2 * (s - 1) + hf + 1)
                        nc.gpsimd.tensor_tensor(sq, st, along_j(q), ALU.mult).then_inc(readq_done, 1)
                        pool.wait_ge(delta_ready, 2 * s + hf + 1)
                        nc.gpsimd.tensor_tensor(outer, along_i(dl), along_j(k), ALU.mult).then_inc(outer_done, 1)

                def low_part(layer, m, c):
                    hi, lo = (t["b_hi"], t["b_lo"]) if layer == 1 else (t["a_hi"], t["a_lo"])
                    pool.wait_ge(hi_done, c * SPLITS + layer * KH + m + 1)
                    nc.gpsimd.tensor_tensor(lo[:, m, :], t["whole"][:, m % 4, :], hi[:, m, :].bitcast(F32),
                                            ALU.subtract).then_inc(lo_done, 1)

                def body(i, ffn, scan, mix, more):
                    if ffn and narrow_w:
                        for m in range(2):
                            low_part(0, m, i)
                    if scan:
                        root(t["rstd2"][:], t["mv2"][:, :, 1], BATCH, inv_pow, ve2, rs2, i - 1)
                    if ffn and narrow_w:
                        for m in range(2, KH):
                            low_part(0, m, i)
                    if mix:
                        root(t["rstd3"][:], t["mv3"][:, :, 1], BATCH, inv_pow, ve3, rs3, i - 2)
                    last = isinstance(i, int) and i == CHUNKS
                    if last:
                        for s in range(2):
                            help_step(i - 1, s)
                    for n in range(2 * KH):
                        if ffn and narrow_w:
                            low_part(1 + n // KH, n % KH, i)
                        if mix and n == KH + 1:
                            root(t["rstd4"][:], t["mv4"][:, :, 1], BATCH, inv_pow, ve4, rs4, i - 2)
                    if last:
                        help_step(i - 1, 2)

                schedule(pool, body)

            def vector_program(dve, narrow_w):
                t = tn if narrow_w else tw
                wide_a, wide_b, S, tmp, kvq = t["wide_a"], t["wide_b"], t["S"], t["tmp"], t["kvq"]
                x3T, y4, x2, x3, Sq, delta = t["x3T"], t["y4"], t["x2"], t["x3"], t["Sq"], t["delta"]
                dve.wait_ge(ffn_in, 16 * N_FFN_IN)
                nc.vector.tensor_scalar(s1half[:], s1[:], 0.5, None, ALU.mult).then_inc(prep, 1)
                nc.vector.tensor_tensor(s12half[:], s1[:], s2[:], ALU.mult).then_inc(prep, 1)
                dve.wait_ge(prep, 2)
                nc.vector.tensor_scalar(s12half[:], s12half[:], 0.5, None, ALU.mult).then_inc(prep, 1)
                nc.vector.tensor_scalar(nu_r[:], mu_r[:], -1.0, 1.0, ALU.mult, ALU.add).then_inc(prep, 1)
                nc.vector.tensor_scalar(nu_k[:], mu_k[:], -1.0, 1.0, ALU.mult, ALU.add).then_inc(prep, 1)
                for k in range(KD):
                    for col in (0, P):
                        nc.vector.memset(x3T[:, k, :, col], 0.0).then_inc(prep, 1)
                dve.wait_ge(prep, 9)
                ln2, ln3, ln4 = (Steps(dve, ln2_steps, N_LN2), Steps(dve, ln3_steps, N_LN3),
                                 Steps(dve, ln4_steps, N_LN4))
                scan, tail = Steps(dve, scan_steps, N_SCAN), Steps(dve, tail_steps, N_TAIL)
                kb4 = kvq[:, :, 0:DIM].rearrange("p b (n j) -> p b n j", j=BS)

                def x1_low(c):
                    for k in range(KD):
                        dve.wait_ge(x1T_done, c * 2 + k + 1)
                        nc.vector.tensor_tensor(t["x1lo"][:, k, :], bank[6 + k][:], t["x1hi"][:, k, :].bitcast(F32),
                                                ALU.subtract).then_inc(x1lo_done, 1)

                def product(c, m):
                    w = t["whole"][:, m % 4, :] if narrow_w else t["a"][:, m, :]
                    dve.wait_ge(th_done, c * KH + m + 1)
                    nc.vector.scalar_tensor_tensor(out=w, in0=w, scalar=1.0, in1=bank[pair(m)][:], op0=ALU.add,
                                                   op1=ALU.mult).then_inc(prod_mid, 1)
                    dve.wait_ge(prod_mid, c * KH + m + 1)
                    nc.vector.scalar_tensor_tensor(out=w, in0=bank[pair(m) + 1][:],
                                                   scalar=s12half[:, m:m + 1], in1=w,
                                                   op0=ALU.mult, op1=ALU.mult).then_inc(prod_done, 1)

                def key_norms(c):
                    scan.begin(c)
                    x, y, z = (t[n][:].rearrange("p b n -> p (b n)") for n in ("norm", "root", "newton"))
                    dve.wait_ge(ksq_done, c + 1)
                    scan.done(nc.vector.tensor_reduce(x, tmp[:, 0:HALF, :, :].rearrange("p n i j -> p (n i) j"),
                                                      AX_X, ALU.add))
                    inverse_root(scan, x, y, z)
                    scan.wait()
                    scan.done(nc.vector.tensor_tensor(x, x, y, ALU.mult))
                    scan.wait()
                    scan.done(nc.vector.tensor_scalar(x, x, 1e-6, None, ALU.add))
                    scan.wait()
                    scan.done(nc.vector.reciprocal(x, x))
                    scan.wait()
                    scan.done(nc.vector.tensor_tensor(kb4, kb4, t["norm"][:].unsqueeze(3).broadcast_to(
                        [P, BATCH, NB, BS]), ALU.mult))
                    scan.wait()
                    assert scan.k == N_NORM, scan.k

                def parts(s, hf):
                    k, v, q, st, _ = half_blocks(t, s, hf)
                    return k, v, q, st, tmp[:, hf * HALF:hf * HALF + HALF]

                def first_update(c):
                    for hf in range(2):
                        k, v, q, s, _ = parts(0, hf)
                        nc.vector.tensor_tensor(s, along_i(v), along_j(k), ALU.mult).then_inc(pre_tanh, 1)

                def read_out(c, s, hf, steps):
                    k, v, q, st, w = parts(s, hf)
                    dve.wait_ge(post_tanh, c * 8 + 2 * s + hf + 1)
                    steps.done(nc.vector.tensor_tensor(w, st, along_j(q), ALU.mult))
                    steps.wait()
                    nc.vector.tensor_reduce(Sq[:, s, hf * HALF * BS:(hf + 1) * HALF * BS].rearrange(
                        "p (n i) -> p n i", i=BS), w, AX_X, ALU.add).then_inc(sq_done, 1)

                def update(c, s, hf):
                    k, v, q, st, w = parts(s, hf)
                    dl = delta[:, hf * HALF:hf * HALF + HALF, :]
                    dve.wait_ge(sq_done, c * 2 * BATCH + 2 * (s - 1) + hf + 1)
                    scan.done(nc.vector.tensor_tensor(w, st, along_j(k), ALU.mult))
                    scan.wait()
                    scan.done(nc.vector.tensor_reduce(dl, w, AX_X, ALU.add))
                    scan.wait()
                    scan.done(nc.vector.tensor_tensor(dl, v, dl, ALU.subtract))
                    scan.wait()
                    scan.done(nc.vector.tensor_tensor(w, along_i(dl), along_j(k), ALU.mult))
                    scan.wait()
                    nc.vector.tensor_tensor(st, st, w, ALU.add).then_inc(pre_tanh, 1)

                def scan_step(c, s):
                    for hf in range(2):
                        read_out(c, s, hf, scan)
                        update(c, s + 1, hf)

                def last_step(c, s):
                    for hf in range(2):
                        k, v, q, st, dl = half_blocks(t, s + 1, hf)
                        w = tmp[:, hf * HALF:hf * HALF + HALF]
                        dve.wait_ge(post_tanh, c * 8 + 2 * s + hf + 1)
                        scan.done(nc.vector.tensor_tensor(w, st, along_j(k), ALU.mult))
                        scan.wait()
                        scan.done(nc.vector.tensor_reduce(dl, w, AX_X, ALU.add))
                        scan.wait()
                        nc.vector.tensor_tensor(dl, v, dl, ALU.subtract).then_inc(delta_ready, 1)
                    for hf in range(2):
                        st, (sq, outer) = half_blocks(t, s, hf)[3], last_buffers(t, hf)
                        dve.wait_ge(outer_done, 2 * s + hf + 1)
                        dve.wait_ge(readq_done, 2 * s + hf + 1)
                        nc.vector.tensor_tensor(st, st, outer, ALU.add).then_inc(pre_tanh, 1)
                        nc.vector.tensor_reduce(Sq[:, s, hf * HALF * BS:(hf + 1) * HALF * BS].rearrange(
                            "p (n i) -> p n i", i=BS), sq, AX_X, ALU.add).then_inc(sq_done, 1)

                def scan_out(c):
                    tail.begin(c)
                    for hf in range(2):
                        read_out(c, BATCH - 1, hf, tail)
                    tail.end()
                    ln3.begin(c)
                    dve.wait_ge(sq_tanh, c + 1)
                    dve.wait_ge(x2_kept, c + 1)
                    sqf = Sq[:].rearrange("p b d -> p (b d)")
                    thf = tmp[:, 0:HALF, :, :].rearrange("p n i j -> p (n i j)")
                    x3f = x3[:].rearrange("p b d -> p (b d)")
                    ln3.done(nc.vector.scalar_tensor_tensor(out=x3f, in0=thf, scalar=1.0, in1=sqf,
                                                            op0=ALU.add, op1=ALU.mult))
                    ln3.wait()
                    ln3.done(nc.vector.scalar_tensor_tensor(out=x3f, in0=x3f, scalar=0.5, in1=sqf,
                                                            op0=ALU.mult, op1=ALU.mult))
                    ln3.wait()
                    ln3.done(nc.vector.tensor_tensor(x3[:], x3[:], t["x2res"][:], ALU.add))
                    layernorm(dve, ln3, x3, t["mv3"], t["rstd3"], ve3, rs3, c, ln3_done)
                    ln3.end()

                def mix_inputs(d, n, dst, mu, done):
                    for k in range(KD):
                        dve.wait_ge(part_done, d * 4 + 2 * n + k + 1)
                        w = dst[:, k, :].rearrange("p (b n) -> p b n", b=BATCH)
                        nc.vector.scalar_tensor_tensor(out=w, in0=x3T[:, k, :, 1:P + 1], scalar=mu[:, k:k + 1],
                                                       in1=w, op0=ALU.mult, op1=ALU.add).then_inc(done, 1)

                def mix_result(d, meanwhile=None):
                    ln4.begin(d)
                    for n in range(2):
                        dve.wait_ge(dv_ps, d * 2 + n + 1)
                        dve.wait_ge(sig_done, d * 2 + n + 1)
                        w = y4[:, 2 * n:2 * n + 2, :]
                        nc.vector.scalar_tensor_tensor(out=w, in0=w, scalar=1.0,
                                                       in1=bank[4 + n][:].rearrange("p (b d) -> p b d", b=2),
                                                       op0=ALU.add, op1=ALU.mult).then_inc(gated4, 1)
                    dve.wait_ge(gated4, d * 2 + 2)
                    yf, xf = y4[:].rearrange("p b d -> p (b d)"), x3[:].rearrange("p b d -> p (b d)")
                    ln4.done(nc.vector.scalar_tensor_tensor(out=yf, in0=yf, scalar=0.5, in1=xf,
                                                            op0=ALU.mult, op1=ALU.add))
                    layernorm(dve, ln4, y4, t["mv4"], t["rstd4"], ve4, rs4, d, ln4_done, meanwhile)
                    ln4.end()

                def ffn_out(c, meanwhile=None):
                    ln2.begin(c)
                    dve.wait_ge(x1res_in, (c + 1) * 16)
                    for n in range(2):
                        dve.wait_ge(w3_ps, c * 2 + n + 1)
                        w = x2[:, 2 * n:2 * n + 2, :]
                        nc.vector.tensor_tensor(w, bank[n][:].rearrange("p (b d) -> p b d", b=2),
                                                s3[:].unsqueeze(1).broadcast_to([P, 2, DIM]),
                                                ALU.mult).then_inc(scaled_done, 1)
                        dve.wait_ge(scaled_done, c * 2 + n + 1)
                        nc.vector.tensor_tensor(w, w, t["x1res"][:, 2 * n:2 * n + 2, :], ALU.add).then_inc(r2_done, 1)
                        dve.wait_ge(r2_done, c * 2 + n + 1)
                        row_stats(ln2, x2, range(2 * n, 2 * n + 2))
                    layernorm(dve, ln2, x2, t["mv2"], t["rstd2"], ve2, rs2, c, ln2_done, meanwhile,
                              have_stats=True)
                    ln2.end()

                def body(i, ffn, has_scan, mix, more):
                    c, d = i - 1, i - 2
                    if has_scan:
                        ffn_out(c, (lambda: product(i, 3)) if ffn else None)
                    if ffn:
                        for m in range(4 if has_scan else 3, KH):
                            product(i, m)
                    if mix:
                        scan_out(d)
                    if has_scan:
                        key_norms(c)
                        first_update(c)
                    if mix:
                        mix_inputs(d, 0, wide_a, mu_k, mixk_done)
                        mix_inputs(d, 1, wide_b, mu_r, mixr_done)
                    last = isinstance(i, int) and i == CHUNKS
                    step = last_step if last else scan_step
                    if has_scan:
                        step(c, 0)
                        step(c, 1)
                    low = more and narrow_w
                    if mix:
                        mix_result(d, (lambda: x1_low(i + 1)) if low else None)
                    elif low:
                        x1_low(i + 1)
                    if has_scan:
                        step(c, 2)
                        if not last:
                            scan.end()
                    if more:
                        for m in range(3):
                            product(i + 1, m)

                if narrow_w:
                    x1_low(0)
                for m in range(3):
                    product(0, m)
                schedule(dve, body)

            block = ctx.enter_context(nc.Block())

            @block.sync
            def _(sp):
                flag = sp.value_load(wide_flag[0:1, 0:1], min_val=0, max_val=1)
                with sp.If(flag > 0):
                    sync_program(sp, False)
                with sp.Else():
                    sync_program(sp, True)

            @block.tensor
            def _(pe):
                flag = pe.value_load(wide_flag[0:1, 0:1], min_val=0, max_val=1)
                with pe.If(flag > 0):
                    tensor_program(pe, False)
                with pe.Else():
                    tensor_program(pe, True)

            @block.scalar
            def _(act):
                flag = act.value_load(wide_flag[0:1, 0:1], min_val=0, max_val=1)
                with act.If(flag > 0):
                    scalar_program(act, False)
                with act.Else():
                    scalar_program(act, True)

            @block.gpsimd
            def _(pool):
                flag = pool.value_load(wide_flag[0:1, 0:1], min_val=0, max_val=1)
                with pool.If(flag > 0):
                    gpsimd_program(pool, False)
                with pool.Else():
                    gpsimd_program(pool, True)

            @block.vector
            def _(dve):
                flag = dve.value_load(wide_flag[0:1, 0:1], min_val=0, max_val=1)
                with dve.If(flag > 0):
                    vector_program(dve, False)
                with dve.Else():
                    vector_program(dve, True)


def tables():
    import numpy as np

    pos = np.arange(LENGTH, dtype=np.float64)
    half = HEAD // 2
    base = (np.arange(0, HEAD, 2) + 0.4 * HEAD) / (1.4 * HEAD)
    scale = base[None, :] ** (pos[:, None] / 512.0)
    freq = 1.0 / 10000.0 ** (np.arange(half) / half)
    angle = (pos[:, None].astype(np.float32) * freq[None, :].astype(np.float32)).astype(np.float64)
    sign = np.tile([-1.0, 1.0], half)
    gammas = 1.0 - np.exp(np.linspace(np.log(1.0 / 32.0), np.log(1.0 / 512.0), HEADS))
    local = (np.arange(LENGTH) % P).astype(np.float64)
    rope = np.empty((LENGTH, 2, 2, HEADS, HEAD))
    for n, (s, power) in enumerate(((scale, local), (1.0 / scale, -local))):
        decay = gammas[None, :] ** power[:, None]
        for m, trig in enumerate((np.cos(angle), np.sin(angle))):
            row = np.repeat(trig * s, 2, axis=1) * (sign if m else 1.0)
            rope[:, m, n] = decay[:, :, None] * row[:, None, :]
    rope = rope.reshape(CHUNKS, P, 2, 2 * DIM)
    causal = np.triu(np.ones((P, P)))
    across = np.zeros((P, GROUPS, P))
    for g in range(GROUPS):
        for j in range(PER_GROUP):
            r = slice(j * HEAD, (j + 1) * HEAD)
            across[r, g, r] = gammas[g * PER_GROUP + j] ** P
    return {n: np.ascontiguousarray(a, dtype=np.float32) for n, a in
            dict(rope=rope, causal=causal, ident=np.eye(P), decay=across).items()}


def kernel(**inputs):
    import numpy as np
    import concourse.bacc as bacc
    from concourse.bass_utils import run_bass_kernel_spmd as run

    a = {n: np.asarray(x) for n, x in inputs.items()}

    def tiles(w):
        return w.reshape(-1, P, w.shape[1]).transpose(1, 0, 2)

    def columns(w):
        return w.reshape(-1, P).T

    def by_output_tile(w):
        return w.reshape(KH, P, KH, P).transpose(1, 2, 0, 3).reshape(P, -1)

    X = a["L0_attn_X"]
    heads = [a[f"L0_attn_W_{n}"].transpose(1, 0, 2).reshape(DIM, DIM) for n in "QKV"]
    arrays = tables()
    arrays.update(
        xT=X.transpose(2, 0, 1).reshape(KD, P, BATCH, LENGTH).transpose(1, 0, 2, 3),
        x=X.reshape(BATCH, CHUNKS, P, DIM),
        wa=tiles(np.concatenate([*heads, a["L0_attn_W_G"]], axis=1)),
        wo=tiles(a["L0_attn_W_O"]),
        gnw=a["L0_attn_gn_weight"][None, :], gnb=a["L0_attn_gn_bias"][None, :],
        ffn=np.concatenate([
            tiles(a["L0_ffn_w1_w"].T).reshape(P, -1), tiles(a["L0_ffn_w2_w"].T).reshape(P, -1),
            tiles(a["L0_ffn_w3_w"].T).reshape(P, -1),
            by_output_tile(a["L0_ffn_h1_w"].T), by_output_tile(a["L0_ffn_h2_w"].T)], axis=1),
        s1=columns(a["L0_ffn_w1_s"]), s2=columns(a["L0_ffn_w2_s"]),
        hs1=columns(a["L0_ffn_h1_s"]), hs2=columns(a["L0_ffn_h2_s"]), s3=a["L0_ffn_w3_s"][None, :],
        wkvq=tiles(np.concatenate([a["L1_attn_W_k"].T, a["L1_attn_W_v"].T, a["L1_attn_W_q"].T], axis=1)),
        wr=tiles(a["L1_ffn_W_r"].T), wk=tiles(a["L1_ffn_W_k"].T), wv=tiles(a["L1_ffn_W_v"].T),
        mur=columns(a["L1_ffn_mu_r"]), muk=columns(a["L1_ffn_mu_k"]),
    )
    arrays = {n: np.ascontiguousarray(x) for n, x in arrays.items()}
    nc = bacc.Bacc("TRN2", target_bir_lowering=False, num_devices=1)
    t = {n: nc.dram_tensor(f"{n}_dram", x.shape, mybir.dt.from_np(x.dtype), kind="ExternalInput").ap()
         for n, x in arrays.items()}
    t_out = nc.dram_tensor("out_dram", (BATCH, LENGTH, DIM), F32, kind="ExternalOutput").ap()
    t_x1 = nc.dram_tensor("x1_dram", (CHUNKS, P, BATCH, DIM), F32, kind="Internal").ap()
    t_ffn = nc.dram_tensor("ffn_copy_dram", (P, FFN_COLS), F32, kind="Internal").ap()
    build(nc, t["xT"], t["x"], t["rope"], t["causal"], t["ident"], t["decay"], t["wa"], t["wo"],
          t["gnw"], t["gnb"], t["ffn"], t["s1"], t["s2"],
          t["hs1"], t["hs2"], t["s3"], t["wkvq"], t["wr"], t["wk"], t["wv"], t["mur"], t["muk"],
          t_out, t_x1, t_ffn)
    r = run(nc, [{f"{n}_dram": x for n, x in arrays.items()}], core_ids=[0])
    return r.results[0]["out_dram"]
```
